# Optimizing a Trainium2 kernel written in Bass

```python
import numpy as np
import jax
import jax.numpy as jnp

def _softmax(x, axis=-1):
    return jax.nn.softmax(x, axis=axis)

def _gelu(x):
    return jax.nn.gelu(x, approximate=True)

def _silu(x):
    return jax.nn.silu(x)

def _sigmoid(x):
    return jax.nn.sigmoid(x)

def _layernorm(x, axis=-1, eps=1e-05):
    m = jnp.mean(x, axis=axis, keepdims=True)
    v = jnp.var(x, axis=axis, keepdims=True)
    return (x - m) / jnp.sqrt(v + eps)

def _scatter_add(tgt, idx, src, axis=0):
    return tgt.at[idx].add(src)

def _segment_sum(src, seg, n):
    return jax.ops.segment_sum(src, seg, n)
kernel_name = 'mk_perceiver_d4_seqx_r8_d43643'

def setup_inputs(seed: int=0):
    np.random.seed(seed)
    _w = jnp.asarray

    def _rec_inputs():
        import jax
        import jax.numpy as jnp
        _rk = jax.random.key(seed)
        x = -0.0002928 + 1 * jax.random.normal(jax.random.fold_in(_rk, 1), (32, 32, 128), jnp.float32)
        _lenS = 32 - jax.random.randint(jax.random.fold_in(_rk, 7), (32,), 0, max(1, 32 // 4) + 1, jnp.int32)
        _lenS2 = 257 - jax.random.randint(jax.random.fold_in(_rk, 8), (32,), 0, max(1, 257 // 4) + 1, jnp.int32)
        _ctx_1024P = jax.random.normal(jax.random.fold_in(_rk, 11), (32, 16, 128), jnp.float32)
        _ctx_1024c = jax.random.dirichlet(jax.random.fold_in(_rk, 511), 0.3 * jnp.ones((16,), jnp.float32), (32, 257))
        _ctx_1024t = jnp.einsum('bsk,bkd->bsd', _ctx_1024c, _ctx_1024P)
        _ctx_1024t = _ctx_1024t * jax.lax.rsqrt(jnp.mean(jnp.square(_ctx_1024t)) + 1e-12) * 0.953939
        ctx_1024 = -0.000292821 + 1.00034 * (_ctx_1024t + 0.3 * jax.random.normal(jax.random.fold_in(_rk, 611), (32, 257, 128), jnp.float32))
        _validS = jnp.arange(32)[None, :] < _lenS[:, None]
        _validS2 = jnp.arange(257)[None, :] < _lenS2[:, None]
        _causal = jnp.tril(jnp.ones((32, 32), dtype=bool))
        mask_1x1xSxS2_ik1 = jnp.where(jnp.broadcast_to(_validS2[0:1, None, None, :], (1, 1, 32, 257)), 1, 0).astype(jnp.int32)
        return (x, ctx_1024, mask_1x1xSxS2_ik1)
    x, ctx_1024, mask_1x1xSxS2_ik1 = _rec_inputs()

    def _L0_xattn_setup():
        import jax, jax.numpy as jnp
        import numpy as np
        HIDDEN = 128
        HEADS = 16
        HEAD_DIM = HIDDEN // HEADS
        SCALE = 1.0 / np.sqrt(HEAD_DIM).astype(np.float32)
        key = jax.random.key(seed)
        ks = jax.random.split(key, 8)
        b, t = (2, 256)
        x = jax.random.normal(ks[0], (b, t, HIDDEN), dtype=jnp.float32)
        context = x
        s = 0.02
        Wq = jax.random.normal(ks[1], (HIDDEN, HIDDEN), dtype=jnp.float32) * s
        Wk = jax.random.normal(ks[2], (HIDDEN, HIDDEN), dtype=jnp.float32) * s
        Wv = jax.random.normal(ks[3], (HIDDEN, HIDDEN), dtype=jnp.float32) * s
        Wo = jax.random.normal(ks[4], (HIDDEN, HIDDEN), dtype=jnp.float32) * s
        bo = jnp.zeros((HIDDEN,), dtype=jnp.float32)
        return {'x': x, 'context': context, 'Wq': Wq, 'Wk': Wk, 'Wv': Wv, 'Wo': Wo, 'bo': bo}
    _L0_xattn_all = _L0_xattn_setup()
    _L0_xattn_in = {k: v for k, v in _L0_xattn_all.items() if k in ('Wq', 'Wk', 'Wv', 'Wo', 'bo')}
    del _L0_xattn_all

    def _L0_attn_setup():
        import jax, jax.numpy as jnp
        import numpy as np
        B, L, D, H = (2, 64, 128, 16)
        DH = D // H
        key = jax.random.key(seed)
        ks = jax.random.split(key, 14)
        s = 0.02
        inp = {'x': jax.random.normal(ks[0], (B, L, D), jnp.float32), 'q1_w': jax.random.normal(ks[1], (D, D), jnp.float32) * s, 'q1_b': jax.random.normal(ks[2], (D,), jnp.float32) * s, 'k1_w': jax.random.normal(ks[3], (D, D), jnp.float32) * s, 'k1_b': jax.random.normal(ks[4], (D,), jnp.float32) * s, 'k2_w': jax.random.normal(ks[5], (D, D), jnp.float32) * s, 'k2_b': jax.random.normal(ks[6], (D,), jnp.float32) * s, 'gw_w': jax.random.normal(ks[7], (DH, 1), jnp.float32) * s, 'gw_b': jax.random.normal(ks[8], (1,), jnp.float32) * s, 'sw_w': jax.random.normal(ks[9], (DH, 1), jnp.float32) * s, 'sw_b': jax.random.normal(ks[10], (1,), jnp.float32) * s, 'cp_w': jax.random.normal(ks[11], (D, D), jnp.float32) * s, 'cp_b': jax.random.normal(ks[12], (D,), jnp.float32) * s}
        return inp
    _L0_attn_all = _L0_attn_setup()
    _L0_attn_in = {k: v for k, v in _L0_attn_all.items() if k in ('q1_w', 'q1_b', 'k1_w', 'k1_b', 'k2_w', 'k2_b', 'gw_w', 'gw_b', 'sw_w', 'sw_b', 'cp_w', 'cp_b')}
    del _L0_attn_all

    def _L0_ffn_setup():
        import jax, jax.numpy as jnp
        import numpy as np
        B, S, D = (1, 256, 128)
        E, F = (16, 128)
        NG, TKG, K = (4, 2, 4)
        NSH = 2
        SCALE = 2.5
        STD = 0.02
        EPG = E // NG

        def _route(x_flat, router_w, bias):
            logits = x_flat.astype(jnp.float32) @ router_w.T
            scores = jax.nn.sigmoid(logits)
            s = scores + bias[None, :]
            sg = s.reshape(-1, NG, EPG)
            group_score = jax.lax.top_k(sg, 2)[0].sum(-1)
            gidx = jax.lax.top_k(group_score, TKG)[1]
            gmask = jnp.sum(jax.nn.one_hot(gidx, NG, dtype=jnp.float32), axis=1) > 0
            emask = jnp.repeat(gmask, EPG, axis=1)
            masked = jnp.where(emask, s, -1.0)
            topk_idx = jax.lax.top_k(masked, K)[1]
            tw = jnp.take_along_axis(scores, topk_idx, axis=1)
            tw = tw / (tw.sum(-1, keepdims=True) + 1e-20)
            tw = tw * SCALE
            return (topk_idx, tw)
        key = jax.random.key(seed)
        ks = jax.random.split(key, 8)
        return {'hidden_states': jax.random.normal(ks[0], (B, S, D), jnp.float32), 'router_w': jax.random.normal(ks[1], (E, D), jnp.float32) * STD, 'bias': jnp.zeros((E,), jnp.float32), 'gate_w': jax.random.normal(ks[2], (E, D, F), jnp.float32) * STD, 'up_w': jax.random.normal(ks[3], (E, D, F), jnp.float32) * STD, 'down_w': jax.random.normal(ks[4], (E, F, D), jnp.float32) * STD, 'sh_gate_w': jax.random.normal(ks[5], (D, NSH * F), jnp.float32) * STD, 'sh_up_w': jax.random.normal(ks[6], (D, NSH * F), jnp.float32) * STD, 'sh_down_w': jax.random.normal(ks[7], (NSH * F, D), jnp.float32) * STD}
    _L0_ffn_all = _L0_ffn_setup()
    _L0_ffn_in = {k: v for k, v in _L0_ffn_all.items() if k in ('router_w', 'bias', 'gate_w', 'up_w', 'down_w', 'sh_gate_w', 'sh_up_w', 'sh_down_w')}
    del _L0_ffn_all

    def _L1_xattn_setup():
        import jax, jax.numpy as jnp
        import numpy as np
        D_MODEL = 128
        NUM_HEADS = 16
        D_K = D_MODEL // NUM_HEADS
        EPS = 1e-06

        def _split_heads(x):
            B, S, _ = x.shape
            return x.reshape(B, S, NUM_HEADS, D_K).transpose(0, 2, 1, 3)
        key = jax.random.key(seed)
        ks = jax.random.split(key, 16)
        B, S = (2, 256)
        sc_in = 1.0 / np.sqrt(D_MODEL)
        sc_na = 1.0 / np.sqrt(D_K)
        inp = {'Q': jax.random.normal(ks[0], (B, S, D_MODEL), jnp.float32), 'K': jax.random.normal(ks[1], (B, S, D_MODEL), jnp.float32), 'V': jax.random.normal(ks[2], (B, S, D_MODEL), jnp.float32), 'mask': jax.random.randint(ks[3], (1, 1, S, S), 0, 2, jnp.int32), 'wq': jax.random.normal(ks[4], (D_MODEL, D_MODEL), jnp.float32) * sc_in, 'bq': jnp.zeros((D_MODEL,), jnp.float32), 'wk': jax.random.normal(ks[5], (D_MODEL, D_MODEL), jnp.float32) * sc_in, 'bk': jnp.zeros((D_MODEL,), jnp.float32), 'wv': jax.random.normal(ks[6], (D_MODEL, D_MODEL), jnp.float32) * sc_in, 'bv': jnp.zeros((D_MODEL,), jnp.float32), 'wo': jax.random.normal(ks[7], (D_MODEL, D_MODEL), jnp.float32) * sc_in, 'bo': jnp.zeros((D_MODEL,), jnp.float32), 'wnq': jax.random.normal(ks[8], (D_K, D_K), jnp.float32) * sc_na, 'bnq': jnp.zeros((D_K,), jnp.float32), 'wnk': jax.random.normal(ks[9], (D_K, D_K), jnp.float32) * sc_na, 'bnk': jnp.zeros((D_K,), jnp.float32), 'temperature': jnp.ones((NUM_HEADS, 1, 1), jnp.float32), 'gamma': jnp.ones((D_MODEL,), jnp.float32)}
        return inp
    _L1_xattn_all = _L1_xattn_setup()
    _L1_xattn_in = {k: v for k, v in _L1_xattn_all.items() if k in ('wq', 'bq', 'wk', 'bk', 'wv', 'bv', 'wo', 'bo', 'wnq', 'bnq', 'wnk', 'bnk', 'temperature', 'gamma')}
    del _L1_xattn_all

    def _L1_attn_setup():
        import jax, jax.numpy as jnp
        import numpy as np
        FOCUS = 3
        EPS = 1e-06

        def _norm_last(t):
            return t / jnp.sum(t, axis=-1, keepdims=True)
        key = jax.random.key(seed)
        ks = jax.random.split(key, 6)
        B, N, C = (4, 512, 128)
        s = 0.02
        return {'x': jax.random.normal(ks[0], (B, N, C), jnp.float32), 'w_qkv': jax.random.normal(ks[1], (3 * C, C), jnp.float32) * s, 'w_proj': jax.random.normal(ks[2], (C, C), jnp.float32) * s, 'b_proj': jax.random.normal(ks[3], (C,), jnp.float32) * s, 'w_dwc': jax.random.normal(ks[4], (C, 3), jnp.float32) * s, 'b_dwc': jax.random.normal(ks[5], (C,), jnp.float32) * s}
    _L1_attn_all = _L1_attn_setup()
    _L1_attn_in = {k: v for k, v in _L1_attn_all.items() if k in ('w_qkv', 'w_proj', 'b_proj', 'w_dwc', 'b_dwc')}
    del _L1_attn_all

    def _L1_ffn_setup():
        import jax, jax.numpy as jnp
        import numpy as np
        D_MODEL = 128
        DEPTH = 8
        M = 2 ** DEPTH
        N_INTERNAL = M - 1
        B, T = (8, 512)

        def _leaf_probs(gate):
            BT = gate.shape[0]
            lp = jnp.ones((BT, M), dtype=gate.dtype)
            for level in range(DEPTH):
                n = 2 ** level
                half = M // (2 * n)
                g = gate[:, n - 1:2 * n - 1]
                f = jnp.stack([1.0 - g, g], axis=-1)
                f = jnp.broadcast_to(f[..., None], (BT, n, 2, half))
                lp = lp * f.reshape(BT, M)
            return lp
        key = jax.random.key(seed)
        ks = jax.random.split(key, 7)
        x = jax.random.normal(ks[0], (B, T, D_MODEL), dtype=jnp.float32)
        Wq = jax.random.normal(ks[1], (D_MODEL, D_MODEL), dtype=jnp.float32) * 0.02
        routers = jax.random.normal(ks[2], (N_INTERNAL, D_MODEL), dtype=jnp.float32) * 0.02
        leaf_keys = jax.random.normal(ks[3], (M, D_MODEL), dtype=jnp.float32) * 0.02
        leaf_values = jax.random.normal(ks[4], (M, D_MODEL), dtype=jnp.float32) * 0.02
        Wout_w = jax.random.normal(ks[5], (D_MODEL, D_MODEL), dtype=jnp.float32) * 0.02
        Wout_b = jax.random.normal(ks[6], (D_MODEL,), dtype=jnp.float32) * 0.02
        return {'x': x, 'Wq': Wq, 'routers': routers, 'leaf_keys': leaf_keys, 'leaf_values': leaf_values, 'Wout_w': Wout_w, 'Wout_b': Wout_b}
    _L1_ffn_all = _L1_ffn_setup()
    _L1_ffn_in = {k: v for k, v in _L1_ffn_all.items() if k in ('Wq', 'routers', 'leaf_keys', 'leaf_values', 'Wout_w', 'Wout_b')}
    del _L1_ffn_all

    def _L2_xattn_setup():
        import jax, jax.numpy as jnp
        import numpy as np
        EPS = 1e-12

        def _l2norm(x):
            n = jnp.linalg.norm(x, axis=-1, keepdims=True)
            return x / jnp.maximum(n, EPS)
        key = jax.random.key(seed)
        k1, k2 = jax.random.split(key)
        img_feat = jax.random.normal(k1, (8, 512, 128), dtype=jnp.float32)
        text_feat = jax.random.normal(k2, (8, 64, 128), dtype=jnp.float32)
        return {'img_feat': img_feat, 'text_feat': text_feat}
    _L2_xattn_all = _L2_xattn_setup()
    _L2_xattn_in = {k: v for k, v in _L2_xattn_all.items() if k in ()}
    del _L2_xattn_all

    def _L2_attn_setup():
        import jax, jax.numpy as jnp
        import numpy as np
        import math
        B, T, E = (1, 256, 128)
        H = 8
        D = E // H // 2
        LAMBDA_INIT = 0.8 - 0.6 * math.exp(-0.3 * 1)
        SCALE_BASE = 512.0
        THETA = 10000.0

        def _rope_tables(T, d):
            inv_freq = 1.0 / THETA ** (jnp.arange(0, d, 2, dtype=jnp.float32) / d)
            pos = jnp.arange(T, dtype=jnp.float32)
            freqs = pos[:, None] * inv_freq[None, :]
            freqs = jnp.repeat(freqs, 2, axis=-1)
            sv = (jnp.arange(0, d, 2, dtype=jnp.float32) + 0.4 * d) / (1.4 * d)
            power = (pos - T // 2) / SCALE_BASE
            scale = sv[None, :] ** power[:, None]
            scale = jnp.concatenate([scale, scale], axis=-1)
            return (freqs, scale)

        def _rotate_half(x):
            x1 = x[..., 0::2]
            x2 = x[..., 1::2]
            return jnp.stack([-x2, x1], axis=-1).reshape(x.shape)

        def _apply_rope(t, freqs, scale):
            f = freqs[None, :, None, :]
            s = scale[None, :, None, :]
            return t * jnp.cos(f) * s + _rotate_half(t) * jnp.sin(f) * s
        key = jax.random.key(seed)
        ks = jax.random.split(key, 9)
        w = 0.02
        return {'x': jax.random.normal(ks[0], (B, T, E), dtype=jnp.float32), 'Wq': jax.random.normal(ks[1], (E, E), dtype=jnp.float32) * w, 'Wk': jax.random.normal(ks[2], (E, E), dtype=jnp.float32) * w, 'Wv': jax.random.normal(ks[3], (E, E), dtype=jnp.float32) * w, 'Wo': jax.random.normal(ks[4], (E, E), dtype=jnp.float32) * w, 'lambda_q1': jax.random.normal(ks[5], (D,), dtype=jnp.float32) * 0.1, 'lambda_k1': jax.random.normal(ks[6], (D,), dtype=jnp.float32) * 0.1, 'lambda_q2': jax.random.normal(ks[7], (D,), dtype=jnp.float32) * 0.1, 'lambda_k2': jax.random.normal(ks[8], (D,), dtype=jnp.float32) * 0.1}
    _L2_attn_all = _L2_attn_setup()
    _L2_attn_in = {k: v for k, v in _L2_attn_all.items() if k in ('Wq', 'Wk', 'Wv', 'Wo', 'lambda_q1', 'lambda_k1', 'lambda_q2', 'lambda_k2')}
    del _L2_attn_all

    def _L2_ffn_setup():
        import jax, jax.numpy as jnp
        import numpy as np
        key = jax.random.key(seed)
        k1, k2, k3, k4 = jax.random.split(key, 4)
        B, T, M = (4, 256, 128)
        E, F = (16, 512)
        x = jax.random.normal(k1, (B, T, M), dtype=jnp.float32) * 0.02
        Wg = jax.random.normal(k2, (M, E), dtype=jnp.float32) * 0.02
        w1 = jax.random.normal(k3, (E, M, F), dtype=jnp.float32) * 0.02
        w2 = jax.random.normal(k4, (E, F, M), dtype=jnp.float32) * 0.02
        return {'x': x, 'Wg': Wg, 'w1': w1, 'w2': w2}
    _L2_ffn_all = _L2_ffn_setup()
    _L2_ffn_in = {k: v for k, v in _L2_ffn_all.items() if k in ('Wg', 'w1', 'w2')}
    del _L2_ffn_all

    def _L3_xattn_setup():
        import jax, jax.numpy as jnp
        import numpy as np
        D = 128
        H = 16
        DH = D // H
        key = jax.random.key(seed)
        ks = jax.random.split(key, 11)
        B, T = (4, 256)
        s = 0.02
        return {'q': jax.random.normal(ks[0], (B, T, D), jnp.float32), 'k': jax.random.normal(ks[1], (B, T, D), jnp.float32), 'v': jax.random.normal(ks[2], (B, T, D), jnp.float32), 'Wq': jax.random.normal(ks[3], (D, D), jnp.float32) * s, 'b_q': jax.random.normal(ks[4], (D,), jnp.float32) * s, 'Wk': jax.random.normal(ks[5], (D, D), jnp.float32) * s, 'b_k': jax.random.normal(ks[6], (D,), jnp.float32) * s, 'Wv': jax.random.normal(ks[7], (D, D), jnp.float32) * s, 'b_v': jax.random.normal(ks[8], (D,), jnp.float32) * s, 'Wo': jax.random.normal(ks[9], (D, D), jnp.float32) * s, 'b_o': jax.random.normal(ks[10], (D,), jnp.float32) * s}
    _L3_xattn_all = _L3_xattn_setup()
    _L3_xattn_in = {k: v for k, v in _L3_xattn_all.items() if k in ('Wq', 'b_q', 'Wk', 'b_k', 'Wv', 'b_v', 'Wo', 'b_o')}
    del _L3_xattn_all

    def _L3_attn_setup():
        import jax, jax.numpy as jnp
        import numpy as np
        import math
        HEADS = 16
        LN_EPS = 1e-05

        def _layernorm(x, w, b):
            mu = jnp.mean(x, axis=-1, keepdims=True)
            var = jnp.mean((x - mu) ** 2, axis=-1, keepdims=True)
            return (x - mu) * jax.lax.rsqrt(var + LN_EPS) * w + b
        key = jax.random.key(seed)
        ks = jax.random.split(key, 8)
        b, t, e = (2, 256, 128)
        s = e // HEADS
        sc = 1.0 / math.sqrt(e)
        inp = {'x': jax.random.normal(ks[0], (b, t, e), dtype=jnp.float32), 'Wk': jax.random.normal(ks[1], (e, e), dtype=jnp.float32) * sc, 'Wq': jax.random.normal(ks[2], (e, e), dtype=jnp.float32) * sc, 'Wv': jax.random.normal(ks[3], (e, e), dtype=jnp.float32) * sc, 'Wo': jax.random.normal(ks[4], (e, e), dtype=jnp.float32) * sc, 'bo': jnp.zeros((e,), dtype=jnp.float32), 'kln_w': jnp.ones((s,), dtype=jnp.float32), 'kln_b': jnp.zeros((s,), dtype=jnp.float32), 'qln_w': jnp.ones((s,), dtype=jnp.float32), 'qln_b': jnp.zeros((s,), dtype=jnp.float32)}
        return inp
    _L3_attn_all = _L3_attn_setup()
    _L3_attn_in = {k: v for k, v in _L3_attn_all.items() if k in ('Wk', 'Wq', 'Wv', 'Wo', 'bo', 'kln_w', 'kln_b', 'qln_w', 'qln_b')}
    del _L3_attn_all

    def _L3_ffn_setup():
        import jax, jax.numpy as jnp
        import numpy as np
        B, S, DIM = (4, 256, 128)
        E, K, HID = (8, 2, 512)
        key = jax.random.key(seed)
        ks = jax.random.split(key, 8)
        init = lambda k, sh: jax.random.normal(k, sh, jnp.float32) * 0.02
        return {'x': jax.random.normal(ks[0], (B, S, DIM), jnp.float32), 'gate_w': init(ks[1], (DIM, E)), 'gate_b': jnp.zeros((E,), jnp.float32), 'w1': init(ks[2], (E, DIM, HID)), 'b1': jnp.zeros((E, HID), jnp.float32), 'w2': init(ks[3], (E, HID, DIM)), 'b2': jnp.zeros((E, DIM), jnp.float32), 'ws1': init(ks[4], (DIM, HID)), 'bs1': jnp.zeros((HID,), jnp.float32), 'ws2': init(ks[5], (HID, DIM)), 'bs2': jnp.zeros((DIM,), jnp.float32)}
    _L3_ffn_all = _L3_ffn_setup()
    _L3_ffn_in = {k: v for k, v in _L3_ffn_all.items() if k in ('gate_w', 'gate_b', 'w1', 'b1', 'w2', 'b2', 'ws1', 'bs1', 'ws2', 'bs2')}
    del _L3_ffn_all
    return {'x': x, 'ctx_1024': ctx_1024, 'mask_1x1xSxS2_ik1': mask_1x1xSxS2_ik1, 'L0_xattn_Wq': _L0_xattn_in['Wq'], 'L0_xattn_Wk': _L0_xattn_in['Wk'], 'L0_xattn_Wv': _L0_xattn_in['Wv'], 'L0_xattn_Wo': _L0_xattn_in['Wo'], 'L0_xattn_bo': _L0_xattn_in['bo'], 'L0_attn_q1_w': _L0_attn_in['q1_w'], 'L0_attn_q1_b': _L0_attn_in['q1_b'], 'L0_attn_k1_w': _L0_attn_in['k1_w'], 'L0_attn_k1_b': _L0_attn_in['k1_b'], 'L0_attn_k2_w': _L0_attn_in['k2_w'], 'L0_attn_k2_b': _L0_attn_in['k2_b'], 'L0_attn_gw_w': _L0_attn_in['gw_w'], 'L0_attn_gw_b': _L0_attn_in['gw_b'], 'L0_attn_sw_w': _L0_attn_in['sw_w'], 'L0_attn_sw_b': _L0_attn_in['sw_b'], 'L0_attn_cp_w': _L0_attn_in['cp_w'], 'L0_attn_cp_b': _L0_attn_in['cp_b'], 'L0_ffn_router_w': _L0_ffn_in['router_w'], 'L0_ffn_bias': _L0_ffn_in['bias'], 'L0_ffn_gate_w': _L0_ffn_in['gate_w'], 'L0_ffn_up_w': _L0_ffn_in['up_w'], 'L0_ffn_down_w': _L0_ffn_in['down_w'], 'L0_ffn_sh_gate_w': _L0_ffn_in['sh_gate_w'], 'L0_ffn_sh_up_w': _L0_ffn_in['sh_up_w'], 'L0_ffn_sh_down_w': _L0_ffn_in['sh_down_w'], 'L1_xattn_wq': _L1_xattn_in['wq'], 'L1_xattn_bq': _L1_xattn_in['bq'], 'L1_xattn_wk': _L1_xattn_in['wk'], 'L1_xattn_bk': _L1_xattn_in['bk'], 'L1_xattn_wv': _L1_xattn_in['wv'], 'L1_xattn_bv': _L1_xattn_in['bv'], 'L1_xattn_wo': _L1_xattn_in['wo'], 'L1_xattn_bo': _L1_xattn_in['bo'], 'L1_xattn_wnq': _L1_xattn_in['wnq'], 'L1_xattn_bnq': _L1_xattn_in['bnq'], 'L1_xattn_wnk': _L1_xattn_in['wnk'], 'L1_xattn_bnk': _L1_xattn_in['bnk'], 'L1_xattn_temperature': _L1_xattn_in['temperature'], 'L1_xattn_gamma': _L1_xattn_in['gamma'], 'L1_attn_w_qkv': _L1_attn_in['w_qkv'], 'L1_attn_w_proj': _L1_attn_in['w_proj'], 'L1_attn_b_proj': _L1_attn_in['b_proj'], 'L1_attn_w_dwc': _L1_attn_in['w_dwc'], 'L1_attn_b_dwc': _L1_attn_in['b_dwc'], 'L1_ffn_Wq': _L1_ffn_in['Wq'], 'L1_ffn_routers': _L1_ffn_in['routers'], 'L1_ffn_leaf_keys': _L1_ffn_in['leaf_keys'], 'L1_ffn_leaf_values': _L1_ffn_in['leaf_values'], 'L1_ffn_Wout_w': _L1_ffn_in['Wout_w'], 'L1_ffn_Wout_b': _L1_ffn_in['Wout_b'], 'L2_attn_Wq': _L2_attn_in['Wq'], 'L2_attn_Wk': _L2_attn_in['Wk'], 'L2_attn_Wv': _L2_attn_in['Wv'], 'L2_attn_Wo': _L2_attn_in['Wo'], 'L2_attn_lambda_q1': _L2_attn_in['lambda_q1'], 'L2_attn_lambda_k1': _L2_attn_in['lambda_k1'], 'L2_attn_lambda_q2': _L2_attn_in['lambda_q2'], 'L2_attn_lambda_k2': _L2_attn_in['lambda_k2'], 'L2_ffn_Wg': _L2_ffn_in['Wg'], 'L2_ffn_w1': _L2_ffn_in['w1'], 'L2_ffn_w2': _L2_ffn_in['w2'], 'L3_xattn_Wq': _L3_xattn_in['Wq'], 'L3_xattn_b_q': _L3_xattn_in['b_q'], 'L3_xattn_Wk': _L3_xattn_in['Wk'], 'L3_xattn_b_k': _L3_xattn_in['b_k'], 'L3_xattn_Wv': _L3_xattn_in['Wv'], 'L3_xattn_b_v': _L3_xattn_in['b_v'], 'L3_xattn_Wo': _L3_xattn_in['Wo'], 'L3_xattn_b_o': _L3_xattn_in['b_o'], 'L3_attn_Wk': _L3_attn_in['Wk'], 'L3_attn_Wq': _L3_attn_in['Wq'], 'L3_attn_Wv': _L3_attn_in['Wv'], 'L3_attn_Wo': _L3_attn_in['Wo'], 'L3_attn_bo': _L3_attn_in['bo'], 'L3_attn_kln_w': _L3_attn_in['kln_w'], 'L3_attn_kln_b': _L3_attn_in['kln_b'], 'L3_attn_qln_w': _L3_attn_in['qln_w'], 'L3_attn_qln_b': _L3_attn_in['qln_b'], 'L3_ffn_gate_w': _L3_ffn_in['gate_w'], 'L3_ffn_gate_b': _L3_ffn_in['gate_b'], 'L3_ffn_w1': _L3_ffn_in['w1'], 'L3_ffn_b1': _L3_ffn_in['b1'], 'L3_ffn_w2': _L3_ffn_in['w2'], 'L3_ffn_b2': _L3_ffn_in['b2'], 'L3_ffn_ws1': _L3_ffn_in['ws1'], 'L3_ffn_bs1': _L3_ffn_in['bs1'], 'L3_ffn_ws2': _L3_ffn_in['ws2'], 'L3_ffn_bs2': _L3_ffn_in['bs2']}

def reference(x, ctx_1024, mask_1x1xSxS2_ik1, L0_xattn_Wq, L0_xattn_Wk, L0_xattn_Wv, L0_xattn_Wo, L0_xattn_bo, L0_attn_q1_w, L0_attn_q1_b, L0_attn_k1_w, L0_attn_k1_b, L0_attn_k2_w, L0_attn_k2_b, L0_attn_gw_w, L0_attn_gw_b, L0_attn_sw_w, L0_attn_sw_b, L0_attn_cp_w, L0_attn_cp_b, L0_ffn_router_w, L0_ffn_bias, L0_ffn_gate_w, L0_ffn_up_w, L0_ffn_down_w, L0_ffn_sh_gate_w, L0_ffn_sh_up_w, L0_ffn_sh_down_w, L1_xattn_wq, L1_xattn_bq, L1_xattn_wk, L1_xattn_bk, L1_xattn_wv, L1_xattn_bv, L1_xattn_wo, L1_xattn_bo, L1_xattn_wnq, L1_xattn_bnq, L1_xattn_wnk, L1_xattn_bnk, L1_xattn_temperature, L1_xattn_gamma, L1_attn_w_qkv, L1_attn_w_proj, L1_attn_b_proj, L1_attn_w_dwc, L1_attn_b_dwc, L1_ffn_Wq, L1_ffn_routers, L1_ffn_leaf_keys, L1_ffn_leaf_values, L1_ffn_Wout_w, L1_ffn_Wout_b, L2_attn_Wq, L2_attn_Wk, L2_attn_Wv, L2_attn_Wo, L2_attn_lambda_q1, L2_attn_lambda_k1, L2_attn_lambda_q2, L2_attn_lambda_k2, L2_ffn_Wg, L2_ffn_w1, L2_ffn_w2, L3_xattn_Wq, L3_xattn_b_q, L3_xattn_Wk, L3_xattn_b_k, L3_xattn_Wv, L3_xattn_b_v, L3_xattn_Wo, L3_xattn_b_o, L3_attn_Wk, L3_attn_Wq, L3_attn_Wv, L3_attn_Wo, L3_attn_bo, L3_attn_kln_w, L3_attn_kln_b, L3_attn_qln_w, L3_attn_qln_b, L3_ffn_gate_w, L3_ffn_gate_b, L3_ffn_w1, L3_ffn_b1, L3_ffn_w2, L3_ffn_b2, L3_ffn_ws1, L3_ffn_bs1, L3_ffn_ws2, L3_ffn_bs2):
    import jax
    import jax.numpy as jnp

    def _L0_xattn_ref(x, context, Wq, Wk, Wv, Wo, bo):
        import jax, jax.numpy as jnp
        import numpy as np
        HIDDEN = 128
        HEADS = 16
        HEAD_DIM = HIDDEN // HEADS
        SCALE = 1.0 / np.sqrt(HEAD_DIM).astype(np.float32)
        b, t, c = x.shape
        kv_t = context.shape[1]
        q = x @ Wq.T
        k = context @ Wk.T
        v = context @ Wv.T
        q = q.reshape(b, t, HEADS, HEAD_DIM).transpose(0, 2, 1, 3)
        k = k.reshape(b, kv_t, HEADS, HEAD_DIM).transpose(0, 2, 1, 3)
        v = v.reshape(b, kv_t, HEADS, HEAD_DIM).transpose(0, 2, 1, 3)
        scores = jnp.einsum('bhqd,bhkd->bhqk', q, k) * SCALE
        causal = jnp.tril(jnp.ones((t, kv_t), dtype=bool))
        scores = jnp.where(causal[None, None, :, :], scores, -jnp.inf)
        probs = jax.nn.softmax(scores, axis=-1)
        y = jnp.einsum('bhqk,bhkd->bhqd', probs, v)
        y = y.transpose(0, 2, 1, 3).reshape(b, t, c)
        return y @ Wo.T + bo

    def _L0_attn_ref(x, q1_w, q1_b, k1_w, k1_b, k2_w, k2_b, gw_w, gw_b, sw_w, sw_b, cp_w, cp_b):
        import jax, jax.numpy as jnp
        import numpy as np
        B, L, D, H = (2, 64, 128, 16)
        DH = D // H
        b, l, dm = x.shape
        dh = gw_w.shape[0]
        h = dm // dh
        Q = (x @ q1_w + q1_b).reshape(b, l, h, dh)
        K = (x @ k1_w + k1_b).reshape(b, l, h, dh)
        V = x.reshape(b, l, h, dh)
        W = K[..., :, None] * V[..., None, :]
        G = jax.nn.sigmoid(x.reshape(b, l, h, dh) @ gw_w + gw_b)
        log_cp = jnp.clip(jnp.cumsum(jnp.log(jnp.clip(G, 1e-06, None)), axis=1), -30.0, 30.0)
        Gc = (jnp.exp(log_cp) + 1e-06)[..., None]
        R = jax.nn.silu(K @ sw_w + sw_b)[..., None]
        Wc = jnp.cumsum(W * R / Gc, axis=1) * Gc
        O1 = jnp.einsum('blhd,blhde->blhe', Q, Wc)
        E = V[:, 1:] - O1[:, :-1]
        sd = jnp.sqrt(jnp.asarray(dh, x.dtype))
        q2 = -jax.nn.leaky_relu(-Q[:, :-1] / sd, 0.02)
        sD = jnp.sqrt(jnp.asarray(dm, x.dtype))
        k2 = jax.nn.sigmoid((x[:, :-1] @ k2_w + k2_b) / sD * 0.02).reshape(b, l - 1, h, dh)
        Wma = jnp.cumsum(k2[..., :, None] * E[..., None, :], axis=1)
        O2 = jnp.einsum('blhd,blhde->blhe', q2, Wma)
        O2 = jnp.concatenate([jnp.zeros_like(O2[:, :1]), O2], axis=1)
        y = (O1 + O2).reshape(b, l, dm)
        return y @ cp_w + cp_b

    def _L0_ffn_ref(hidden_states, router_w, bias, gate_w, up_w, down_w, sh_gate_w, sh_up_w, sh_down_w):
        import jax, jax.numpy as jnp
        import numpy as np
        B, S, D = (1, 256, 128)
        E, F = (16, 128)
        NG, TKG, K = (4, 2, 4)
        NSH = 2
        SCALE = 2.5
        STD = 0.02
        EPG = E // NG

        def _route(x_flat, router_w, bias):
            logits = x_flat.astype(jnp.float32) @ router_w.T
            scores = jax.nn.sigmoid(logits)
            s = scores + bias[None, :]
            sg = s.reshape(-1, NG, EPG)
            group_score = jax.lax.top_k(sg, 2)[0].sum(-1)
            gidx = jax.lax.top_k(group_score, TKG)[1]
            gmask = jnp.sum(jax.nn.one_hot(gidx, NG, dtype=jnp.float32), axis=1) > 0
            emask = jnp.repeat(gmask, EPG, axis=1)
            masked = jnp.where(emask, s, -1.0)
            topk_idx = jax.lax.top_k(masked, K)[1]
            tw = jnp.take_along_axis(scores, topk_idx, axis=1)
            tw = tw / (tw.sum(-1, keepdims=True) + 1e-20)
            tw = tw * SCALE
            return (topk_idx, tw)
        x = hidden_states.reshape(-1, D)
        topk_idx, tw = _route(x, router_w, bias)
        combine = (jax.nn.one_hot(topk_idx, E, dtype=tw.dtype) * tw[..., None]).sum(1)
        h = jnp.einsum('td,edf->etf', x, gate_w)
        u = jnp.einsum('td,edf->etf', x, up_w)
        y = jnp.einsum('etf,efd->etd', jax.nn.silu(h) * u, down_w)
        routed = jnp.einsum('etd,te->td', y, combine)
        sh = jax.nn.silu(x @ sh_gate_w) * (x @ sh_up_w) @ sh_down_w
        return (routed + sh).reshape(hidden_states.shape)

    def _L1_xattn_ref(Q, K, V, mask, wq, bq, wk, bk, wv, bv, wo, bo, wnq, bnq, wnk, bnk, temperature, gamma):
        import jax, jax.numpy as jnp
        import numpy as np
        D_MODEL = 128
        NUM_HEADS = 16
        D_K = D_MODEL // NUM_HEADS
        EPS = 1e-06

        def _split_heads(x):
            B, S, _ = x.shape
            return x.reshape(B, S, NUM_HEADS, D_K).transpose(0, 2, 1, 3)
        B, S, _ = Q.shape
        q = _split_heads(Q @ wq + bq)
        k = _split_heads(K @ wk + bk)
        v = _split_heads(V @ wv + bv)
        qf = jnp.tanh(q @ wnq + bnq)
        kf = jnp.tanh(k @ wnk + bnk)
        scores = jnp.einsum('bhqd,bhkd->bhqk', qf, kf) / jnp.sqrt(jnp.float32(D_K))
        scores = scores / temperature
        scores = jnp.where(mask == 0, jnp.float32(-1000000000.0), scores)
        attn = jax.nn.softmax(scores, axis=-1)
        ctx = jnp.einsum('bhqk,bhkd->bhqd', attn, v)
        out = ctx.transpose(0, 2, 1, 3).reshape(B, S, D_MODEL) @ wo + bo
        rms = jax.lax.rsqrt(jnp.mean(out * out, axis=-1, keepdims=True) + EPS)
        return out * rms * gamma

    def _L1_attn_ref(x, w_qkv, w_proj, b_proj, w_dwc, b_dwc):
        import jax, jax.numpy as jnp
        import numpy as np
        FOCUS = 3
        EPS = 1e-06

        def _norm_last(t):
            return t / jnp.sum(t, axis=-1, keepdims=True)
        B, N, C = x.shape
        H = 16
        d = C // H
        qkv = jnp.einsum('bnc,oc->bno', x, w_qkv).reshape(B, N, 3, H, d)
        qkv = jnp.transpose(qkv, (2, 0, 3, 1, 4))
        q, k, v = (qkv[0], qkv[1], qkv[2])
        q = _norm_last(jax.nn.relu(q) + EPS)
        k = _norm_last(jax.nn.relu(k) + EPS)
        q = _norm_last(q ** FOCUS)
        k = _norm_last(k ** FOCUS)
        kv = jnp.einsum('bhnd,bhne->bhde', k, v)
        z = 1.0 / (jnp.einsum('bhnd,bhd->bhn', q, k.sum(axis=2)) + EPS)
        out = jnp.einsum('bhnd,bhde,bhn->bhne', q, kv, z)
        out = jnp.transpose(out, (0, 2, 1, 3)).reshape(B, N, C)
        xp = jnp.pad(out, ((0, 0), (1, 1), (0, 0)))
        conv = xp[:, 0:N, :] * w_dwc[:, 0] + xp[:, 1:N + 1, :] * w_dwc[:, 1] + xp[:, 2:N + 2, :] * w_dwc[:, 2] + b_dwc
        out = out + conv
        return jnp.einsum('bnc,oc->bno', out, w_proj) + b_proj

    def _L1_ffn_ref(x, Wq, routers, leaf_keys, leaf_values, Wout_w, Wout_b):
        import jax, jax.numpy as jnp
        import numpy as np
        D_MODEL = 128
        DEPTH = 8
        M = 2 ** DEPTH
        N_INTERNAL = M - 1
        B, T = (8, 512)

        def _leaf_probs(gate):
            BT = gate.shape[0]
            lp = jnp.ones((BT, M), dtype=gate.dtype)
            for level in range(DEPTH):
                n = 2 ** level
                half = M // (2 * n)
                g = gate[:, n - 1:2 * n - 1]
                f = jnp.stack([1.0 - g, g], axis=-1)
                f = jnp.broadcast_to(f[..., None], (BT, n, 2, half))
                lp = lp * f.reshape(BT, M)
            return lp
        Bv, Tv, d = x.shape
        q = jnp.einsum('btd,ed->bte', x, Wq)
        q_flat = q.reshape(Bv * Tv, d)
        gate = jax.nn.sigmoid(q_flat @ routers.T)
        leaf_prob = _leaf_probs(gate)
        ret = (leaf_prob @ leaf_values).reshape(Bv, Tv, d)
        return jnp.einsum('btd,ed->bte', ret, Wout_w) + Wout_b

    def _L2_xattn_ref(img_feat, text_feat):
        import jax, jax.numpy as jnp
        import numpy as np
        EPS = 1e-12

        def _l2norm(x):
            n = jnp.linalg.norm(x, axis=-1, keepdims=True)
            return x / jnp.maximum(n, EPS)
        img_norm = _l2norm(img_feat)
        text_norm = _l2norm(text_feat)
        sim = jnp.einsum('bic,btc->bit', img_norm, text_norm)
        min_idx = jnp.argmax(sim, axis=-1)
        text_aligned = jnp.take_along_axis(text_feat, min_idx[..., None], axis=1)
        return text_aligned

    def _L2_attn_ref(x, Wq, Wk, Wv, Wo, lambda_q1, lambda_k1, lambda_q2, lambda_k2):
        import jax, jax.numpy as jnp
        import numpy as np
        import math
        B, T, E = (1, 256, 128)
        H = 8
        D = E // H // 2
        LAMBDA_INIT = 0.8 - 0.6 * math.exp(-0.3 * 1)
        SCALE_BASE = 512.0
        THETA = 10000.0

        def _rope_tables(T, d):
            inv_freq = 1.0 / THETA ** (jnp.arange(0, d, 2, dtype=jnp.float32) / d)
            pos = jnp.arange(T, dtype=jnp.float32)
            freqs = pos[:, None] * inv_freq[None, :]
            freqs = jnp.repeat(freqs, 2, axis=-1)
            sv = (jnp.arange(0, d, 2, dtype=jnp.float32) + 0.4 * d) / (1.4 * d)
            power = (pos - T // 2) / SCALE_BASE
            scale = sv[None, :] ** power[:, None]
            scale = jnp.concatenate([scale, scale], axis=-1)
            return (freqs, scale)

        def _rotate_half(x):
            x1 = x[..., 0::2]
            x2 = x[..., 1::2]
            return jnp.stack([-x2, x1], axis=-1).reshape(x.shape)

        def _apply_rope(t, freqs, scale):
            f = freqs[None, :, None, :]
            s = scale[None, :, None, :]
            return t * jnp.cos(f) * s + _rotate_half(t) * jnp.sin(f) * s
        b, t, e = x.shape
        scaling = D ** (-0.5)
        q = (x @ Wq.T).reshape(b, t, 2 * H, D)
        k = (x @ Wk.T).reshape(b, t, 2 * H, D)
        v = (x @ Wv.T).reshape(b, t, H, 2 * D)
        freqs, scale = _rope_tables(t, D)
        q = _apply_rope(q, freqs, scale)
        k = _apply_rope(k, freqs, 1.0 / scale)
        q = jnp.transpose(q, (0, 2, 1, 3)) * scaling
        k = jnp.transpose(k, (0, 2, 1, 3))
        v = jnp.transpose(v, (0, 2, 1, 3))
        scores = jnp.einsum('bhtd,bhsd->bhts', q, k)
        probs = jax.nn.softmax(scores.astype(jnp.float32), axis=-1).astype(scores.dtype)
        lam1 = jnp.exp(jnp.sum(lambda_q1 * lambda_k1))
        lam2 = jnp.exp(jnp.sum(lambda_q2 * lambda_k2))
        lam = lam1 - lam2 + LAMBDA_INIT
        probs = probs.reshape(b, H, 2, t, t)
        diff = probs[:, :, 0] - lam * probs[:, :, 1]
        attn = jnp.einsum('bhts,bhsd->bhtd', diff, v)
        attn = attn * jax.lax.rsqrt(jnp.mean(attn * attn, axis=-1, keepdims=True) + 1e-05)
        attn = attn * (1.0 - LAMBDA_INIT)
        attn = jnp.transpose(attn, (0, 2, 1, 3)).reshape(b, t, e)
        return attn @ Wo.T

    def _L2_ffn_ref(x, Wg, w1, w2):
        import jax, jax.numpy as jnp
        import numpy as np
        d = x.shape[-1]
        xr = x.reshape(-1, d)
        S = xr.shape[0]
        E = Wg.shape[1]
        C = (S + E - 1) // E
        gate = jax.nn.softmax(xr @ Wg, axis=-1)
        idx = jnp.argmax(gate, axis=1)
        gates_s = jnp.take_along_axis(gate, idx[:, None], axis=1)[:, 0]
        onehot = jax.nn.one_hot(idx, E, dtype=jnp.int32)
        loc = jnp.sum((jnp.cumsum(onehot, axis=0) - 1) * onehot, axis=1)
        valid = loc < C
        loc_pad = jnp.minimum(loc, C)
        dispatched = jnp.zeros((E, C + 1, d), dtype=x.dtype).at[idx, loc_pad].set(xr)
        dispatched = dispatched[:, :C]
        h = jax.nn.relu(jnp.einsum('ecm,emf->ecf', dispatched, w1))
        expert_out = jnp.einsum('ecf,efm->ecm', h, w2)
        gathered = expert_out[idx, jnp.minimum(loc, C - 1)]
        combined = gathered * (gates_s * valid.astype(x.dtype))[:, None]
        return combined.reshape(x.shape)

    def _L3_xattn_ref(q, k, v, Wq, b_q, Wk, b_k, Wv, b_v, Wo, b_o):
        import jax, jax.numpy as jnp
        import numpy as np
        D = 128
        H = 16
        DH = D // H
        B, Tq, _ = q.shape
        Tk = k.shape[1]
        Q = (q @ Wq + b_q).reshape(B, Tq, H, DH)
        K = (k @ Wk + b_k).reshape(B, Tk, H, DH)
        V = (v @ Wv + b_v).reshape(B, Tk, H, DH)
        scores = jnp.einsum('bthd,bshd->bhts', Q, K) / jnp.sqrt(jnp.float32(DH))
        P = jax.nn.softmax(scores, axis=-1)
        out = jnp.einsum('bhts,bshd->bthd', P, V).reshape(B, Tq, D)
        return out @ Wo + b_o

    def _L3_attn_ref(x, Wk, Wq, Wv, Wo, bo, kln_w, kln_b, qln_w, qln_b):
        import jax, jax.numpy as jnp
        import numpy as np
        import math
        HEADS = 16
        LN_EPS = 1e-05

        def _layernorm(x, w, b):
            mu = jnp.mean(x, axis=-1, keepdims=True)
            var = jnp.mean((x - mu) ** 2, axis=-1, keepdims=True)
            return (x - mu) * jax.lax.rsqrt(var + LN_EPS) * w + b
        b, t, e = x.shape
        h = HEADS
        s = e // h
        scale = 1.0 / math.sqrt(s)
        k = (x @ Wk).reshape(b, t, h, s)
        q = (x @ Wq).reshape(b, t, h, s)
        v = (x @ Wv).reshape(b, t, h, s)
        k = _layernorm(k, kln_w, kln_b)
        q = _layernorm(q, qln_w, qln_b)
        dot = jnp.einsum('bqhs,bkhs->bhqk', q, k) * scale
        causal = jnp.tril(jnp.ones((t, t), dtype=bool))
        dot = jnp.where(causal, dot, -jnp.inf)
        attn = jax.nn.softmax(dot, axis=-1)
        out = jnp.einsum('bhqk,bkhs->bqhs', attn, v).reshape(b, t, e)
        return out @ Wo + bo

    def _L3_ffn_ref(x, gate_w, gate_b, w1, b1, w2, b2, ws1, bs1, ws2, bs2):
        import jax, jax.numpy as jnp
        import numpy as np
        B, S, DIM = (4, 256, 128)
        E, K, HID = (8, 2, 512)
        orig_shape = x.shape
        xf = x.reshape(-1, DIM)
        logits = xf @ gate_w + gate_b
        top_w, top_i = jax.lax.top_k(logits, K)
        gw = jax.nn.softmax(top_w, axis=-1).astype(xf.dtype)
        combine = (gw[:, :, None] * jax.nn.one_hot(top_i, E, dtype=xf.dtype)).sum(axis=1)
        out = jnp.zeros_like(xf)
        for e in range(E):
            h = jax.nn.gelu(xf @ w1[e] + b1[e], approximate=False)
            out = out + combine[:, e:e + 1] * (h @ w2[e] + b2[e])
        shared = jax.nn.gelu(xf @ ws1 + bs1, approximate=False) @ ws2 + bs2
        return (out + shared).reshape(orig_shape)
    x = x + _L0_xattn_ref(_layernorm(x, axis=-1), ctx_1024, L0_xattn_Wq, L0_xattn_Wk, L0_xattn_Wv, L0_xattn_Wo, L0_xattn_bo)
    x = x + _L0_attn_ref(_layernorm(x, axis=-1), L0_attn_q1_w, L0_attn_q1_b, L0_attn_k1_w, L0_attn_k1_b, L0_attn_k2_w, L0_attn_k2_b, L0_attn_gw_w, L0_attn_gw_b, L0_attn_sw_w, L0_attn_sw_b, L0_attn_cp_w, L0_attn_cp_b)
    x = x + _L0_ffn_ref(_layernorm(x, axis=-1), L0_ffn_router_w, L0_ffn_bias, L0_ffn_gate_w, L0_ffn_up_w, L0_ffn_down_w, L0_ffn_sh_gate_w, L0_ffn_sh_up_w, L0_ffn_sh_down_w)
    x = x + _L1_xattn_ref(_layernorm(x, axis=-1), ctx_1024, ctx_1024, mask_1x1xSxS2_ik1, L1_xattn_wq, L1_xattn_bq, L1_xattn_wk, L1_xattn_bk, L1_xattn_wv, L1_xattn_bv, L1_xattn_wo, L1_xattn_bo, L1_xattn_wnq, L1_xattn_bnq, L1_xattn_wnk, L1_xattn_bnk, L1_xattn_temperature, L1_xattn_gamma)
    x = x + _L1_attn_ref(_layernorm(x, axis=-1), L1_attn_w_qkv, L1_attn_w_proj, L1_attn_b_proj, L1_attn_w_dwc, L1_attn_b_dwc)
    x = x + _L1_ffn_ref(_layernorm(x, axis=-1), L1_ffn_Wq, L1_ffn_routers, L1_ffn_leaf_keys, L1_ffn_leaf_values, L1_ffn_Wout_w, L1_ffn_Wout_b)
    x = x + _L2_xattn_ref(_layernorm(x, axis=-1), ctx_1024)
    x = x + _L2_attn_ref(_layernorm(x, axis=-1), L2_attn_Wq, L2_attn_Wk, L2_attn_Wv, L2_attn_Wo, L2_attn_lambda_q1, L2_attn_lambda_k1, L2_attn_lambda_q2, L2_attn_lambda_k2)
    x = x + _L2_ffn_ref(_layernorm(x, axis=-1), L2_ffn_Wg, L2_ffn_w1, L2_ffn_w2)
    x = x + _L3_xattn_ref(_layernorm(x, axis=-1), ctx_1024, ctx_1024, L3_xattn_Wq, L3_xattn_b_q, L3_xattn_Wk, L3_xattn_b_k, L3_xattn_Wv, L3_xattn_b_v, L3_xattn_Wo, L3_xattn_b_o)
    x = x + _L3_attn_ref(_layernorm(x, axis=-1), L3_attn_Wk, L3_attn_Wq, L3_attn_Wv, L3_attn_Wo, L3_attn_bo, L3_attn_kln_w, L3_attn_kln_b, L3_attn_qln_w, L3_attn_qln_b)
    x = x + _L3_ffn_ref(_layernorm(x, axis=-1), L3_ffn_gate_w, L3_ffn_gate_b, L3_ffn_w1, L3_ffn_b1, L3_ffn_w2, L3_ffn_b2, L3_ffn_ws1, L3_ffn_bs1, L3_ffn_ws2, L3_ffn_bs2)
    return x

_drawn_inputs = setup_inputs


def setup_inputs(seed=0):
    import zlib

    import numpy as np

    out = dict(_drawn_inputs(seed))
    spreads = {'L0_xattn_bo': (0.0, 0.1),
     'L0_ffn_bias': (0.0, 0.1),
     'L1_xattn_bq': (0.0, 0.1),
     'L1_xattn_bk': (0.0, 0.1),
     'L1_xattn_bv': (0.0, 0.1),
     'L1_xattn_bo': (0.0, 0.1),
     'L1_xattn_bnq': (0.0, 0.1),
     'L1_xattn_bnk': (0.0, 0.1),
     'L1_xattn_temperature': (1.0, 0.2),
     'L1_xattn_gamma': (1.0, 0.2),
     'L3_attn_bo': (0.0, 0.1),
     'L3_attn_kln_w': (1.0, 0.6),
     'L3_attn_kln_b': (0.0, 2.0),
     'L3_attn_qln_w': (1.0, 0.6),
     'L3_attn_qln_b': (0.0, 0.8),
     'L3_ffn_gate_b': (0.0, 0.294),
     'L3_ffn_b1': (0.0, 0.8),
     'L3_ffn_b2': (0.0, 0.352),
     'L3_ffn_bs1': (0.0, 0.706),
     'L3_ffn_bs2': (0.0, 0.1)}
    factors = {'L0_xattn_Wq': 2.916,
     'L0_attn_k1_w': 7.075,
     'L0_attn_k1_b': 5.631,
     'L0_attn_k2_w': 200.0,
     'L0_attn_k2_b': 200.0,
     'L0_attn_gw_w': 5.631,
     'L0_attn_sw_w': 8.0,
     'L1_ffn_Wq': 8.0,
     'L1_ffn_routers': 8.0,
     'L1_ffn_leaf_values': 5.63,
     'L1_ffn_Wout_w': 7.078,
     'L2_attn_Wq': 8.0,
     'L2_attn_Wk': 8.0,
     'L2_attn_lambda_q1': 8.0,
     'L2_attn_lambda_k1': 8.0,
     'L2_attn_lambda_q2': 8.0,
     'L2_attn_lambda_k2': 8.0,
     'L2_ffn_Wg': 8.0,
     'L2_ffn_w1': 8.0,
     'L2_ffn_w2': 8.0,
     'L3_xattn_Wq': 8.0,
     'L3_xattn_b_q': 8.0,
     'L3_xattn_Wk': 8.0,
     'L3_xattn_b_k': 200.0,
     'L3_xattn_Wv': 3.89,
     'L3_xattn_b_v': 8.0,
     'L3_xattn_Wo': 3.919,
     'L3_xattn_b_o': 4.683,
     'L3_ffn_w1': 3.167,
     'L3_ffn_w2': 2.879,
     'L3_ffn_ws1': 2.687}
    for name, (base, spread) in spreads.items():
        noise = np.random.default_rng([zlib.crc32(name.encode()), seed]).standard_normal(out[name].shape)
        drawn = base * np.exp(spread * noise) if base else spread * noise
        out[name] = jnp.asarray(drawn.astype(out[name].dtype))
    for name, factor in factors.items():
        out[name] = (out[name] * factor).astype(out[name].dtype)
    return out
```

```python
from contextlib import ExitStack

import numpy as np

import concourse.bass as bass
from concourse import mybir

F32 = mybir.dt.float32
BF16 = mybir.dt.bfloat16
I32 = mybir.dt.int32
ALU = mybir.AluOpType
ACT = mybir.ActivationFunctionType
AX = mybir.AxisListType

P = 128
B, Q = 32, 32
T = B * Q
KEYS = 257
NT = T // P
HB = 512
HALVES = (0, 1)
HD = 8
LN_EPS = 1e-5
SHAPE_SCALE = float(1.0 / np.sqrt(np.float32(HD)))
LAMBDA_INIT = 0.8 - 0.6 * float(np.exp(-0.3))
BIG = 3.0e38
CAPACITY = T // 16
FAR_SLOT = 4096.0

WEIGHTS = [
    ("L0_xattn_Wk", True), ("L0_xattn_Wv", True), ("L0_xattn_Wq", True), ("L0_xattn_Wo", True),
    ("L0_attn_q1_w", False), ("L0_attn_k1_w", False), ("L0_attn_k2_w", False), ("L0_attn_cp_w", False),
    ("L1_xattn_wq", False), ("L1_xattn_wk", False), ("L1_xattn_wv", False), ("L1_xattn_wo", False),
    ("L1_attn_w_proj", True), ("L1_ffn_Wq", True), ("L1_ffn_Wout_w", True),
    ("L2_attn_Wq", True), ("L2_attn_Wk", True), ("L2_attn_Wv", True), ("L2_attn_Wo", True),
    ("L3_xattn_Wq", False), ("L3_xattn_Wk", False), ("L3_xattn_Wv", False), ("L3_xattn_Wo", False),
    ("L3_attn_Wq", False), ("L3_attn_Wk", False), ("L3_attn_Wv", False), ("L3_attn_Wo", False),
]
MORE_WEIGHTS = ["L1a_q", "L1a_k", "L1a_v", "leaves0", "leaves1"]
WIDX = {n: i for i, n in enumerate([w for w, _ in WEIGHTS] + MORE_WEIGHTS)}
VECTORS = [
    "L0_xattn_bo", "L0_attn_q1_b", "L0_attn_k1_b", "L0_attn_k2_b", "L0_attn_cp_b",
    "L0_attn_gw_w", "L0_attn_gw_b", "L0_attn_sw_w", "L0_attn_sw_b",
    "L1_xattn_bq", "L1_xattn_bk", "L1_xattn_bv", "L1_xattn_bo", "L1_xattn_bnq", "L1_xattn_bnk",
    "L1_xattn_temperature", "L1_xattn_gamma", "L1_attn_b_proj", "L1_attn_b_dwc",
    "L1_ffn_Wout_b", "L3_xattn_b_q", "L3_xattn_b_k", "L3_xattn_b_v", "L3_xattn_b_o",
    "L3_attn_bo", "L3_attn_kln_w", "L3_attn_kln_b", "L3_attn_qln_w", "L3_attn_qln_b", "L3_ffn_bs2",
]
VIDX = {n: i for i, n in enumerate(VECTORS)}


def rope_tables():
    inv_freq = (1.0 / np.float32(10000.0) ** (np.arange(0, HD, 2, dtype=np.float32) / HD)).astype(np.float32)
    pos = np.arange(Q, dtype=np.float32)
    freqs = np.repeat(pos[:, None] * inv_freq[None, :], 2, axis=-1).astype(np.float32)
    sv = ((np.arange(0, HD, 2, dtype=np.float32) + np.float32(0.4 * HD)) / np.float32(1.4 * HD)).astype(np.float32)
    power = ((pos - Q // 2) / np.float32(512.0)).astype(np.float32)
    scale = (sv[None, :] ** power[:, None]).astype(np.float32)
    scale = np.concatenate([scale, scale], axis=-1)
    c, s = np.cos(freqs), np.sin(freqs)
    inv = np.float32(1.0) / scale
    return [x.T.astype(np.float32) for x in (c * scale, s * scale, c * inv, s * inv)]


def constant_blocks():
    p = np.arange(P)[:, None]
    c = np.arange(P)[None, :]
    head, col = p // HD, c // HD
    rot = np.zeros((P, P), np.float32)
    for i in range(0, P, 2):
        rot[i + 1, i] = -1.0
        rot[i, i + 1] = 1.0
    rope = [np.tile(x, (P // HD, 1)) for x in rope_tables()]
    q32 = np.arange(Q)[None, :]
    blocks = {
        "ident": p == c,
        "mean": np.full((P, P), 1.0 / P),
        "ones": np.ones((P, P)),
        "same_head": head == col,
        "head_mean": (head == col) / HD,
        "pair_mean": (p // 16 == c // 16) / 16.0,
        "in_four": (p % 32) // HD == c // 32,
        "in_two": (p % 32) // 16 == np.arange(64)[None, :] // 32,
        "causal_cap": np.where(q32 <= p % 32, BIG, -BIG),
        "causal_keep": (p % 32) <= q32,
        "rot": rot,
        "rope": np.concatenate(rope, axis=1),
        "seg_keep": np.broadcast_to(np.arange(P)[None, :] % Q != 0, (P, P)),
        "batch_of": p // 32 == np.arange(4)[None, :],
        "g_row": p == c // 32,
        "own_head": p // 32 == (c % 32) // HD,
        "q_of": p % 32 == q32,
        "key_back": np.broadcast_to(np.arange(KEYS)[None, :] - 512.0, (P, KEYS)),
        "slot_iota": np.broadcast_to(np.arange(T)[None, :], (P, T)),
        "slot_of": p + P * np.arange(NT)[None, :],
        "until": p <= c,
        "before16": np.broadcast_to((np.arange(16)[None, :] < np.arange(16)[:, None]).reshape(1, 256), (P, 256)),
        "rest16": np.broadcast_to(15.0 - np.arange(16)[None, :], (P, 16)),
        "expert_back": np.broadcast_to(np.arange(16)[None, :] - 64.0, (P, 16)),
    }
    return {k: np.ascontiguousarray(v, dtype=np.float32) for k, v in blocks.items()}


def part_selectors(n):
    r = np.arange(3 * n)[None, :, None] % n == np.arange(n)[:, None, None]
    return np.ascontiguousarray(np.broadcast_to(r, (n, 3 * n, P))).astype(mybir.dt.np(BF16))


CONST_COLS = {}
_at = 0
for _name, _block in constant_blocks().items():
    CONST_COLS[_name] = (_at, _block.shape[1])
    _at += _block.shape[1]
CONST_WIDTH = _at


FAMILIES = {
    "q_projected": [(n, 2) for n in ("l0x_q", "l0a_q", "l1x_qa", "l1a_q", "l1f_q", "l2a_q", "l3x_q", "l3a_q")],
    "k_projected": [(n, 2) for n in ("l0x_k", "l0a_k", "l2a_k", "l3a_k")],
    "v_projected": [(n, 2) for n in ("l0x_v", "l0a_v", "l2a_v", "l3a_v")],
    "v_copied": [(n, 2) for n in ("l0x_vc", "l0a_vc", "l1a_vc", "l2a_vc", "l3a_vc")],
    "q_copied": [(n, 2) for n in ("l0x_qc", "l1f_qc", "l2a_qc", "l3a_qc")],
    "k_copied": [(n, 2) for n in ("l0x_kc", "l2a_kc", "l3a_kc")],
    "out_projected": [(n, 2) for n in ("l0x_out", "l0a_out", "l0f_out", "l1x_out", "l1a_out", "l1f_out", "l2a_out",
                                       "l3x_out", "l3a_out", "l3f_out")],
    "block_masked": [(n + "_masked", 8) for n in ("l0x", "l0a", "l0b", "l2a", "l3a")],
    "block_scores": [(n + "_scores", 4) for n in ("l0x", "l0a", "l0b", "l2a", "l3a")],
    "block_pt": [(n + "_pt", 4) for n in ("l0x", "l0a", "l0b", "l2a", "l3a")],
    "block_o": [(n + "_o", 4) for n in ("l0x", "l0a", "l0b", "l2a", "l3a")],
    "block_o_read": [(n + "_o_read", 4) for n in ("l0x", "l0a", "l0b", "l2a", "l3a")],
    "block_y": [(n + "_y", 4) for n in ("l0x", "l0a", "l0b", "l2a", "l3a")],
    "block_s_read": [(n + "_s_read", 4) for n in ("l0x", "l2a", "l3a")],
    "block_sm": [(n + "_sm", 4) for n in ("l0x", "l3a")],
    "block_exp": [(n + "_exp", 4) for n in ("l0x", "l2a", "l3a")],
    "combine_parts": [("l0f_parts", 1), ("l3f_parts", 1)],
    "combine_turned": [("l0f_turned", 2), ("l3f_turned", 2)],
    "combine_copied": [("l0f_combt", 2), ("l3f_combt", 2)],
    "router_logits": [("l0f_logits", 1), ("l2f_logits", 1), ("l3f_logits", 1)],
    "projection_biased": [("l0a_kc", 2), ("l1x_qc", 2)],
    "operands_prepared": [("l0a_gb", 1), ("l1x_heads", 1), ("l2x_sq", 1), ("l2a_ls", 1)],
    "queries_ready": [("l0a_qp", 2), ("l1a_qf", 4), ("l2a_qrope", 2), ("l3a_qn", 1)],
    "keys_ready": [("l0a_kp", 2), ("l1a_kf", 2), ("l2a_krope", 2), ("l3a_kn", 2)],
    "attended": [("l0a_yy", 2), ("l1a_y", 2), ("l2a_yn", 2)],
    "logits_shifted": [("l2f_lg", 1), ("l3f_lg", 1)],
    "units_weighted": [("l0f_mix", 2 + 36), ("l3f_mix", 4 + 72)],
    "to_be_summed": [("l1x_o2", 2), ("l1a_qk", 2)],
    "squared": [("l1x_sq", 2), ("l2a_sq", 2)],
    "rms_ready": [("l1x_rms", 2), ("l2a_rms", 2)],
    "exp_ready": [("l2a_le", 1), ("l2f_e", 1), ("l3f_e", 1)],
    "activated": [("l0a_gs", 2), ("l0f_scores", 1), ("l1x_qt", 2), ("l1f_gs", 4)],
    "bank_copied": [("l0a_ec", 2), ("l1f_rc", 2), ("l2f_dc", 2), ("l3f_cc", 2)],
    "units_activated": [("l0f_silu", 2 + 36), ("l3f_gelu", 4 + 72)],
    "second_product": [("l0a_g", 2), ("l1x_qn", 2), ("l1a_qs", 4), ("l2a_qr", 2)],
    "third_product": [("l0a_r", 2), ("l2a_kr", 2)],
    "summed": [("l1x_ms", 2), ("l1a_den", 2), ("l2a_ms", 2)],
    "turned": [("l0a_e", 2), ("l1f_t", 4), ("l2f_xt", 1), ("l3f_ct", 2)],
    "expert_units": [("l0f_gate", 36), ("l2f_h", 16), ("l3f_h", 72)],
    "expert_w0": [("l0f_w0", 288), ("l2f_w0", 128), ("l3f_w0", 96)],
    "expert_w1": [("l0f_w1", 288), ("l2f_w1", 128), ("l3f_w1", 96)],
    "ctx_c0": [("l1x_c0", 256), ("l2x_c0", 128), ("l3x_c0", 256)],
    "ctx_c1": [("l1x_c1", 256), ("l2x_c1", 128), ("l3x_c1", 256)],
    **{"ctx_" + s: [("l1x_" + s, n), ("l3x_" + s, n)] for s, n in (
        ("k", B), ("ki", B + 2), ("kv", B + 2), ("vall", B + 2), ("kall", B + 2), ("kb0", 8 * B), ("kb1", 8 * B), ("s", 4 * B), ("mx", 4 * B), ("p", 4 * B), ("t", B), ("t0", B), ("t1", B),
        ("o", B), ("om", B), ("ot", B), ("att", B), ("qb", B), ("q0", 1))},
}
FAMILY = {}
for _family, _members in FAMILIES.items():
    _n = 0
    for _name, _count in _members:
        FAMILY[_name] = (_family, _n)
        _n += _count


def build(nc, io, layers):
    ctx = ExitStack()
    with ctx:
        def sb(name, shape, dt=F32):
            return ctx.enter_context(nc.sbuf_tensor(name, shape, dt))

        sems = {}

        def sem(name):
            name = FAMILY.get(name, (name, 0))[0]
            if name not in sems:
                sems[name] = ctx.enter_context(nc.semaphore(name))
            return sems[name]

        def since(name, n):
            return n + FAMILY.get(name, (name, 0))[1]

        ps = ctx.enter_context(nc.psum_tensor("ps", [P, 8, HB], F32))
        CST = sb("CST", [P, CONST_WIDTH])
        WTS = sb("WTS", [P, len(WIDX), P])
        VEC = sb("VEC", [P, len(VECTORS)])
        X = sb("X", [P, T])
        XN = sb("XN", [P, T])
        SCRATCH = sb("SCRATCH", [P, 6, T])
        A0, A1, A2, A3, A4, A5 = (SCRATCH[:, i, :] for i in range(6))
        TOK = sb("TOK", [P, NT, P])
        CT32 = sb("CT32", [P, B, Q])
        SHARED = sb("SHARED", [P, 12416])

        def part_of_shared(at, pattern, **sizes):
            n = int(np.prod(list(sizes.values())))
            return SHARED[:, at:at + n].rearrange(pattern, **sizes)

        MASKED = part_of_shared(0, "p (b c) -> p b c", b=B, c=P)
        SM = part_of_shared(4096, "p (r h k) -> p r h k", r=2, h=32, k=Q)
        PR = part_of_shared(6144, "p (r h k) -> p r h k", r=2, h=32, k=Q)
        PT = part_of_shared(8192, "p (r c) -> p r c", r=2, c=2 * HB)
        OM = part_of_shared(10240, "p (r c) -> p r c", r=2, c=2 * HB)
        KALL = part_of_shared(0, "p (b k) -> p b k", b=B, k=KEYS)
        VLAST = part_of_shared(B * KEYS, "p (b c) -> p b c", b=B, c=P)
        DIFF = sb("DIFF", [P, 2, 16, Q])
        ST = sb("ST", [P, 4, 64])

        def cst(name):
            a, n = CONST_COLS[name]
            return CST[:, a:a + n]

        def w(name):
            return WTS[:, WIDX[name], :]

        def vec(name):
            return VEC[:, VIDX[name]:VIDX[name] + 1]

        def half(x, h):
            return x[:, h * HB:(h + 1) * HB]

        def tile4(x, t):
            return x[:, t * P:(t + 1) * P].rearrange("p (b q) -> p b q", b=4)

        def over(x, axis, n):
            y = x.unsqueeze(axis)
            shape = list(y.shape)
            shape[axis] = n
            return y.broadcast_to(shape)

        EPS = sb("EPS", [P, 4])
        WNQ = sb("WNQ", [P, P])
        WNK = sb("WNK", [P, P])
        CONVW = sb("CONVW", [P, 3])
        ROUT = sb("ROUT", [P, 255])
        WG2 = sb("WG2", [P, 16])
        WG3 = sb("WG3", [P, 8])
        RW0 = sb("RW0", [P, 16])
        ROW = sb("ROW", [P, 32])
        SMALL_LOADS = 14

        v, a, pe_, pool_ = nc.vector, nc.scalar, nc.tensor, nc.gpsimd

        def norm_tensor(pe, name, n, src, sq, mat, src_ready, src_count):
            for h in HALVES:
                pe.wait_ge(sem(src_ready), since(src_ready, src_count + h + 1))
                pe.matmul(ps[:, h, :], cst(mat), half(src, h), start=True, stop=True).then_inc(sem(name + "_mean"), 1)
            for h in HALVES:
                pe.wait_ge(sem(name + "_sq"), since(name + "_sq", 2 * n + h + 1))
                pe.matmul(ps[:, 2 + h, :], cst(mat), half(sq, h), start=True, stop=True).then_inc(sem(name + "_var"), 1)

        def norm_scalar(act, name, n, xc, sq, sd, eps):
            for h in HALVES:
                act.wait_ge(sem(name + "_xc"), since(name + "_xc", 2 * n + h + 1))
                act.activation(half(sq, h), half(xc, h), ACT.Square).then_inc(sem(name + "_sq"), 1)
            for h in HALVES:
                act.wait_ge(sem(name + "_var"), since(name + "_var", 2 * n + h + 1))
                act.activation(half(sd, h), ps[:, 2 + h, :], ACT.Sqrt, bias=eps).then_inc(sem(name + "_sd"), 1)

        def norm_vector(dve, name, n, src, xc, sd, out, out_ready):
            for h in HALVES:
                dve.wait_ge(sem(name + "_mean"), since(name + "_mean", 2 * n + h + 1))
                dve.tensor_tensor(half(xc, h), half(src, h), ps[:, h, :], ALU.subtract).then_inc(sem(name + "_xc"), 1)
            for h in HALVES:
                dve.wait_ge(sem(name + "_sd"), since(name + "_sd", 2 * n + h + 1))
                dve.reciprocal(half(sd, h), half(sd, h))
                dve.drain()
                dve.tensor_tensor(half(out, h), half(xc, h), half(sd, h), ALU.mult).then_inc(sem(out_ready), 1)

        def ln_tensor(pe, n):
            norm_tensor(pe, "ln", n, X, A1, "mean", "x_ready", 2 * n)

        def ln_scalar(act, n):
            norm_scalar(act, "ln", n, A0, A1, A2, EPS[:, 0:1])

        def ln_vector(dve, n):
            norm_vector(dve, "ln", n, X, A0, A2, XN, "xn_ready")

        def project(pe, weight, src, banks, done, waits=()):
            for h in HALVES:
                for name, count in waits:
                    pe.wait_ge(sem(name), since(name, count + h))
                pe.matmul(ps[:, banks[h], :], weight, half(src, h), start=True, stop=True).then_inc(sem(done), 1)

        def add_to_residual(dve, name, banks, bias):
            for h in HALVES:
                dve.wait_ge(sem(name), since(name, h + 1))
                dve.scalar_tensor_tensor(out=half(X, h), in0=ps[:, banks[h], :], scalar=bias, in1=half(X, h),
                                         op0=ALU.add, op1=ALU.add).then_inc(sem("x_ready"), 1)

        def spread(pool, name, src, ready, base=0):
            for t in range(NT):
                if t % 4 == 0:
                    pool.wait_ge(sem(ready), since(ready, base + t // 4 + 1))
                pool.tensor_tensor(MASKED[:, 4 * t:4 * t + 4, :].rearrange("p b (h q) -> p b h q", h=4),
                                   over(tile4(src, t), 2, 4),
                                   over(cst("in_four").rearrange("p (h q) -> p h q", h=4), 1, 4),
                                   ALU.mult).then_inc(sem(name + "_masked"), 1)

        PAIRS = NT // 2

        def block_scores(pe, name, fixed, u, read):
            pe.wait_ge(sem(name + "_masked"), since(name + "_masked", 2 * u + 2))
            if u >= 1:
                pe.wait_ge(sem(name + read), since(name + read, u))
            for s in range(2):
                for b in range(4):
                    n = 4 * (2 * u + s) + b
                    for g in range(4):
                        m = pe.matmul(ps[32 * b:32 * b + 32, g, s * P:(s + 1) * P],
                                      fixed[32 * g:32 * g + 32, n * Q:(n + 1) * Q],
                                      MASKED[32 * g:32 * g + 32, n, :], start=True, stop=True)
            m.then_inc(sem(name + "_scores"), 1)

        def block_values(pe, name, values, u, width):
            pe.wait_ge(sem(name + "_pt"), since(name + "_pt", u + 1))
            if u >= 1:
                pe.wait_ge(sem(name + "_o_read"), since(name + "_o_read", u))
            for s in range(2):
                for b in range(4):
                    for g in range(4):
                        c = (2 * g + s) * width
                        m = pe.matmul(ps[32 * g:32 * g + 32, 4 + b, s * width:(s + 1) * width],
                                      values[32 * b:32 * b + 32, 2 * u + s, 32 * g:32 * g + 32],
                                      PT[32 * b:32 * b + 32, u % 2, c:c + width], start=True, stop=True)
            m.then_inc(sem(name + "_o"), 1)

        def block_tensor(pe, name, fixed, values, read, width=P):
            for u in range(PAIRS + 1):
                if u < PAIRS:
                    block_scores(pe, name, fixed, u, read)
                if u >= 1:
                    block_values(pe, name, values, u - 1, width)

        def block_take(dve, name, out, u, width=P):
            n = width // Q
            dve.wait_ge(sem(name + "_o"), since(name + "_o", u + 1))
            own = cst("in_four" if n == 4 else "in_two")
            om = OM[:, u % 2, 0:8 * width]
            dve.tensor_tensor(om.rearrange("p (b t c) -> p b t c", b=4, t=2),
                              ps[:, 4:8, 0:2 * width].rearrange("p b (t c) -> p b t c", t=2),
                              over(over(own, 1, 2), 1, 4), ALU.mult).then_inc(sem(name + "_o_read"), 1)
            dve.drain()
            for s in range(2):
                m = dve.tensor_reduce(tile4(out, 2 * u + s),
                                      om.rearrange("p (b t h q) -> p t b q h", b=4, t=2, h=n)[:, s], AX.X, ALU.add)
            m.then_inc(sem(name + "_y"), 1)

        def pair_scores(name):
            return ps[:, 0:4, 0:2 * P]

        def block_softmax_vector(dve, name, out, causal):
            for u in range(PAIRS + 2):
                if u < PAIRS:
                    dve.wait_ge(sem(name + "_scores"), since(name + "_scores", u + 1))
                    if u >= 2:
                        dve.wait_ge(sem(name + "_exp"), since(name + "_exp", u - 1))
                    sm = SM[:, u % 2]
                    s3 = pair_scores(name).rearrange("p g (c k) -> p g c k", k=Q)
                    sm3 = sm.rearrange("p (g c) k -> p g c k", g=4)
                    mx = ST[:, 0, 0:32]
                    if causal:
                        dve.tensor_tensor(sm3, s3, over(over(cst("causal_cap"), 1, 8), 1, 4),
                                          ALU.min).then_inc(sem(name + "_s_read"), 1)
                        dve.drain()
                        dve.tensor_reduce(mx, sm, AX.X, ALU.max)
                        dve.drain()
                        dve.tensor_tensor(sm, sm, over(mx, 2, Q), ALU.subtract).then_inc(sem(name + "_sm"), 1)
                    else:
                        mx3 = mx.rearrange("p (g c) -> p g c", g=4)
                        dve.tensor_reduce(mx3, s3, AX.X, ALU.max)
                        dve.drain()
                        dve.tensor_tensor(sm3, s3, over(mx3, 3, Q), ALU.subtract).then_inc(sem(name + "_s_read"), 1)
                if 1 <= u <= PAIRS:
                    n = u - 1
                    dve.wait_ge(sem(name + "_exp"), since(name + "_exp", n + 1))
                    pr = PR[:, n % 2]
                    total, inv = ST[:, 1, 0:32], ST[:, 2, 0:32]
                    dve.tensor_reduce(total, pr, AX.X, ALU.add)
                    dve.drain()
                    dve.reciprocal(inv, total)
                    dve.drain()
                    dve.tensor_tensor(pr, pr, over(inv, 2, Q), ALU.mult)
                    dve.drain()
                    if n >= 2:
                        dve.wait_ge(sem(name + "_o"), since(name + "_o", n - 1))
                    if name == "l2a":
                        two = pr.rearrange("p (h j) k -> p h j k", j=2)
                        diff = DIFF[:, n % 2]
                        dve.scalar_tensor_tensor(out=diff, in0=two[:, :, 1], scalar=NEG_LAMBDA[:], in1=two[:, :, 0],
                                                 op0=ALU.mult, op1=ALU.add)
                        dve.drain()
                        dve.transpose(PT[:, n % 2, 0:512],
                                      diff.rearrange("p h k -> p (h k)")).then_inc(sem(name + "_pt"), 1)
                    else:
                        dve.transpose(PT[:, n % 2], pr.rearrange("p h k -> p (h k)")).then_inc(sem(name + "_pt"), 1)
                if u >= 2:
                    block_take(dve, name, out, u - 2, 64 if name == "l2a" else P)

        def block_softmax_scalar(act, name, causal):
            for u in range(PAIRS):
                act.wait_ge(sem(name + ("_sm" if causal else "_s_read")), since(name + ("_sm" if causal else "_s_read"), u + 1))
                if u >= 2:
                    act.wait_ge(sem(name + "_pt"), since(name + "_pt", u - 1))
                act.activation(PR[:, u % 2], SM[:, u % 2], ACT.Exp).then_inc(sem(name + "_exp"), 1)

        def block_linear_vector(dve, name, out):
            for u in range(PAIRS + 1):
                if u < PAIRS:
                    dve.wait_ge(sem(name + "_scores"), since(name + "_scores", u + 1))
                    if u >= 2:
                        dve.wait_ge(sem(name + "_o"), since(name + "_o", u - 1))
                    dve.tensor_tensor(PT[:, u % 2].rearrange("p (g c k) -> p g c k", g=4, k=Q),
                                      pair_scores(name).rearrange("p g (c k) -> p g c k", k=Q),
                                      over(over(cst("causal_keep"), 1, 8), 1, 4), ALU.mult).then_inc(sem(name + "_pt"), 1)
                if u >= 1:
                    block_take(dve, name, out, u - 1)

        def l0x_tensor(pe):
            ctx32 = CT32[:].rearrange("p b q -> p (b q)")
            pe.wait_ge(sem("ld_first"), since("ld_first", 16))
            pe.wait_ge(sem("ld_ctx32"), since("ld_ctx32", 16))
            project(pe, w("L0_xattn_Wk"), ctx32, (6, 7), "l0x_k")
            for t in range(NT):
                m = pe.matmul(ps[:, 4 + t // 4, (t % 4) * P:(t % 4 + 1) * P], ctx32[:, t * P:(t + 1) * P], w("L0_xattn_Wv"),
                              start=True, stop=True)
                if t % 4 == 3:
                    m.then_inc(sem("l0x_v"), 1)
            ln_tensor(pe, 0)
            project(pe, w("L0_xattn_Wq"), XN, (6, 7), "l0x_q", [("xn_ready", 1), ("l0x_kc", 1)])
            pe.wait_ge(sem("l0x_qc"), since("l0x_qc", 2))
            pe.wait_ge(sem("l0x_vc"), since("l0x_vc", 2))
            block_tensor(pe, "l0x", A4, TOK, "_s_read")
            for h in HALVES:
                pe.wait_ge(sem("l0x_y"), since("l0x_y", 2 * h + 2))
                pe.matmul(ps[:, h, :], w("L0_xattn_Wo"), half(A5, h), start=True, stop=True).then_inc(sem("l0x_out"), 1)

        def l0x_scalar(act):
            for h in HALVES:
                act.wait_ge(sem("l0x_k"), since("l0x_k", h + 1))
                act.copy(half(A3, h), ps[:, 6 + h, :]).then_inc(sem("l0x_kc"), 1)
            for h in HALVES:
                act.wait_ge(sem("l0x_v"), since("l0x_v", h + 1))
                act.copy(TOK[:, 4 * h:4 * h + 4, :].rearrange("p t c -> p (t c)"), ps[:, 4 + h, :]).then_inc(sem("l0x_vc"), 1)
            ln_scalar(act, 0)
            for h in HALVES:
                act.wait_ge(sem("l0x_q"), since("l0x_q", h + 1))
                act.activation(half(A4, h), ps[:, 6 + h, :], ACT.Copy, scale=SHAPE_SCALE).then_inc(sem("l0x_qc"), 1)
            block_softmax_scalar(act, "l0x", True)

        def l0x_vector(dve):
            ln_vector(dve, 0)
            block_softmax_vector(dve, "l0x", A5, True)
            add_to_residual(dve, "l0x_out", (0, 1), vec("L0_xattn_bo"))

        def l0x_gpsimd(pool):
            pool.wait_ge(sem("ld_first"), since("ld_first", 16))
            spread(pool, "l0x", A3, "l0x_kc")

        SQD = float(np.sqrt(np.float32(HD)))
        K2_SCALE = float(0.02 / np.sqrt(np.float32(P)))
        GB = sb("GB", [P, 2, P])
        K2B = sb("K2B", [P, 1])

        def l0a_tensor(pe):
            ln_tensor(pe, 1)
            project(pe, w("L0_attn_q1_w"), XN, (4, 5), "l0a_q", [("xn_ready", 3)])
            project(pe, w("L0_attn_k1_w"), XN, (6, 7), "l0a_k")
            pe.wait_ge(sem("l0a_gb"), since("l0a_gb", 1))
            project(pe, GB[:, 0, :], XN, (0, 1), "l0a_g")
            project(pe, w("L0_attn_k2_w"), XN, (2, 3), "l0a_k2")
            project(pe, GB[:, 1, :], A1, (4, 5), "l0a_r", [("l0a_kc", 1)])
            for t in range(NT):
                m = pe.transpose(ps[:, 6 + t // 4, (t % 4) * P:(t % 4 + 1) * P], XN[:, t * P:(t + 1) * P], cst("ident"))
                if t % 4 == 3:
                    m.then_inc(sem("l0a_v"), 1)
            pe.wait_ge(sem("l0a_vc"), since("l0a_vc", 2))
            pe.wait_ge(sem("l0a_kp"), since("l0a_kp", 2))
            block_tensor(pe, "l0a", A3, TOK, "_pt")
            pe.wait_ge(sem("l0a_et"), since("l0a_et", 2))
            for t in range(NT):
                m = pe.transpose(ps[:, 4 + t // 4, (t % 4) * P:(t % 4 + 1) * P], A1[:, t * P:(t + 1) * P], cst("ident"))
                if t % 4 == 3:
                    m.then_inc(sem("l0a_e"), 1)
            pe.wait_ge(sem("l0a_ec"), since("l0a_ec", 2))
            block_tensor(pe, "l0b", A5, TOK, "_pt")
            for h in HALVES:
                pe.wait_ge(sem("l0a_yy"), since("l0a_yy", h + 1))
                pe.matmul(ps[:, h, :], w("L0_attn_cp_w"), half(A3, h), start=True, stop=True).then_inc(sem("l0a_out"), 1)

        def l0a_scalar(act):
            ln_scalar(act, 1)
            for h in HALVES:
                act.wait_ge(sem("l0a_g"), since("l0a_g", h + 1))
                act.activation(half(A2, h), ps[:, h, :], ACT.Sigmoid, bias=vec("L0_attn_gw_b")).then_inc(sem("l0a_gs"), 1)
            for h in HALVES:
                act.wait_ge(sem("l0a_k2"), since("l0a_k2", h + 1))
                act.activation(half(A5, h), ps[:, 2 + h, :], ACT.Sigmoid, bias=K2B[:], scale=K2_SCALE).then_inc(sem("l0a_k2s"), 1)
            for h in HALVES:
                act.wait_ge(sem("l0a_r"), since("l0a_r", h + 1))
                act.activation(half(A3, h), ps[:, 4 + h, :], ACT.Silu, bias=vec("L0_attn_sw_b")).then_inc(sem("l0a_rs"), 1)
            for h in HALVES:
                act.wait_ge(sem("l0a_v"), since("l0a_v", h + 1))
                act.copy(TOK[:, 4 * h:4 * h + 4, :].rearrange("p t c -> p (t c)"), ps[:, 6 + h, :]).then_inc(sem("l0a_vc"), 1)
            for h in HALVES:
                act.wait_ge(sem("l0a_gmax"), since("l0a_gmax", h + 1))
                act.activation(half(A2, h), half(A2, h), ACT.Ln).then_inc(sem("l0a_ln"), 1)
            for h in HALVES:
                act.wait_ge(sem("l0a_cum"), since("l0a_cum", h + 1))
                act.activation(half(A2, h), half(A4, h), ACT.Exp).then_inc(sem("l0a_gc"), 1)
            for h in HALVES:
                act.wait_ge(sem("l0a_e"), since("l0a_e", h + 1))
                act.copy(TOK[:, 4 * h:4 * h + 4, :].rearrange("p t c -> p (t c)"), ps[:, 4 + h, :]).then_inc(sem("l0a_ec"), 1)

        def l0a_vector(dve):
            dve.tensor_scalar(GB[:, 0, :], cst("same_head"), vec("L0_attn_gw_w"), None, ALU.mult)
            dve.tensor_scalar(GB[:, 1, :], cst("same_head"), vec("L0_attn_sw_w"), None, ALU.mult)
            dve.tensor_scalar(K2B[:], vec("L0_attn_k2_b"), K2_SCALE, None, ALU.mult).then_inc(sem("l0a_gb"), 1)
            ln_vector(dve, 1)
            for h in HALVES:
                dve.wait_ge(sem("l0a_q"), since("l0a_q", h + 1))
                dve.tensor_scalar(half(A0, h), ps[:, 4 + h, :], vec("L0_attn_q1_b"), None, ALU.add)
                dve.wait_ge(sem("l0a_k"), since("l0a_k", h + 1))
                dve.tensor_scalar(half(A1, h), ps[:, 6 + h, :], vec("L0_attn_k1_b"), None, ALU.add).then_inc(sem("l0a_kc"), 1)
            for h in HALVES:
                dve.wait_ge(sem("l0a_gs"), since("l0a_gs", h + 1))
                dve.tensor_scalar(half(A2, h), half(A2, h), 1e-6, None, ALU.max).then_inc(sem("l0a_gmax"), 1)
            for h in HALVES:
                dve.wait_ge(sem("l0a_ln"), since("l0a_ln", h + 1))
                for t in range(4 * h, 4 * h + 4):
                    last = dve.tensor_tensor_scan(A4[:, t * P:(t + 1) * P], cst("seg_keep"), A2[:, t * P:(t + 1) * P], 0.0,
                                                  ALU.mult, ALU.add)
                dve.drain()
                dve.tensor_scalar(half(A4, h), half(A4, h), -30.0, 30.0, ALU.max, ALU.min).then_inc(sem("l0a_cum"), 1)
            for h in HALVES:
                dve.wait_ge(sem("l0a_rs"), since("l0a_rs", h + 1))
                dve.tensor_tensor(half(A3, h), half(A3, h), half(A1, h), ALU.mult)
                dve.wait_ge(sem("l0a_gc"), since("l0a_gc", h + 1))
                dve.tensor_scalar(half(A2, h), half(A2, h), 1e-6, None, ALU.add)
                dve.drain()
                dve.tensor_scalar(half(A1, h), half(A0, h), 1.0 / SQD, None, ALU.mult)
                dve.drain()
                dve.tensor_tensor(half(A0, h), half(A0, h), half(A2, h), ALU.mult).then_inc(sem("l0a_qp"), 1)
                dve.drain()
                dve.scalar_tensor_tensor(out=half(A4, h), in0=half(A1, h), scalar=0.02, in1=half(A1, h), op0=ALU.mult,
                                         op1=ALU.min)
                dve.reciprocal(half(A2, h), half(A2, h))
                dve.drain()
                dve.tensor_tensor(half(A3, h), half(A3, h), half(A2, h), ALU.mult).then_inc(sem("l0a_kp"), 1)
            block_linear_vector(dve, "l0a", A2)
            dve.drain()
            for h in HALVES:
                def batches(x):
                    return half(x, h).rearrange("p (b q) -> p b q", q=Q)
                dve.memset(batches(A1)[:, :, Q - 1:Q], 0.0)
                dve.tensor_tensor(batches(A1)[:, :, 0:Q - 1], batches(XN)[:, :, 1:Q], batches(A2)[:, :, 0:Q - 1],
                                  ALU.subtract)
            dve.drain().then_inc(sem("l0a_et"), 2)
            block_linear_vector(dve, "l0b", A0)
            dve.drain()
            for h in HALVES:
                def batches(x):
                    return half(x, h).rearrange("p (b q) -> p b q", q=Q)
                dve.tensor_copy(batches(A3)[:, :, 0:1], batches(A2)[:, :, 0:1])
                dve.tensor_tensor(batches(A3)[:, :, 1:Q], batches(A2)[:, :, 1:Q], batches(A0)[:, :, 0:Q - 1], ALU.add)
                dve.drain().then_inc(sem("l0a_yy"), 1)
            add_to_residual(dve, "l0a_out", (0, 1), vec("L0_attn_cp_b"))

        def l0a_gpsimd(pool):
            spread(pool, "l0a", A0, "l0a_qp")
            pool.wait_ge(sem("l0a_scores"), since("l0a_scores", PAIRS))
            spread(pool, "l0b", A4, "l0a_kp")

        NEG_LAMBDA = sb("NEG_LAMBDA", [P, 1])

        E0 = 18
        TURNS = sb("TURNS", [P, B * 2 * P])

        def part_of_turns(at, pattern, **sizes):
            n = int(np.prod(list(sizes.values())))
            return TURNS[:, at:at + n].rearrange(pattern, **sizes)

        EW = part_of_turns(3084 + 2 * T, "p (r a n) -> p r a n", r=2, a=3, n=P)
        ESEL = sb("ESEL", [P, 2, P], BF16)
        RT = sb("RT", [P, 12, P])
        PARTS = sb("PARTS", [P, NT, 54], BF16)
        COMBT = sb("COMBT", [P, T], BF16)
        IDB = sb("IDB", [P, P], BF16)
        ZB = sb("ZB", [P, HB], BF16)
        HC = part_of_turns(3084, "p (r t) -> p r t", r=2, t=T)

        def rank(dve, values, out, n, big):
            m = big.rearrange("p (t j i) -> p t j i", t=NT, i=n)
            before = cst("before16").rearrange("p (j i) -> p j i", i=16)[:, 0:n, 0:n]
            dve.tensor_tensor(m, over(values, 2, n), over(values, 3, n), ALU.is_ge)
            dve.drain()
            dve.tensor_tensor(m, m, over(before, 1, NT), ALU.mult)
            dve.drain()
            rows, cols = RT[:, 10, 0:NT * n].rearrange("p (t j) -> p t j", t=NT), RT[:, 11, 0:NT * n].rearrange("p (t j) -> p t j", t=NT)
            dve.tensor_reduce(rows, m, AX.X, ALU.add)
            dve.tensor_reduce(cols, m.rearrange("p t j i -> p t i j"), AX.X, ALU.add)
            dve.drain()
            dve.tensor_tensor(rows, rows, cols, ALU.subtract)
            dve.drain()
            dve.tensor_tensor(out, rows, over(cst("rest16")[:, 16 - n:16], 1, NT), ALU.add)
            dve.drain()

        def split_parts(dve, comb, n, done):
            left = RT[:, 10, 0:NT * n] if n <= 16 else RT[:, 10:12, :].rearrange("p a b -> p (a b)")[:, 0:NT * n]
            left = left.rearrange("p (t e) -> p t e", t=NT)
            dve.tensor_copy(PARTS[:, :, 0:n], comb)
            dve.drain()
            dve.tensor_tensor(left, comb, PARTS[:, :, 0:n], ALU.subtract)
            dve.drain()
            dve.tensor_copy(PARTS[:, :, n:2 * n], left)
            dve.drain()
            dve.tensor_tensor(left, left, PARTS[:, :, n:2 * n], ALU.subtract)
            dve.drain()
            dve.tensor_copy(PARTS[:, :, 2 * n:3 * n], left).then_inc(sem(done), 1)

        def tiles(i, n=16, count=1):
            x = RT[:, i:i + count, :].rearrange("p a b -> p (a b)")
            return x[:, 0:NT * n].rearrange("p (t e) -> p t e", t=NT)

        def route_tensor(pe, weight, n):
            for t in range(NT):
                m = pe.matmul(ps[:, 0, t * n:(t + 1) * n], XN[:, t * P:(t + 1) * P], weight, start=True, stop=True)
            return m

        def turn_parts_tensor(pe, rows, name):
            pe.wait_ge(sem(name + "_parts"), since(name + "_parts", 1))
            for t in range(NT):
                m = pe.matmul(ps[0:rows, t // 4, (t % 4) * P:(t % 4 + 1) * P], PARTS[:, t, 0:rows], IDB[:], start=True, stop=True)
                if t % 4 == 3:
                    m.then_inc(sem(name + "_turned"), 1)

        def turn_parts_scalar(act, rows, name):
            for h in HALVES:
                act.wait_ge(sem(name + "_turned"), since(name + "_turned", h + 1))
                act.copy(half(COMBT, h)[0:rows], ps[0:rows, h, :]).then_inc(sem(name + "_combt"), 1)

        def l0f_tensor(pe):
            ln_tensor(pe, 2)
            pe.wait_ge(sem("xn_ready"), since("xn_ready", 6))
            pe.wait_ge(sem("ld_small"), since("ld_small", 16 * SMALL_LOADS))
            route_tensor(pe, RW0[:], 16).then_inc(sem("l0f_logits"), 1)
            turn_parts_tensor(pe, 54, "l0f")
            pe.wait_ge(sem("l0f_combt"), since("l0f_combt", 2))
            for h in HALVES:
                m = pe.matmul(ps[:, 6 + h, :], ZB[:, 0:P], ZB[:], start=True, stop=False, skip_group_check=True)
            m.then_inc(sem("l0f_down"), 1)

            def step(i, p):
                pe.wait_ge(sem("l0f_w%d" % p), since("l0f_w%d" % p, 32 * i + 32))
                for h in HALVES:
                    pe.wait_ge(sem("l0f_silu"), since("l0f_silu", 4 * i + 2 * p + h + 1))
                    pe.matmul(ps[:, h, :], EW[:, p, 0, :], half(XN, h), start=True, stop=True).then_inc(sem("l0f_gate"), 1)
                for h in HALVES:
                    pe.wait_ge(sem("l0f_mix"), since("l0f_mix", 4 * i + 2 * p + h + 1))
                    m = pe.matmul(ps[:, 6 + h, :], EW[:, 1 - p, 2, :], half(HC[:, 1 - p], h), start=False, stop=False,
                                  skip_group_check=True)
                m.then_inc(sem("l0f_down"), 1)
                for h in HALVES:
                    pe.matmul(ps[:, 2 + h, :], EW[:, p, 1, :], half(XN, h), start=True, stop=True)
                    pe.matmul(ps[:, 4 + h, :], ESEL[0:54, p, :], half(COMBT, h)[0:54], start=True, stop=True).then_inc(sem("l0f_up"), 1)

            with pe.Fori(0, E0 // 2) as i:
                step(i, 0)
                step(i, 1)
            for h in HALVES:
                pe.wait_ge(sem("l0f_mix"), since("l0f_mix", 2 * E0 + h + 1))
                pe.matmul(ps[:, 6 + h, :], EW[:, 1, 2, :], half(HC[:, 1], h), start=False, stop=True,
                          skip_group_check=True).then_inc(sem("l0f_out"), 1)

        def l0f_scalar(act):
            ln_scalar(act, 2)
            act.wait_ge(sem("l0f_logits"), since("l0f_logits", 1))
            act.activation(RT[:, 0, :], ps[:, 0, 0:P], ACT.Sigmoid).then_inc(sem("l0f_scores"), 1)
            turn_parts_scalar(act, 54, "l0f")
            act.drain().then_inc(sem("l0f_silu"), 2)
            with act.Fori(0, E0 // 2) as i:
                for p in range(2):
                    for h in HALVES:
                        act.wait_ge(sem("l0f_gate"), since("l0f_gate", 4 * i + 2 * p + h + 1))
                        act.wait_ge(sem("l0f_mix"), since("l0f_mix", 4 * i + 2 * p + h + 1))
                        act.activation(half(A0, h), ps[:, h, :], ACT.Silu).then_inc(sem("l0f_silu"), 1)

        def l0f_vector(dve):
            ln_vector(dve, 2)
            dve.memset(ZB[:], 0.0)
            dve.memset(HC[:, 1], 0.0)
            dve.memset(EW[:, 1, 2, :], 0.0)
            dve.tensor_copy(IDB[:], cst("ident"))
            dve.wait_ge(sem("l0f_scores"), since("l0f_scores", 1))
            scores, s = tiles(0), tiles(1)
            dve.tensor_tensor(s, scores, over(ROW[:, 0:16], 1, NT), ALU.add)
            dve.drain()
            four = RT[:, 1, :].rearrange("p (g a b) -> p g a b", a=2, b=2)
            hi, lo = (RT[:, k, 0:64].rearrange("p (g a) -> p g a", a=2) for k in (2, 3))
            dve.tensor_tensor(hi, four[:, :, :, 0], four[:, :, :, 1], ALU.max)
            dve.tensor_tensor(lo, four[:, :, :, 0], four[:, :, :, 1], ALU.min)
            dve.drain()
            top, low, second = RT[:, 4, 0:32], RT[:, 5, 0:32], RT[:, 6, 0:32]
            dve.tensor_tensor(top, hi[:, :, 0], hi[:, :, 1], ALU.max)
            dve.tensor_tensor(second, hi[:, :, 0], hi[:, :, 1], ALU.min)
            dve.tensor_tensor(low, lo[:, :, 0], lo[:, :, 1], ALU.max)
            dve.drain()
            dve.tensor_tensor(second, second, low, ALU.max)
            dve.drain()
            dve.tensor_tensor(top, top, second, ALU.add)
            dve.drain()
            big = SCRATCH[:, 0:2, :].rearrange("p a b -> p (a b)")
            grank = tiles(7, 4)
            rank(dve, tiles(4, 4), grank, 4, big[:, 0:P])
            dve.tensor_scalar(grank, grank, 2.0, None, ALU.is_lt)
            dve.drain()
            s4 = RT[:, 1, :].rearrange("p (g e) -> p g e", e=4)
            masked = RT[:, 8, :].rearrange("p (g e) -> p g e", e=4)
            gate4 = over(RT[:, 7, 0:32], 2, 4)
            dve.tensor_tensor(masked, s4, gate4, ALU.mult)
            dve.drain()
            dve.tensor_scalar(RT[:, 7, 0:32], RT[:, 7, 0:32], 1.0, None, ALU.subtract)
            dve.drain()
            dve.tensor_tensor(masked, masked, gate4, ALU.add)
            dve.drain()
            chosen = tiles(9)
            rank(dve, tiles(8), chosen, 16, big)
            dve.tensor_scalar(chosen, chosen, 4.0, None, ALU.is_lt)
            dve.drain()
            dve.tensor_tensor(chosen, chosen, scores, ALU.mult)
            dve.drain()
            total = RT[:, 2, 0:NT]
            dve.tensor_reduce(total, chosen, AX.X, ALU.add)
            dve.drain()
            dve.tensor_scalar(total, total, 1e-20, None, ALU.add)
            dve.drain()
            dve.reciprocal(total, total)
            dve.drain()
            dve.tensor_tensor(chosen, chosen, over(total, 2, 16), ALU.mult)
            comb = tiles(3, E0, 2)
            dve.memset(comb[:, :, 0:2], 1.0)
            dve.drain()
            dve.tensor_scalar(comb[:, :, 2:E0], chosen, 2.5, None, ALU.mult)
            dve.drain()
            split_parts(dve, comb, E0, "l0f_parts")
            dve.drain().then_inc(sem("l0f_mix"), 2)
            with dve.Fori(0, E0 // 2) as i:
                for p in range(2):
                    for h in HALVES:
                        dve.wait_ge(sem("l0f_silu"), since("l0f_silu", 4 * i + 2 * p + h + 3))
                        dve.wait_ge(sem("l0f_up"), since("l0f_up", 4 * i + 2 * p + h + 1))
                        dve.tensor_tensor(half(A1, h), half(A0, h), ps[:, 2 + h, :], ALU.mult)
                        dve.drain()
                        dve.tensor_tensor(half(HC[:, p], h), half(A1, h), ps[:, 4 + h, :], ALU.mult).then_inc(sem("l0f_mix"), 1)
            for h in HALVES:
                dve.wait_ge(sem("l0f_out"), since("l0f_out", h + 1))
                dve.tensor_tensor(half(X, h), ps[:, 6 + h, :], half(X, h), ALU.add).then_inc(sem("x_ready"), 1)

        def l0f_gpsimd(pool):
            pass

        def l0f_sync(sp):
            sp.wait_ge(sem("l0f_down"), since("l0f_down", 1))
            with sp.Fori(0, E0 // 2) as i:
                for p in range(2):
                    sp.wait_ge(sem("l0f_down"), since("l0f_down", 2 * i + p + 1))
                    sp.dma_start(EW[:, p].rearrange("p a b -> p (a b)"),
                                 io["l0f_w"][bass.ds(2 * i + p, 1), :, :].rearrange("a p c -> (a p) c")).then_inc(sem("l0f_w%d" % p), 16)
                    sp.dma_start(ESEL[0:54, p, :],
                                 io["l0f_sel"][bass.ds(2 * i + p, 1), :, :].rearrange("a p c -> (a p) c")).then_inc(sem("l0f_w%d" % p), 16)

        CB = sb("CB", [P, 2, KEYS])
        KI = sb("KI", [P, 2, KEYS])
        VALL = part_of_turns(0, "p (b c) -> p b c", b=B, c=2 * P)
        KB = CB
        QB = sb("QB", [P, 2, P])
        PX = sb("PX", [P, 2, 4, KEYS])
        PTX = sb("PTX", [P, 2, 2, HB])
        PTL = sb("PTL", [4, 2, P])
        OX = sb("OX", [P, 2, P])
        XST = sb("XST", [P, 2, 3, 4])
        ONEB = sb("ONEB", [P, P])
        ONEK = sb("ONEK", [P, P])
        KCAP = sb("KCAP", [P, KEYS])
        MASKI = sb("MASKI", [P, KEYS], I32)
        INVT = sb("INVT", [P, 1])

        def ctx_loads(sp, n):
            with sp.Fori(0, B // 2) as i:
                for p in range(2):
                    sp.wait_ge(sem(n + "_kv"), since(n + "_kv", 2 * i + p + 1))
                    sp.dma_start(CB[:, p, :], io["ctx"][:, bass.ds(2 * i + p, 1), :].rearrange("p a k -> p (a k)"))\
                        .then_inc(sem(n + "_c%d" % p), 16)

        def key_loads(sp, n):
            sp.wait_ge(sem(n + "_kall"), since(n + "_kall", B + 2))
            def load(b, p):
                sp.dma_start(KB[:, p, :], KALL[:, bass.ds(b, 1), :].rearrange("p a k -> p (a k)")).then_inc(sem(n + "_kb%d" % p), 16)
            load(0, 0)
            load(1, 1)
            with sp.Fori(1, B // 2) as i:
                for p in range(2):
                    sp.wait_ge(sem(n + "_s"), since(n + "_s", 4 * (2 * i + p - 1)))
                    load(2 * i + p, p)

        def kv_tensor(pe, n, wk, wv, wnk):
            with pe.Fori(0, B // 2) as i:
                for p in range(2):
                    pe.wait_ge(sem(n + "_c%d" % p), since(n + "_c%d" % p, 16 * i + 16))
                    pe.wait_ge(sem(n + "_ki"), since(n + "_ki", 2 * i + p + 1))
                    pe.matmul(ps[:, p, 0:KEYS], wk, CB[:, p, :], start=True, stop=True).then_inc(sem(n + "_k"), 1)
                    pe.wait_ge(sem(n + "_vall"), since(n + "_vall", 2 * i + p + 1))
                    for c in range(2):
                        pe.matmul(ps[:, 2 + p, c * P:(c + 1) * P], CB[:, p, c * P:(c + 1) * P], wv, start=True, stop=True)
                    pe.matmul(ps[0:4, 2 + p, 2 * P:3 * P], CB[:, p, KEYS - 1:KEYS].broadcast_to([P, 4]), wv,
                              start=True, stop=True).then_inc(sem(n + "_kv"), 1)
                if wnk is not None:
                    for p in range(2):
                        pe.wait_ge(sem(n + "_ki"), since(n + "_ki", 2 * i + p + 3))
                        pe.wait_ge(sem(n + "_kall"), since(n + "_kall", 2 * i + p + 1))
                        pe.matmul(ps[:, 4 + p, 0:KEYS], wnk, KI[:, p, :], start=True, stop=True).then_inc(sem(n + "_k2"), 1)

        def kv_scalar(act, n, bk, bnk):
            act.drain().then_inc(sem(n + "_ki"), 2)
            with act.Fori(0, B // 2) as i:
                for p in range(2):
                    act.wait_ge(sem(n + "_k"), since(n + "_k", 2 * i + p + 1))
                    if bnk is None:
                        act.wait_ge(sem(n + "_kall"), since(n + "_kall", 2 * i + p + 1))
                    act.activation(KI[:, p, :], ps[:, p, 0:KEYS], ACT.Identity, bias=bk).then_inc(sem(n + "_ki"), 1)
                if bnk is not None:
                    for p in range(2):
                        act.wait_ge(sem(n + "_k2"), since(n + "_k2", 2 * i + p + 1))
                        act.wait_ge(sem(n + "_kall"), since(n + "_kall", 2 * i + p + 1))
                        act.activation(PX[:, p, 0, :], ps[:, 4 + p, 0:KEYS], ACT.Tanh, bias=bnk).then_inc(sem(n + "_kt"), 1)

        def kv_vector(dve, n, two):
            dve.drain().then_inc(sem(n + "_vall"), 2)
            dve.drain().then_inc(sem(n + "_kv"), 2)
            dve.drain().then_inc(sem(n + "_kall"), 2)
            with dve.Fori(0, B // 2) as i:
                for p in range(2):
                    b = 2 * i + p
                    dve.wait_ge(sem(n + "_kv"), since(n + "_kv", b + 3))
                    dve.tensor_scalar(VALL[:, bass.ds(b, 1), :].rearrange("p a c -> p (a c)"), ps[:, 2 + p, 0:2 * P], 1.0, None,
                                      ALU.mult)
                    dve.tensor_tensor(VLAST[0:4, bass.ds(b, 1), :].rearrange("p a c -> p (a c)"), ps[0:4, 2 + p, 2 * P:3 * P],
                                      cst("g_row")[0:4], ALU.mult).then_inc(sem(n + "_vall"), 1)
                for p in range(2):
                    b = 2 * i + p
                    src = PX[:, p, 0, :] if two else KI[:, p, :]
                    dve.wait_ge(sem(n + ("_kt" if two else "_ki")), since(n + ("_kt" if two else "_ki"), b + (1 if two else 3)))
                    dve.tensor_scalar(KALL[:, bass.ds(b, 1), :].rearrange("p a k -> p (a k)"), src, 1.0, None,
                                      ALU.mult).then_inc(sem(n + "_kall"), 1)

        def pipeline(eng, step):
            for b in range(4):
                step(b, b % 2, b // 2)
            with eng.Fori(2, B // 2 - 1) as i:
                step(2 * i, 0, i)
                step(2 * i + 1, 1, i)
            for b in range(B - 2, B + 3):
                step(b, b % 2, b // 2)

        def is_static(b):
            return isinstance(b, int)

        def has(b, lag):
            return not is_static(b) or 0 <= b - lag < B

        def later(b, n):
            return not is_static(b) or b - n >= 0

        def ctx_tensor(pe, n, read):
            pe.wait_ge(sem(n + "_q0"), since(n + "_q0", 1))

            def step(b, p, i):
                o = 1 - p
                if has(b, 0):
                    pe.wait_ge(sem(n + "_kb%d" % p), since(n + "_kb%d" % p, 16 * i + 16))
                    pe.wait_ge(sem(n + "_qb"), since(n + "_qb", b + 1))
                    for g in range(4):
                        if later(b, 1):
                            pe.wait_ge(sem(n + read), since(n + read, 4 * b + g - 3))
                        pe.matmul(ps[:, g, 0:KEYS], QB[32 * g:32 * g + 32, p, :], KB[32 * g:32 * g + 32, p, :],
                                  start=True, stop=True).then_inc(sem(n + "_s"), 1)
                if has(b, 1):
                    pe.wait_ge(sem(n + "_p"), since(n + "_p", 4 * b))
                    if later(b, 2):
                        pe.wait_ge(sem(n + "_t0"), since(n + "_t0", b - 1))
                        pe.wait_ge(sem(n + "_t1"), since(n + "_t1", b - 1))
                    for c in range(2):
                        for g in range(4):
                            pe.transpose(ps[:, 6 + c, g * P:(g + 1) * P], PX[:, o, g, c * P:(c + 1) * P], cst("ident"))
                    pe.transpose(ps[0:4, 4, 0:P], PX[:, o, :, KEYS - 1:KEYS].rearrange("p g a -> p (g a)"), cst("ident"))\
                        .then_inc(sem(n + "_t"), 1)
                if has(b, 3):
                    pe.wait_ge(sem(n + "_om"), since(n + "_om", b - 2))
                    if later(b, 4):
                        pe.wait_ge(sem(n + "_att"), since(n + "_att", b - 3))
                    pe.matmul(ps[:, 4, 256:288], OX[:, o, :], cst("q_of"), start=True, stop=True).then_inc(sem(n + "_ot"), 1)
                if has(b, 2):
                    pe.wait_ge(sem(n + "_t0"), since(n + "_t0", b - 1))
                    pe.wait_ge(sem(n + "_t1"), since(n + "_t1", b - 1))
                    def of(x, a, z):
                        x = x[:, bass.ds(b - 2, 1), a:z] if not is_static(b) else x[:, b - 2:b - 1, a:z]
                        return x.rearrange("p a c -> p (a c)")
                    pe.matmul(ps[:, 5, 0:P], PTL[:, p, :], of(VLAST[0:4], 0, P), start=True, stop=False, skip_group_check=True)
                    for g in range(4):
                        for c in range(2):
                            m = pe.matmul(ps[:, 5, 32 * g:32 * g + 32], PTX[:, p, c, g * P:(g + 1) * P],
                                          of(VALL, c * P + 32 * g, c * P + 32 * g + 32), start=False, stop=(g == 3 and c == 1),
                                          skip_group_check=True)
                    m.then_inc(sem(n + "_o"), 1)

            pipeline(pe, step)

        def ctx_scalar(act, n, masked):
            def step(b, p, i):
                o = 1 - p
                if has(b, 0):
                    for g in range(4):
                        act.wait_ge(sem(n + "_mx"), since(n + "_mx", 4 * b + g + 1))
                        if later(b, 2) and not masked:
                            act.wait_ge(sem(n + "_t"), since(n + "_t", b - 1))
                        src = PX[:, p, g, :] if masked else ps[:, g, 0:KEYS]
                        act.activation(PX[:, p, g, :], src, ACT.Exp, bias=XST[:, p, 0, g:g + 1],
                                       accum_out=XST[:, p, 1, g:g + 1]).then_inc(sem(n + "_p"), 1)
                if has(b, 1):
                    act.wait_ge(sem(n + "_t"), since(n + "_t", b))
                    if later(b, 3):
                        act.wait_ge(sem(n + "_o"), since(n + "_o", b - 2))
                    act.copy(PTX[:, o, 0, :], ps[:, 6, :]).then_inc(sem(n + "_t0"), 1)

            pipeline(act, step)

        def ctx_vector(dve, n, masked, queries, out, bias):
            def columns(x, b):
                return x[:, b * Q:(b + 1) * Q] if is_static(b) else x[:, bass.ds(b * Q, Q)]

            def spread_queries(b, p):
                if later(b, 2):
                    dve.wait_ge(sem(n + "_s"), since(n + "_s", 4 * b - 4))
                dve.tensor_tensor(QB[:, p, :].rearrange("p (h q) -> p h q", h=4), over(columns(queries, b), 1, 4),
                                  cst("in_four").rearrange("p (h q) -> p h q", h=4), ALU.mult).then_inc(sem(n + "_qb"), 1)

            def step(b, p, i):
                o = 1 - p
                if is_static(b) and b == 0:
                    spread_queries(0, 0)
                if has(b, 0) and (not is_static(b) or b + 1 < B):
                    spread_queries(b + 1, o)
                if has(b, 0):
                    for g in range(4):
                        dve.wait_ge(sem(n + "_s"), since(n + "_s", 4 * b + g + 1))
                        if masked:
                            if later(b, 2):
                                dve.wait_ge(sem(n + "_t"), since(n + "_t", b - 1))
                            dve.tensor_tensor(PX[:, p, g, :], ps[:, g, 0:KEYS], KCAP[:], ALU.min).then_inc(sem(n + "_sr"), 1)
                            dve.drain()
                            src = PX[:, p, g, :]
                        else:
                            src = ps[:, g, 0:KEYS]
                        dve.tensor_reduce(XST[:, p, 0, g:g + 1], src, AX.X, ALU.max, negate=True).then_inc(sem(n + "_mx"), 1)
                if has(b, 1):
                    dve.wait_ge(sem(n + "_t"), since(n + "_t", b))
                    if later(b, 3):
                        dve.wait_ge(sem(n + "_o"), since(n + "_o", b - 2))
                    dve.tensor_copy(PTX[:, o, 1, :], ps[:, 7, :])
                    dve.reciprocal(XST[:, o, 2, :], XST[:, o, 1, :])
                if has(b, 3):
                    dve.wait_ge(sem(n + "_ot"), since(n + "_ot", b - 2))
                    dve.tensor_scalar(columns(out, b - 3), ps[:, 4, 256:288], bias, None, ALU.add).then_inc(sem(n + "_att"), 1)
                if has(b, 1):
                    dve.tensor_copy(PTL[:, o, :], ps[0:4, 4, 0:P])
                    dve.drain().then_inc(sem(n + "_t1"), 1)
                if has(b, 2):
                    dve.wait_ge(sem(n + "_o"), since(n + "_o", b - 1))
                    ox = OX[:, p, :].rearrange("p (g c) -> p g c", g=4)
                    dve.tensor_tensor(ox, ps[:, 5, 0:P].rearrange("p (g c) -> p g c", g=4), over(XST[:, p, 2, :], 2, 32), ALU.mult)
                    dve.drain()
                    dve.tensor_tensor(OX[:, p, :], OX[:, p, :], cst("own_head"), ALU.mult).then_inc(sem(n + "_om"), 1)

            pipeline(dve, step)

        def l1x_tensor(pe):
            ln_tensor(pe, 3)
            project(pe, w("L1_xattn_wq"), XN, (4, 5), "l1x_qa", [("xn_ready", 7)])
            pe.wait_ge(sem("l1x_heads"), since("l1x_heads", 1))
            project(pe, ONEB[:], A0, (6, 7), "l1x_qn", [("l1x_qc", 1)])
            kv_tensor(pe, "l1x", w("L1_xattn_wk"), w("L1_xattn_wv"), ONEK[:])
            ctx_tensor(pe, "l1x", "_sr")
            pe.wait_ge(sem("l1x_att"), since("l1x_att", B))
            for h in HALVES:
                pe.matmul(ps[:, h, :], w("L1_xattn_wo"), half(A2, h), start=True, stop=True).then_inc(sem("l1x_out"), 1)
            for h in HALVES:
                pe.wait_ge(sem("l1x_sq"), since("l1x_sq", h + 1))
                pe.matmul(ps[:, 2 + h, :], cst("mean"), half(A1, h), start=True, stop=True).then_inc(sem("l1x_ms"), 1)

        def l1x_scalar(act):
            ln_scalar(act, 3)
            for h in HALVES:
                act.wait_ge(sem("l1x_qn"), since("l1x_qn", h + 1))
                act.activation(half(A1, h), ps[:, 6 + h, :], ACT.Tanh, bias=vec("L1_xattn_bnq")).then_inc(sem("l1x_qt"), 1)
            kv_scalar(act, "l1x", vec("L1_xattn_bk"), vec("L1_xattn_bnk"))
            ctx_scalar(act, "l1x", True)
            for h in HALVES:
                act.wait_ge(sem("l1x_o2"), since("l1x_o2", h + 1))
                act.activation(half(A1, h), half(A0, h), ACT.Square).then_inc(sem("l1x_sq"), 1)
            for h in HALVES:
                act.wait_ge(sem("l1x_ms"), since("l1x_ms", h + 1))
                act.activation(half(A1, h), ps[:, 2 + h, :], ACT.Sqrt, bias=EPS[:, 1:2]).then_inc(sem("l1x_rms"), 1)

        def l1x_vector(dve):
            dve.tensor_tensor(ONEB[:], WNQ[:], cst("same_head"), ALU.mult)
            dve.tensor_tensor(ONEK[:], WNK[:], cst("same_head"), ALU.mult)
            dve.reciprocal(INVT[:], vec("L1_xattn_temperature"))
            dve.tensor_scalar(KCAP[:], MASKI[:], 0.0, None, ALU.is_equal)
            dve.drain()
            dve.tensor_scalar(PX[:, 0, 0, :], KCAP[:], -BIG, BIG, ALU.mult, ALU.add)
            dve.drain()
            dve.scalar_tensor_tensor(out=KCAP[:], in0=KCAP[:], scalar=-1.0e9, in1=PX[:, 0, 0, :], op0=ALU.mult, op1=ALU.add)
            dve.drain().then_inc(sem("l1x_heads"), 1)
            ln_vector(dve, 3)
            for h in HALVES:
                dve.wait_ge(sem("l1x_qa"), since("l1x_qa", h + 1))
                dve.tensor_scalar(half(A0, h), ps[:, 4 + h, :], vec("L1_xattn_bq"), None, ALU.add).then_inc(sem("l1x_qc"), 1)
            for h in HALVES:
                dve.wait_ge(sem("l1x_qt"), since("l1x_qt", h + 1))
                dve.tensor_scalar(half(A1, h), half(A1, h), SHAPE_SCALE, INVT[:], ALU.mult, ALU.mult)
            dve.drain()
            kv_vector(dve, "l1x", True)
            dve.drain().then_inc(sem("l1x_q0"), 1)
            ctx_vector(dve, "l1x", True, A1, A2, vec("L1_xattn_bv"))
            for h in HALVES:
                dve.wait_ge(sem("l1x_out"), since("l1x_out", h + 1))
                dve.tensor_scalar(half(A0, h), ps[:, h, :], vec("L1_xattn_bo"), None, ALU.add).then_inc(sem("l1x_o2"), 1)
            for h in HALVES:
                dve.wait_ge(sem("l1x_rms"), since("l1x_rms", h + 1))
                dve.reciprocal(half(A1, h), half(A1, h))
                dve.drain()
                dve.tensor_tensor(half(A0, h), half(A0, h), half(A1, h), ALU.mult)
                dve.drain()
                dve.scalar_tensor_tensor(out=half(X, h), in0=half(A0, h), scalar=vec("L1_xattn_gamma"), in1=half(X, h),
                                         op0=ALU.mult, op1=ALU.add).then_inc(sem("x_ready"), 1)

        def l1x_sync(sp):
            ctx_loads(sp, "l1x")
            key_loads(sp, "l1x")

        def nothing(eng):
            pass

        VO = part_of_shared(0, "p (t c) -> p t c", t=NT, c=132)
        KVM = part_of_shared(2048, "p (r b t c) -> p r b t c", r=2, b=4, t=2, c=P)
        KSUM = sb("KSUM", [P, B])

        def half_tok(x, h):
            return x[:, 4 * h:4 * h + 4, :].rearrange("p t c -> p (t c)")

        def l1a_tensor(pe):
            ln_tensor(pe, 4)
            project(pe, w("L1a_q"), XN, (4, 5), "l1a_q", [("xn_ready", 9)])
            for name, bank in (("L1a_k", 6), ("L1a_v", 0)):
                for t in range(NT):
                    m = pe.matmul(ps[:, bank + t // 4, (t % 4) * P:(t % 4 + 1) * P], XN[:, t * P:(t + 1) * P], w(name),
                                  start=True, stop=True)
                    if t % 4 == 3:
                        m.then_inc(sem("l1a_kv"), 1)
            for r, bank in ((0, 4), (1, 4)):
                for h in HALVES:
                    pe.wait_ge(sem("l1a_qf"), since("l1a_qf", 2 * r + h + 1))
                    pe.matmul(ps[:, bank + h, :], cst("same_head"), half(A0, h), start=True, stop=True).then_inc(sem("l1a_qs"), 1)
            pe.wait_ge(sem("l1a_vc"), since("l1a_vc", 2))
            pe.wait_ge(sem("l1a_kf"), since("l1a_kf", 2))
            for u in range(PAIRS):
                if u >= 1:
                    pe.wait_ge(sem("l1a_m"), since("l1a_m", u))
                for s in range(2):
                    t = 2 * u + s
                    for b in range(4):
                        m = pe.matmul(ps[:, b, s * 129:(s + 1) * 129], TOK[32 * b:32 * b + 32, t, :],
                                      VO[32 * b:32 * b + 32, t, 0:129], start=True, stop=True)
                m.then_inc(sem("l1a_w"), 1)
                if u >= 1:
                    l1a_out(pe, u - 1)
            l1a_out(pe, PAIRS - 1)
            for h in HALVES:
                pe.wait_ge(sem("l1a_qk"), since("l1a_qk", h + 1))
                pe.matmul(ps[:, 4 + h, :], cst("same_head"), half(A1, h), start=True, stop=True).then_inc(sem("l1a_den"), 1)
            project(pe, w("L1_attn_w_proj"), A3, (0, 1), "l1a_out", [("l1a_y", 1)])

        def l1a_out(pe, u):
            pe.wait_ge(sem("l1a_m"), since("l1a_m", u + 1))
            pe.wait_ge(sem("l1a_q2"), since("l1a_q2", 2))
            for s in range(2):
                for b in range(4):
                    c = (2 * u + s) * P + b * Q
                    m = pe.matmul(ps[:, 6 + u // 2, c % HB:c % HB + Q], KVM[:, u % 2, b, s, :], A0[:, c:c + Q], start=True, stop=True)
            m.then_inc(sem("l1a_num"), 1)

        def l1a_scalar(act):
            ln_scalar(act, 4)
            for h in HALVES:
                act.wait_ge(sem("l1a_kv"), since("l1a_kv", 3 + h))
                act.copy(VO[:, 4 * h:4 * h + 4, 0:P], ps[:, h, :].rearrange("p (t c) -> p t c", t=4)).then_inc(sem("l1a_vc"), 1)

        def l1a_vector(dve):
            ln_vector(dve, 4)
            dve.memset(VO[:, :, P:P + 1], 1.0)

            def token_norm(h, x):
                g = x.rearrange("p (g d) -> p g d", d=HD)
                total = RT[:, 0, 0:64]
                dve.tensor_reduce(total, g, AX.X, ALU.add)
                dve.drain()
                dve.reciprocal(total, total)
                dve.drain()
                dve.tensor_tensor(g, g, over(total, 2, HD), ALU.mult)
                dve.drain()

            for h in HALVES:
                dve.wait_ge(sem("l1a_q"), since("l1a_q", h + 1))
                dve.tensor_scalar(half(A0, h), ps[:, 4 + h, :], 0.0, 1e-6, ALU.max, ALU.add).then_inc(sem("l1a_qf"), 1)
            for h in HALVES:
                dve.wait_ge(sem("l1a_kv"), since("l1a_kv", 1 + h))
                k, sq = half_tok(TOK, h), half(A4, h)
                dve.tensor_scalar(k, ps[:, 6 + h, :], 0.0, 1e-6, ALU.max, ALU.add)
                dve.drain()
                token_norm(h, k)
                dve.tensor_tensor(sq, k, k, ALU.mult)
                dve.drain()
                dve.tensor_tensor(k, sq, k, ALU.mult)
                dve.drain()
                token_norm(h, k)
                dve.drain().then_inc(sem("l1a_kf"), 1)
            for r in range(2):
                for h in HALVES:
                    q, i, sq = half(A0, h), half(A1, h), half(A2, h)
                    dve.wait_ge(sem("l1a_qs"), since("l1a_qs", 2 * r + h + 1))
                    dve.reciprocal(i, ps[:, 4 + h, :])
                    dve.drain()
                    if r == 1:
                        dve.tensor_tensor(q, q, i, ALU.mult).then_inc(sem("l1a_q2"), 1)
                        continue
                    dve.tensor_tensor(q, q, i, ALU.mult)
                    dve.drain()
                    dve.tensor_tensor(sq, q, q, ALU.mult)
                    dve.drain()
                    dve.tensor_tensor(q, sq, q, ALU.mult).then_inc(sem("l1a_qf"), 1)
            for u in range(PAIRS):
                dve.wait_ge(sem("l1a_w"), since("l1a_w", u + 1))
                if u >= 2:
                    dve.wait_ge(sem("l1a_num"), since("l1a_num", u - 1))
                for s in range(2):
                    kv = ps[:, 0:4, s * 129:(s + 1) * 129]
                    dve.tensor_tensor(KVM[:, u % 2, :, s, :], kv[:, :, 0:P], over(cst("same_head"), 1, 4), ALU.mult)
                    dve.tensor_copy(KSUM[:, (2 * u + s) * 4:(2 * u + s) * 4 + 4], kv[:, :, P:P + 1].rearrange("p b a -> p (b a)"))
                dve.drain().then_inc(sem("l1a_m"), 1)
            for h in HALVES:
                def batches(x):
                    return half(x, h).rearrange("p (b q) -> p b q", q=Q)
                dve.tensor_tensor(batches(A1), batches(A0), over(KSUM[:, 16 * h:16 * h + 16], 2, Q),
                                  ALU.mult).then_inc(sem("l1a_qk"), 1)
            for h in HALVES:
                def batches(x):
                    return half(x, h).rearrange("p (b q) -> p b q", q=Q)
                z, y, o = half(A2, h), half(A4, h), half(A3, h)
                dve.wait_ge(sem("l1a_den"), since("l1a_den", h + 1))
                dve.tensor_scalar(z, ps[:, 4 + h, :], 1e-6, None, ALU.add)
                dve.drain()
                dve.reciprocal(z, z)
                dve.drain()
                dve.wait_ge(sem("l1a_num"), since("l1a_num", 2 * h + 2))
                dve.tensor_tensor(y, ps[:, 6 + h, :], z, ALU.mult)
                dve.drain()
                dve.tensor_scalar(o, y, CONVW[:, 1:2], vec("L1_attn_b_dwc"), ALU.mult, ALU.add)
                dve.drain()
                dve.scalar_tensor_tensor(out=batches(A3)[:, :, 1:Q], in0=batches(A4)[:, :, 0:Q - 1], scalar=CONVW[:, 0:1],
                                         in1=batches(A3)[:, :, 1:Q], op0=ALU.mult, op1=ALU.add)
                dve.drain()
                dve.scalar_tensor_tensor(out=batches(A3)[:, :, 0:Q - 1], in0=batches(A4)[:, :, 1:Q], scalar=CONVW[:, 2:3],
                                         in1=batches(A3)[:, :, 0:Q - 1], op0=ALU.mult, op1=ALU.add)
                dve.drain()
                dve.tensor_tensor(o, o, y, ALU.add).then_inc(sem("l1a_y"), 1)
            add_to_residual(dve, "l1a_out", (0, 1), vec("L1_attn_b_proj"))

        GATE = part_of_shared(0, "p (t n) -> p t n", t=NT, n=255)
        LEFT = part_of_shared(2048, "p (t n) -> p t n", t=NT, n=255)
        LP = [part_of_shared(4096 + 2048 * i, "p (t n) -> p t n", t=NT, n=256) for i in range(2)]
        LPT = part_of_shared(8192, "p (c n) -> p c n", c=2, n=T)

        def l1f_tensor(pe):
            ln_tensor(pe, 5)
            project(pe, w("L1_ffn_Wq"), XN, (4, 5), "l1f_q", [("xn_ready", 11)])
            for t in range(NT):
                pe.wait_ge(sem("l1f_qc"), since("l1f_qc", t // 4 + 1))
                m = pe.matmul(ps[:, t // 2, (t % 2) * 255:(t % 2 + 1) * 255], A0[:, t * P:(t + 1) * P], ROUT[:], start=True, stop=True)
                if t % 2 == 1:
                    m.then_inc(sem("l1f_g"), 1)
            pe.wait_ge(sem("l1f_lp"), since("l1f_lp", 1))
            for c in range(2):
                for t in range(NT):
                    m = pe.transpose(ps[:, 4 + 2 * c + t // 4, (t % 4) * P:(t % 4 + 1) * P], LP[1][:, t, c * P:(c + 1) * P], cst("ident"))
                    if t % 4 == 3:
                        m.then_inc(sem("l1f_t"), 1)
            pe.wait_ge(sem("l1f_lpt"), since("l1f_lpt", 4))
            for h in HALVES:
                pe.matmul(ps[:, h, :], w("leaves0"), half(LPT[:, 0, :], h), start=True, stop=False)
                pe.matmul(ps[:, h, :], w("leaves1"), half(LPT[:, 1, :], h), start=False, stop=True).then_inc(sem("l1f_r"), 1)
            project(pe, w("L1_ffn_Wout_w"), A1, (2, 3), "l1f_out", [("l1f_rc", 1)])

        def l1f_scalar(act):
            ln_scalar(act, 5)
            for h in HALVES:
                act.wait_ge(sem("l1f_q"), since("l1f_q", h + 1))
                act.copy(half(A0, h), ps[:, 4 + h, :]).then_inc(sem("l1f_qc"), 1)
            for u in range(4):
                act.wait_ge(sem("l1f_g"), since("l1f_g", u + 1))
                act.activation(GATE[:, 2 * u:2 * u + 2, :], ps[:, u, 0:510].rearrange("p (t n) -> p t n", t=2),
                               ACT.Sigmoid).then_inc(sem("l1f_gs"), 1)
            for c in range(2):
                for h in HALVES:
                    act.wait_ge(sem("l1f_t"), since("l1f_t", 2 * c + h + 1))
                    act.copy(half(LPT[:, c, :], h), ps[:, 4 + 2 * c + h, :]).then_inc(sem("l1f_lpt"), 1)
            for h in HALVES:
                act.wait_ge(sem("l1f_r"), since("l1f_r", h + 1))
                act.copy(half(A1, h), ps[:, h, :]).then_inc(sem("l1f_rc"), 1)

        def l1f_vector(dve):
            ln_vector(dve, 5)
            dve.wait_ge(sem("l1f_gs"), since("l1f_gs", 4))
            dve.tensor_scalar(LEFT, GATE, -1.0, 1.0, ALU.mult, ALU.add)
            dve.drain()
            dve.tensor_copy(LP[0][:, :, 0:1], LEFT[:, :, 0:1])
            dve.tensor_copy(LP[0][:, :, 1:2], GATE[:, :, 0:1])
            dve.drain()
            for level in range(1, 8):
                n = 2 ** level
                src, dst = LP[(level - 1) % 2][:, :, 0:n], LP[level % 2][:, :, 0:2 * n].rearrange("p t (n s) -> p t n s", s=2)
                dve.tensor_tensor(dst[:, :, :, 0], src, LEFT[:, :, n - 1:2 * n - 1], ALU.mult)
                dve.tensor_tensor(dst[:, :, :, 1], src, GATE[:, :, n - 1:2 * n - 1], ALU.mult)
                dve.drain()
            dve.drain().then_inc(sem("l1f_lp"), 1)
            add_to_residual(dve, "l1f_out", (2, 3), vec("L1_ffn_Wout_b"))

        CX = part_of_shared(0, "p (r b k) -> p r b k", r=2, b=4, k=KEYS)
        CTOK = part_of_shared(2056, "p (r b c n) -> p r b c n", r=2, b=4, c=2, n=P)
        SIM = part_of_shared(4104, "p (r k) -> p r k", r=2, k=KEYS)
        HIT = part_of_shared(4618, "p (r k) -> p r k", r=2, k=KEYS)
        RNB = part_of_shared(5132, "p (r k) -> p r k", r=2, k=KEYS)
        HITT = part_of_shared(5646, "p (r c n) -> p r c n", r=2, c=2, n=P)
        SQC = part_of_shared(6158, "p (g n) -> p g n", g=8, n=P)
        LASTROW = part_of_shared(7182, "p (b n) -> p b n", b=B, n=P)
        LASTT = sb("LASTT", [P, B])
        HITL = sb("HITL", [1, 2, P])
        RN = sb("RN", [P, 2, 8])
        RL = sb("RL", [P, 16])
        XC = sb("XC", [P, 2, 4])

        def l2x_sync(sp):
            sp.wait_ge(sem("x_ready"), since("x_ready", 14))
            sp.dma_start(LASTT[:], io["ctx_last_t"]).then_inc(sem("l2x_last"), 16)
            sp.dma_start(LASTROW[0:1].rearrange("p b n -> p (b n)"), io["ctx_last"]).then_inc(sem("l2x_last"), 16)
            for t in range(NT):
                if t >= 2:
                    sp.wait_ge(sem("l2x_pv"), since("l2x_pv", t - 1))
                sp.dma_start(CX[:, t % 2], io["ctx"][:, 4 * t:4 * t + 4, :]).then_inc(sem("l2x_c%d" % (t % 2)), 16)
                sp.dma_start(CTOK[:, t % 2], io["ctx_tok"][:, 4 * t:4 * t + 4]).then_inc(sem("l2x_c%d" % (t % 2)), 16)

        def l2x_tensor(pe):
            ln_tensor(pe, 6)
            pe.wait_ge(sem("l2x_sq"), since("l2x_sq", 1))
            for t in range(NT):
                pe.matmul(ps[:, 7, t:t + 1], A1[:, t * P:(t + 1) * P], cst("ones")[:, 0:1], start=True, stop=True)
                m = pe.matmul(ps[:, 7, 8 + t:9 + t], A2[:, t * P:(t + 1) * P], cst("ones")[:, 0:1], start=True, stop=True)
            m.then_inc(sem("l2x_n2"), 1)
            for t in range(NT + 1):
                if t < NT:
                    p = t % 2
                    pe.wait_ge(sem("l2x_c%d" % p), since("l2x_c%d" % p, 32 * (t // 2 + 1)))
                    if t >= 2:
                        pe.wait_ge(sem("l2x_sim"), since("l2x_sim", t - 1))
                    for b in range(4):
                        n = (4 * t + b) * Q
                        m = pe.matmul(ps[32 * b:32 * b + 32, p, 0:KEYS], XN[:, n:n + Q], CX[:, p, b, :], start=True, stop=True)
                    m.then_inc(sem("l2x_s"), 1)
                    pe.wait_ge(sem("l2x_rn"), since("l2x_rn", t + 1))
                    if t >= 2:
                        pe.wait_ge(sem("l2x_rnb"), since("l2x_rnb", t - 1))
                    for c in range(2):
                        for b in range(4):
                            m = pe.matmul(ps[32 * b:32 * b + 32, 2 + p, c * P:(c + 1) * P],
                                          RN[:, p, 4 * c + b:4 * c + b + 1].broadcast_to([P, Q]), cst("ident"), start=True, stop=True)
                    m.then_inc(sem("l2x_r"), 1)
                if t >= 1:
                    u, p = t - 1, (t - 1) % 2
                    pe.wait_ge(sem("l2x_hit"), since("l2x_hit", u + 1))
                    for c in range(2):
                        pe.transpose(ps[:, 4 + p, c * P:(c + 1) * P], HIT[:, p, c * P:(c + 1) * P], cst("ident"))
                    pe.transpose(ps[0:1, 4 + p, 2 * P:3 * P], HIT[:, p, KEYS - 1:KEYS], cst("ident")).then_inc(sem("l2x_ht"), 1)
                    pe.wait_ge(sem("l2x_hc"), since("l2x_hc", u + 1))
                    if u >= 1:
                        pe.wait_ge(sem("l2x_x"), since("l2x_x", u))
                    for b in range(4):
                        out = ps[:, 6, b * Q:(b + 1) * Q]
                        for c in range(2):
                            pe.matmul(out, CTOK[:, p, b, c, :], HITT[:, p, c, b * Q:(b + 1) * Q], start=(c == 0), stop=False)
                        m = pe.matmul(out, LASTROW[0:1, 4 * u + b, :], HITL[0:1, p, b * Q:(b + 1) * Q], start=False, stop=True)
                    m.then_inc(sem("l2x_pv"), 1)

        def l2x_scalar(act):
            ln_scalar(act, 6)
            act.wait_ge(sem("l2x_n2"), since("l2x_n2", 1))
            act.activation(RL[:], ps[:, 7, 0:16], ACT.Sqrt).then_inc(sem("l2x_nl"), 1)
            for t in range(NT + 1):
                if t < NT:
                    p = t % 2
                    act.wait_ge(sem("l2x_c%d" % p), since("l2x_c%d" % p, 32 * (t // 2 + 1)))
                    if t >= 1:
                        act.wait_ge(sem("l2x_ns"), since("l2x_ns", t))
                    act.activation(SQC, CTOK[:, p].rearrange("p b c n -> p (b c) n"), ACT.Square).then_inc(sem("l2x_sc"), 1)
                    act.wait_ge(sem("l2x_ns"), since("l2x_ns", t + 1))
                    act.activation(RN[:, p, :], RN[:, p, :], ACT.Sqrt).then_inc(sem("l2x_nr"), 1)
                    act.wait_ge(sem("l2x_r"), since("l2x_r", t + 1))
                    if t >= 2:
                        act.wait_ge(sem("l2x_sim"), since("l2x_sim", t - 1))
                    act.copy(RNB[:, p, 0:2 * P], ps[:, 2 + p, 0:2 * P]).then_inc(sem("l2x_rnb"), 1)
                if t >= 1:
                    u, p = t - 1, (t - 1) % 2
                    act.wait_ge(sem("l2x_ht"), since("l2x_ht", u + 1))
                    if u >= 2:
                        act.wait_ge(sem("l2x_pv"), since("l2x_pv", u - 1))
                    act.copy(HITT[:, p].rearrange("p c n -> p (c n)"), ps[:, 4 + p, 0:2 * P])
                    act.copy(HITL[0:1, p, :], ps[0:1, 4 + p, 2 * P:3 * P])
                    act.drain().then_inc(sem("l2x_hc"), 1)

        def l2x_vector(dve):
            ln_vector(dve, 6)
            dve.wait_ge(sem("l2x_last"), since("l2x_last", 32))
            dve.drain()
            dve.tensor_tensor(A2, XN[:], XN[:], ALU.mult)
            dve.tensor_tensor(A1.rearrange("p (b q) -> p b q", q=Q), over(LASTT[:], 2, Q), over(LASTT[:], 2, Q), ALU.mult)
            dve.drain().then_inc(sem("l2x_sq"), 1)
            dve.wait_ge(sem("l2x_nl"), since("l2x_nl", 1))
            dve.tensor_scalar(RL[:], RL[:], 1e-12, None, ALU.max)
            dve.drain()
            dve.reciprocal(RL[:], RL[:])
            dve.drain()
            for t in range(NT + 1):
                if t < NT:
                    p = t % 2
                    dve.wait_ge(sem("l2x_sc"), since("l2x_sc", t + 1))
                    if t >= 2:
                        dve.wait_ge(sem("l2x_r"), since("l2x_r", t - 1))
                    dve.tensor_reduce(RN[:, p, :].rearrange("p (c b) -> p b c", c=2), SQC.rearrange("p (b c) n -> p b c n", c=2),
                                      AX.X, ALU.add).then_inc(sem("l2x_ns"), 1)
                    dve.wait_ge(sem("l2x_nr"), since("l2x_nr", t + 1))
                    dve.tensor_scalar(RN[:, p, :], RN[:, p, :], 1e-12, None, ALU.max)
                    dve.drain()
                    dve.reciprocal(RN[:, p, :], RN[:, p, :]).then_inc(sem("l2x_rn"), 1)
                    dve.tensor_copy(RNB[:, p, 2 * P:KEYS], RL[:, t:t + 1])
                    dve.drain()
                    dve.wait_ge(sem("l2x_rnb"), since("l2x_rnb", t + 1))
                    dve.wait_ge(sem("l2x_s"), since("l2x_s", t + 1))
                    if t >= 2:
                        dve.wait_ge(sem("l2x_ht"), since("l2x_ht", t - 1))
                    sim, hit, x = SIM[:, p, :], HIT[:, p, :], XC[:, p, :]
                    dve.scalar_tensor_tensor(out=sim, in0=ps[:, p, 0:KEYS], scalar=RL[:, 8 + t:9 + t], in1=RNB[:, p, :],
                                             op0=ALU.mult, op1=ALU.mult).then_inc(sem("l2x_sim"), 1)
                    dve.drain()
                    dve.tensor_reduce(x[:, 0:1], sim, AX.X, ALU.max)
                    dve.drain()
                    dve.scalar_tensor_tensor(out=sim, in0=sim, scalar=x[:, 0:1], in1=cst("key_back"), op0=ALU.is_equal, op1=ALU.mult)
                    dve.drain()
                    dve.tensor_reduce(x[:, 1:2], sim, AX.X, ALU.min)
                    dve.drain()
                    dve.tensor_scalar(hit, cst("key_back"), x[:, 1:2], None, ALU.is_equal).then_inc(sem("l2x_hit"), 1)
                if t >= 1:
                    u = t - 1
                    dve.wait_ge(sem("l2x_pv"), since("l2x_pv", u + 1))
                    xs = X[:, u * P:(u + 1) * P]
                    dve.tensor_tensor(xs, ps[:, 6, 0:P], xs, ALU.add).then_inc(sem("l2x_x"), 1)
                    if u % 4 == 3:
                        dve.drain().then_inc(sem("x_ready"), 1)

        LROW = sb("LROW", [P, 4, HD])
        LSM = sb("LSM", [P, 4])

        def l2a_tensor(pe):
            ln_tensor(pe, 7)
            project(pe, w("L2_attn_Wq"), XN, (4, 5), "l2a_q", [("xn_ready", 15)])
            project(pe, w("L2_attn_Wk"), XN, (6, 7), "l2a_k")
            for t in range(NT):
                m = pe.matmul(ps[:, t // 4, (t % 4) * P:(t % 4 + 1) * P], XN[:, t * P:(t + 1) * P], w("L2_attn_Wv"), start=True, stop=True)
                if t % 4 == 3:
                    m.then_inc(sem("l2a_v"), 1)
            project(pe, cst("rot"), A0, (2, 3), "l2a_qr", [("l2a_qc", 1)])
            project(pe, cst("rot"), A1, (4, 5), "l2a_kr", [("l2a_kc", 1)])
            pe.wait_ge(sem("l2a_vc"), since("l2a_vc", 2))
            pe.wait_ge(sem("l2a_qrope"), since("l2a_qrope", 2))
            block_tensor(pe, "l2a", A2, TOK, "_s_read", 64)
            norm_part = (("l2a_y", A4),)
            for h in HALVES:
                pe.wait_ge(sem("l2a_sq"), since("l2a_sq", h + 1))
                pe.matmul(ps[:, h, :], cst("pair_mean"), half(A1, h), start=True, stop=True).then_inc(sem("l2a_ms"), 1)
            project(pe, w("L2_attn_Wo"), A0, (2, 3), "l2a_out", [("l2a_yn", 1)])

        def l2a_scalar(act):
            act.wait_ge(sem("l2a_ls"), since("l2a_ls", 1))
            act.activation(LSM[:, 0:2], LSM[:, 0:2], ACT.Exp).then_inc(sem("l2a_le"), 1)
            ln_scalar(act, 7)
            for h in HALVES:
                act.wait_ge(sem("l2a_q"), since("l2a_q", h + 1))
                act.copy(half(A0, h), ps[:, 4 + h, :]).then_inc(sem("l2a_qc"), 1)
            for h in HALVES:
                act.wait_ge(sem("l2a_k"), since("l2a_k", h + 1))
                act.copy(half(A1, h), ps[:, 6 + h, :]).then_inc(sem("l2a_kc"), 1)
            for h in HALVES:
                act.wait_ge(sem("l2a_v"), since("l2a_v", h + 1))
                act.copy(half_tok(TOK, h), ps[:, h, :]).then_inc(sem("l2a_vc"), 1)
            block_softmax_scalar(act, "l2a", False)
            for h in HALVES:
                act.wait_ge(sem("l2a_y"), since("l2a_y", 2 * h + 2))
                act.activation(half(A1, h), half(A4, h), ACT.Square).then_inc(sem("l2a_sq"), 1)
            for h in HALVES:
                act.wait_ge(sem("l2a_ms"), since("l2a_ms", h + 1))
                act.activation(half(A1, h), ps[:, h, :], ACT.Sqrt, bias=EPS[:, 0:1]).then_inc(sem("l2a_rms"), 1)

        def l2a_vector(dve):
            dve.tensor_tensor(LROW[:, 0, :], LROW[:, 0, :], LROW[:, 1, :], ALU.mult)
            dve.tensor_tensor(LROW[:, 2, :], LROW[:, 2, :], LROW[:, 3, :], ALU.mult)
            dve.drain()
            dve.tensor_reduce(LSM[:, 0:2], LROW[:].rearrange("p (a b) d -> p a b d", b=2)[:, :, 0], AX.X, ALU.add).then_inc(sem("l2a_ls"), 1)
            dve.wait_ge(sem("l2a_le"), since("l2a_le", 1))
            dve.tensor_tensor(NEG_LAMBDA[:], LSM[:, 1:2], LSM[:, 0:1], ALU.subtract)
            dve.drain()
            dve.tensor_scalar(NEG_LAMBDA[:], NEG_LAMBDA[:], LAMBDA_INIT, None, ALU.subtract)
            ln_vector(dve, 7)
            rope = cst("rope").rearrange("p (k q) -> p k q", k=4)

            def rotate(x, bank, k, out, done, scale):
                for h in HALVES:
                    dve.wait_ge(sem(done[0]), since(done[0], h + 1))
                    def batches(y):
                        return y.rearrange("p (b q) -> p b q", q=Q)
                    dve.tensor_tensor(batches(half(out, h)), batches(ps[:, bank + h, :]), over(rope[:, k + 1], 1, 16), ALU.mult)
                    dve.tensor_tensor(batches(half(A5, h)), batches(half(x, h)), over(rope[:, k], 1, 16), ALU.mult)
                    dve.drain()
                    dve.tensor_tensor(half(out, h), half(out, h), half(A5, h), ALU.add)
                    dve.drain()
                    if scale:
                        dve.tensor_scalar(half(out, h), half(out, h), SHAPE_SCALE, None, ALU.mult)
                        dve.drain()
                    dve.drain().then_inc(sem(done[1]), 1)

            rotate(A0, 2, 0, A2, ("l2a_qr", "l2a_qrope"), True)
            rotate(A1, 4, 2, A3, ("l2a_kr", "l2a_krope"), False)
            block_softmax_vector(dve, "l2a", A4, False)
            for h in HALVES:
                dve.wait_ge(sem("l2a_rms"), since("l2a_rms", h + 1))
                dve.reciprocal(half(A1, h), half(A1, h))
                dve.drain()
                dve.tensor_tensor(half(A0, h), half(A4, h), half(A1, h), ALU.mult)
                dve.drain()
                dve.tensor_scalar(half(A0, h), half(A0, h), 1.0 - LAMBDA_INIT, None, ALU.mult).then_inc(sem("l2a_yn"), 1)
            for h in HALVES:
                dve.wait_ge(sem("l2a_out"), since("l2a_out", h + 1))
                dve.tensor_tensor(half(X, h), ps[:, 2 + h, :], half(X, h), ALU.add).then_inc(sem("x_ready"), 1)

        def l2a_gpsimd(pool):
            spread(pool, "l2a", A3, "l2a_krope")

        DISPATCH = part_of_shared(0, "p (t s) -> p t s", t=NT, s=HB).bitcast(BF16)
        COLLECT = part_of_shared(4096, "p (s t) -> p s t", s=NT, t=HB).bitcast(BF16)
        XPARTS = part_of_shared(8192, "p (r t c) -> p r t c", r=3, t=NT, c=64).bitcast(BF16)
        YPARTS = part_of_shared(9728, "p (r t c) -> p r t c", r=3, t=NT, c=64).bitcast(BF16)
        BIGW = part_of_turns(0, "p (r c) -> p r c", r=3, c=1028)
        HR = sb("HR", [P, 2, 4, CAPACITY])
        SLOT = sb("SLOT", [P, 2, NT])
        OHB = sb("OHB", [P, P], BF16)
        UNTB = sb("UNTB", [P, 2, P], BF16)

        def three_parts(dve, x, parts, left):
            dve.tensor_copy(parts[:, 0], x)
            dve.drain()
            dve.tensor_tensor(left, x, parts[:, 0], ALU.subtract)
            dve.drain()
            dve.tensor_copy(parts[:, 1], left)
            dve.drain()
            dve.tensor_tensor(left, left, parts[:, 1], ALU.subtract)
            dve.drain()
            dve.tensor_copy(parts[:, 2], left)
            dve.drain()

        def as_tiles(x):
            return x.rearrange("p (t c) -> p t c", t=NT)

        def l2f_tensor(pe):
            ln_tensor(pe, 8)
            pe.wait_ge(sem("xn_ready"), since("xn_ready", 18))
            route_tensor(pe, WG2[:], 16).then_inc(sem("l2f_logits"), 1)
            for t in range(NT):
                m = pe.transpose(ps[:, 4 + t // 4, (t % 4) * P:(t % 4 + 1) * P], XN[:, t * P:(t + 1) * P], cst("ident"))
            m.then_inc(sem("l2f_xt"), 1)
            pe.wait_ge(sem("l2f_oh"), since("l2f_oh", 1))
            pe.matmul(ps[:, 1, 0:P], UNTB[:, 0, :], OHB[:], start=True, stop=True)
            pe.matmul(ps[:, 1, P:2 * P], UNTB[:, 1, :], OHB[:], start=True, stop=True).then_inc(sem("l2f_pre"), 1)
            for k in range(2):
                pe.wait_ge(sem("l2f_diag"), since("l2f_diag", k + 1))
                for t in range(NT):
                    m = pe.matmul(ps[:, 2 * k + t // 4, (t % 4) * P:(t % 4 + 1) * P], cst("ones"), (A3, A4)[k][:, t * P:(t + 1) * P],
                                  start=True, stop=True)
                m.then_inc(sem("l2f_row"), 1)
            pe.wait_ge(sem("l2f_disp"), since("l2f_disp", 1))
            for h in HALVES:
                n = 0
                for t in range(NT):
                    for r in range(3):
                        m = pe.matmul(ps[:, 6 + h, :], XPARTS[:, r, t, :], half(DISPATCH[:, t, :], h), start=(n == 0), stop=(n == 23))
                        n += 1
                m.then_inc(sem("l2f_ds"), 1)
            pe.wait_ge(sem("l2f_dc"), since("l2f_dc", 2))
            with pe.Fori(0, 8) as i:
                for p in range(2):
                    pe.wait_ge(sem("l2f_w%d" % p), since("l2f_w%d" % p, 16 * i + 16))
                    pe.wait_ge(sem("l2f_hr"), since("l2f_hr", 2 * i + p + 1))
                    for c in range(4):
                        m = pe.matmul(ps[:, p, c * CAPACITY:(c + 1) * CAPACITY], BIGW[:, p, c * P:(c + 1) * P],
                                      A0[:, bass.ds(CAPACITY * (2 * i + p), CAPACITY)], start=True, stop=True)
                    m.then_inc(sem("l2f_h"), 1)
                pe.wait_ge(sem("l2f_yc"), since("l2f_yc", i + 1))
                for p in range(2):
                    pe.wait_ge(sem("l2f_hr"), since("l2f_hr", 2 * i + p + 3))
                    for c in range(4):
                        m = pe.matmul(ps[64 * p:64 * p + 64, 2, 0:P], HR[:, p, c, :], BIGW[:, p, 512 + c * P:512 + (c + 1) * P],
                                      start=(c == 0), stop=(c == 3))
                    m.then_inc(sem("l2f_y"), 1)
            pe.wait_ge(sem("l2f_yp"), since("l2f_yp", 1))
            for h in HALVES:
                n = 0
                for t in range(NT):
                    for r in range(3):
                        m = pe.matmul(ps[:, 4 + h, :], YPARTS[:, r, t, :], half(COLLECT[:, t, :], h), start=(n == 0), stop=(n == 23))
                        n += 1
                m.then_inc(sem("l2f_out"), 1)

        def l2f_scalar(act):
            ln_scalar(act, 8)
            act.wait_ge(sem("l2f_lg"), since("l2f_lg", 1))
            act.activation(RT[:, 1, :], RT[:, 0, :], ACT.Exp).then_inc(sem("l2f_e"), 1)
            for k in range(2):
                act.wait_ge(sem("l2f_row"), since("l2f_row", k + 1))
                for h in HALVES:
                    act.copy(half((A1, A2)[k], h), ps[:, 2 * k + h, :])
                act.drain().then_inc(sem("l2f_rowc"), 1)
            for h in HALVES:
                act.wait_ge(sem("l2f_ds"), since("l2f_ds", h + 1))
                act.copy(half(A0, h), ps[:, 6 + h, :]).then_inc(sem("l2f_dc"), 1)
            act.drain().then_inc(sem("l2f_hr"), 2)
            with act.Fori(0, 8) as i:
                for p in range(2):
                    act.wait_ge(sem("l2f_h"), since("l2f_h", 2 * i + p + 1))
                    act.activation(HR[:, p].rearrange("p c s -> p (c s)"), ps[:, p, 0:4 * CAPACITY], ACT.Relu).then_inc(sem("l2f_hr"), 1)

        def l2f_vector(dve):
            dve.tensor_copy(UNTB[:, 0, :], cst("until"))
            dve.tensor_copy(UNTB[:, 1, :], cst("ones"))
            ln_vector(dve, 8)
            logit, e, oh, key = tiles(0), tiles(1), tiles(2), tiles(3)
            mx, total, gate, idx, loc = (RT[:, 4, 16 * k:16 * k + NT] for k in range(5))
            dve.wait_ge(sem("l2f_logits"), since("l2f_logits", 1))
            lg = ps[:, 0, 0:P].rearrange("p (t e) -> p t e", t=NT)
            dve.tensor_reduce(mx, lg, AX.X, ALU.max)
            dve.drain()
            dve.tensor_tensor(logit, lg, over(mx, 2, 16), ALU.subtract).then_inc(sem("l2f_lg"), 1)
            dve.wait_ge(sem("l2f_xt"), since("l2f_xt", 1))
            three_parts(dve, ps[:, 4:6, :].rearrange("p h (t c) -> p (h t) c", t=4), XPARTS, as_tiles(A5))
            dve.wait_ge(sem("l2f_e"), since("l2f_e", 1))
            dve.tensor_reduce(total, e, AX.X, ALU.add)
            dve.drain()
            dve.reciprocal(total, total)
            dve.drain()
            dve.tensor_tensor(e, e, over(total, 2, 16), ALU.mult)
            dve.drain()
            dve.tensor_reduce(gate, e, AX.X, ALU.max)
            dve.drain()
            dve.tensor_tensor(oh, e, over(gate, 2, 16), ALU.is_equal)
            dve.drain()
            dve.tensor_tensor(oh, oh, over(cst("expert_back"), 1, NT), ALU.mult)
            dve.drain()
            dve.tensor_reduce(idx, oh, AX.X, ALU.min)
            dve.drain()
            dve.tensor_tensor(oh, over(cst("expert_back"), 1, NT), over(idx, 2, 16), ALU.is_equal)
            dve.drain()
            dve.tensor_copy(OHB[:], RT[:, 2, :]).then_inc(sem("l2f_oh"), 1)
            dve.wait_ge(sem("l2f_pre"), since("l2f_pre", 1))
            dve.memset(key[:, 0:1, :], 0.0)
            dve.drain()
            for t in range(1, NT):
                dve.tensor_tensor(key[:, t:t + 1, :], key[:, t - 1:t, :], ps[:, 1, P + (t - 1) * 16:P + t * 16].unsqueeze(1), ALU.add)
                dve.drain()
            dve.tensor_tensor(RT[:, 3, :], RT[:, 3, :], ps[:, 1, 0:P], ALU.add)
            dve.drain()
            dve.tensor_tensor(RT[:, 3, :], RT[:, 3, :], RT[:, 2, :], ALU.mult)
            dve.drain()
            dve.tensor_reduce(loc, key, AX.X, ALU.add)
            dve.drain()
            dve.tensor_scalar(loc, loc, 1.0, None, ALU.subtract)
            dve.drain()
            slot = SLOT[:, 0, :]
            dve.tensor_scalar(slot, loc, float(CAPACITY), FAR_SLOT, ALU.is_ge, ALU.mult)
            dve.drain()
            dve.tensor_tensor(slot, slot, loc, ALU.add)
            dve.drain()
            dve.tensor_scalar(idx, idx, 64.0, float(CAPACITY), ALU.add, ALU.mult)
            dve.drain()
            dve.tensor_tensor(slot, slot, idx, ALU.add)
            dve.drain()
            dve.tensor_tensor(as_tiles(A3), over(cst("ident"), 1, NT), over(slot, 2, P), ALU.mult).then_inc(sem("l2f_diag"), 1)
            dve.tensor_tensor(as_tiles(A4), over(cst("ident"), 1, NT), over(gate, 2, P), ALU.mult).then_inc(sem("l2f_diag"), 1)
            for t in range(NT):
                dve.tensor_scalar(DISPATCH[:, t, :], cst("slot_iota"), slot[:, t:t + 1], None, ALU.is_equal)
            dve.drain().then_inc(sem("l2f_disp"), 1)
            dve.wait_ge(sem("l2f_rowc"), since("l2f_rowc", 1))
            for t in range(NT):
                dve.tensor_scalar(COLLECT[:, t, :], A1, cst("slot_of")[:, t:t + 1], None, ALU.is_equal)
            dve.drain().then_inc(sem("l2f_yc"), 1)
            with dve.Fori(0, 8) as i:
                dve.wait_ge(sem("l2f_y"), since("l2f_y", 2 * i + 2))
                dve.tensor_scalar(A5[:, bass.ds(P * i, P)], ps[:, 2, 0:P], 1.0, None, ALU.mult).then_inc(sem("l2f_yc"), 1)
            dve.drain()
            three_parts(dve, as_tiles(A5), YPARTS, as_tiles(A3))
            dve.drain().then_inc(sem("l2f_yp"), 1)
            dve.wait_ge(sem("l2f_rowc"), since("l2f_rowc", 2))
            for h in HALVES:
                dve.wait_ge(sem("l2f_out"), since("l2f_out", h + 1))
                dve.tensor_tensor(half(A3, h), ps[:, 4 + h, :], half(A2, h), ALU.mult)
                dve.drain()
                dve.tensor_tensor(half(X, h), half(X, h), half(A3, h), ALU.add).then_inc(sem("x_ready"), 1)

        def l2f_sync(sp):
            def load(e, p):
                src = io["l2f_w"][bass.ds(e, 1)] if not is_static(e) else io["l2f_w"][e:e + 1]
                sp.dma_start(BIGW[:, p, 0:1024], src.rearrange("a p c -> (a p) c")).then_inc(sem("l2f_w%d" % p), 16)
            load(0, 0)
            load(1, 1)
            with sp.Fori(1, 8) as i:
                for p in range(2):
                    sp.wait_ge(sem("l2f_y"), since("l2f_y", 2 * i + p - 1))
                    load(2 * i + p, p)

        def l3x_tensor(pe):
            ln_tensor(pe, 9)
            project(pe, w("L3_xattn_Wq"), XN, (4, 5), "l3x_q", [("xn_ready", 19)])
            kv_tensor(pe, "l3x", w("L3_xattn_Wk"), w("L3_xattn_Wv"), None)
            ctx_tensor(pe, "l3x", "_p")
            pe.wait_ge(sem("l3x_att"), since("l3x_att", B))
            for h in HALVES:
                pe.matmul(ps[:, h, :], w("L3_xattn_Wo"), half(A2, h), start=True, stop=True).then_inc(sem("l3x_out"), 1)

        def l3x_scalar(act):
            ln_scalar(act, 9)
            kv_scalar(act, "l3x", vec("L3_xattn_b_k"), None)
            ctx_scalar(act, "l3x", False)

        def l3x_vector(dve):
            ln_vector(dve, 9)
            for h in HALVES:
                dve.wait_ge(sem("l3x_q"), since("l3x_q", h + 1))
                dve.tensor_scalar(half(A1, h), ps[:, 4 + h, :], vec("L3_xattn_b_q"), SHAPE_SCALE, ALU.add, ALU.mult)
            dve.drain()
            kv_vector(dve, "l3x", False)
            dve.drain().then_inc(sem("l3x_q0"), 1)
            ctx_vector(dve, "l3x", False, A1, A2, vec("L3_xattn_b_v"))
            add_to_residual(dve, "l3x_out", (0, 1), vec("L3_xattn_b_o"))

        def l3x_sync(sp):
            ctx_loads(sp, "l3x")
            key_loads(sp, "l3x")

        def l3a_tensor(pe):
            ln_tensor(pe, 10)
            project(pe, w("L3_attn_Wq"), XN, (4, 5), "l3a_q", [("xn_ready", 21)])
            project(pe, w("L3_attn_Wk"), XN, (6, 7), "l3a_k")
            for t in range(NT):
                m = pe.matmul(ps[:, t // 4, (t % 4) * P:(t % 4 + 1) * P], XN[:, t * P:(t + 1) * P], w("L3_attn_Wv"), start=True, stop=True)
                if t % 4 == 3:
                    m.then_inc(sem("l3a_v"), 1)
            pe.wait_ge(sem("l3a_vc"), since("l3a_vc", 2))
            norm_tensor(pe, "hn", 0, A3, A1, "head_mean", "l3a_qc", 0)
            norm_tensor(pe, "hn", 1, A4, A1, "head_mean", "l3a_kc", 0)
            pe.wait_ge(sem("l3a_qn"), since("l3a_qn", 1))
            block_tensor(pe, "l3a", A3, TOK, "_s_read")
            for h in HALVES:
                pe.wait_ge(sem("l3a_y"), since("l3a_y", 2 * h + 2))
                pe.matmul(ps[:, h, :], w("L3_attn_Wo"), half(A5, h), start=True, stop=True).then_inc(sem("l3a_out"), 1)

        def l3a_scalar(act):
            ln_scalar(act, 10)
            for h in HALVES:
                act.wait_ge(sem("l3a_q"), since("l3a_q", h + 1))
                act.copy(half(A3, h), ps[:, 4 + h, :]).then_inc(sem("l3a_qc"), 1)
            for h in HALVES:
                act.wait_ge(sem("l3a_k"), since("l3a_k", h + 1))
                act.copy(half(A4, h), ps[:, 6 + h, :]).then_inc(sem("l3a_kc"), 1)
            for h in HALVES:
                act.wait_ge(sem("l3a_v"), since("l3a_v", h + 1))
                act.copy(half_tok(TOK, h), ps[:, h, :]).then_inc(sem("l3a_vc"), 1)
            norm_scalar(act, "hn", 0, A0, A1, A2, EPS[:, 0:1])
            norm_scalar(act, "hn", 1, A0, A1, A2, EPS[:, 0:1])
            block_softmax_scalar(act, "l3a", True)

        def l3a_vector(dve):
            ln_vector(dve, 10)
            norm_vector(dve, "hn", 0, A3, A0, A2, A3, "l3a_qm")
            dve.drain()
            dve.tensor_scalar(A3, A3, vec("L3_attn_qln_w"), vec("L3_attn_qln_b"), ALU.mult, ALU.add)
            dve.drain()
            dve.tensor_scalar(A3, A3, SHAPE_SCALE, None, ALU.mult).then_inc(sem("l3a_qn"), 1)
            norm_vector(dve, "hn", 1, A4, A0, A2, A4, "l3a_qm")
            dve.drain()
            dve.tensor_scalar(A4, A4, vec("L3_attn_kln_w"), vec("L3_attn_kln_b"), ALU.mult, ALU.add)
            dve.drain().then_inc(sem("l3a_kn"), 2)
            block_softmax_vector(dve, "l3a", A5, True)
            add_to_residual(dve, "l3a_out", (0, 1), vec("L3_attn_bo"))

        def l3a_gpsimd(pool):
            spread(pool, "l3a", A4, "l3a_kn")

        E3 = 9
        ESEL3 = sb("ESEL3", [32, 3, P], BF16)
        B2 = sb("B2", [E3, P])
        COMB9 = sb("COMB9", [E3, T])

        def l3f_tensor(pe):
            ln_tensor(pe, 11)
            pe.wait_ge(sem("xn_ready"), since("xn_ready", 24))
            route_tensor(pe, WG3[:], 8).then_inc(sem("l3f_logits"), 1)
            turn_parts_tensor(pe, 3 * E3, "l3f")
            comb = tiles(3, E3)
            for t in range(NT):
                m = pe.transpose(ps[0:E3, 2 + t // 4, (t % 4) * P:(t % 4 + 1) * P], comb[:, t, :], cst("ident"))
                if t % 4 == 3:
                    m.then_inc(sem("l3f_ct"), 1)
            pe.wait_ge(sem("l3f_combt"), since("l3f_combt", 2))
            for h in HALVES:
                pe.wait_ge(sem("l3f_cc"), since("l3f_cc", h + 1))
                pe.matmul(ps[:, 6 + h, :], B2[:], half(COMB9, h), start=True, stop=False, skip_group_check=True)
            with pe.Fori(0, E3 // 3) as i:
                for r in range(3):
                    e = 3 * i + r
                    pe.wait_ge(sem("l3f_w%d" % r), since("l3f_w%d" % r, 32 * i + 32))
                    for c in range(4):
                        n, o = 8 * e + 2 * c, (r - 1) % 3 if c == 0 else r
                        for h in HALVES:
                            pe.wait_ge(sem("l3f_gelu"), since("l3f_gelu", n + h + 1))
                            pe.matmul(ps[:, 2 * (c % 2) + h, :], BIGW[:, r, c * P:(c + 1) * P], half(XN, h),
                                      start=True, stop=True).then_inc(sem("l3f_h"), 1)
                        for h in HALVES:
                            pe.wait_ge(sem("l3f_mix"), since("l3f_mix", n + h + 3))
                            d = (c - 1) % 4
                            m = pe.matmul(ps[:, 6 + h, :], BIGW[:, o, 512 + d * P:512 + (d + 1) * P], half(HC[:, 1 - c % 2], h),
                                          start=False, stop=False, skip_group_check=True)
                        if c == 0:
                            m.then_inc(sem("l3f_used"), 1)
                            for h in HALVES:
                                m = pe.matmul(ps[:, 4 + h, :], ESEL3[0:3 * E3, r, :], half(COMBT, h)[0:3 * E3], start=True, stop=True)
                            m.then_inc(sem("l3f_b"), 1)
            for h in HALVES:
                pe.wait_ge(sem("l3f_mix"), since("l3f_mix", 8 * E3 + h + 3))
                pe.matmul(ps[:, 6 + h, :], BIGW[:, 2, 896:1024], half(HC[:, 1], h), start=False, stop=True,
                          skip_group_check=True).then_inc(sem("l3f_out"), 1)

        def l3f_scalar(act):
            ln_scalar(act, 11)
            act.wait_ge(sem("l3f_lg"), since("l3f_lg", 1))
            act.activation(tiles(2, 8), tiles(1, 8), ACT.Exp).then_inc(sem("l3f_e"), 1)
            turn_parts_scalar(act, 3 * E3, "l3f")
            for h in HALVES:
                act.wait_ge(sem("l3f_ct"), since("l3f_ct", h + 1))
                act.copy(half(COMB9, h), ps[0:E3, 2 + h, :]).then_inc(sem("l3f_cc"), 1)
            act.drain().then_inc(sem("l3f_gelu"), 4)
            with act.Fori(0, E3 // 3) as i:
                for r in range(3):
                    for c in range(4):
                        for h in HALVES:
                            n = 8 * (3 * i + r) + 2 * c + h
                            act.wait_ge(sem("l3f_h"), since("l3f_h", n + 1))
                            act.wait_ge(sem("l3f_mix"), since("l3f_mix", n + 1))
                            act.activation(half((A0, A1)[c % 2], h), ps[:, 2 * (c % 2) + h, :], ACT.Gelu,
                                           bias=BIGW[:, r, 1024 + c:1025 + c]).then_inc(sem("l3f_gelu"), 1)

        def l3f_vector(dve):
            ln_vector(dve, 11)
            dve.memset(HC[:, 1], 0.0)
            dve.memset(BIGW[:, 2, 896:1024], 0.0)
            logit, less, ex, comb = tiles(0, 8), tiles(1, 8), tiles(2, 8), tiles(3, E3)
            mx, total = RT[:, 5, 0:NT], RT[:, 5, 16:16 + NT]
            dve.wait_ge(sem("l3f_logits"), since("l3f_logits", 1))
            dve.tensor_tensor(logit, ps[:, 0, 0:64].rearrange("p (t e) -> p t e", t=NT), over(ROW[:, 16:24], 1, NT), ALU.add)
            dve.drain()
            dve.tensor_reduce(mx, logit, AX.X, ALU.max)
            dve.drain()
            dve.tensor_tensor(less, logit, over(mx, 2, 8), ALU.subtract).then_inc(sem("l3f_lg"), 1)
            chosen = tiles(9, 8)
            rank(dve, logit, chosen, 8, SCRATCH[:, 0, 0:512])
            dve.tensor_scalar(chosen, chosen, 2.0, None, ALU.is_lt)
            dve.drain()
            dve.wait_ge(sem("l3f_e"), since("l3f_e", 1))
            dve.tensor_tensor(chosen, chosen, ex, ALU.mult)
            dve.drain()
            dve.tensor_reduce(total, chosen, AX.X, ALU.add)
            dve.drain()
            dve.reciprocal(total, total)
            dve.memset(comb[:, :, 0:1], 1.0)
            dve.drain()
            dve.tensor_tensor(comb[:, :, 1:E3], chosen, over(total, 2, 8), ALU.mult)
            dve.drain()
            split_parts(dve, comb, E3, "l3f_parts")
            dve.drain().then_inc(sem("l3f_mix"), 4)
            with dve.Fori(0, E3 // 3) as i:
                for r in range(3):
                    dve.wait_ge(sem("l3f_b"), since("l3f_b", 3 * i + r + 1))
                    for c in range(4):
                        for h in HALVES:
                            n = 8 * (3 * i + r) + 2 * c + h
                            dve.wait_ge(sem("l3f_gelu"), since("l3f_gelu", n + 5))
                            dve.tensor_tensor(half(HC[:, c % 2], h), half((A0, A1)[c % 2], h), ps[:, 4 + h, :],
                                              ALU.mult).then_inc(sem("l3f_mix"), 1)
            for h in HALVES:
                dve.wait_ge(sem("l3f_out"), since("l3f_out", h + 1))
                dve.tensor_tensor(half(X, h), ps[:, 6 + h, :], half(X, h), ALU.add).then_inc(sem("x_ready"), 1)

        def l3f_sync(sp):
            def load(e, r):
                src = io["l3f_w"][bass.ds(e, 1)] if not is_static(e) else io["l3f_w"][e:e + 1]
                sel = io["l3f_sel"][bass.ds(e, 1)] if not is_static(e) else io["l3f_sel"][e:e + 1]
                sp.dma_start(BIGW[:, r, :], src.rearrange("a p c -> (a p) c")).then_inc(sem("l3f_w%d" % r), 16)
                sp.dma_start(ESEL3[0:3 * E3, r, :], sel.rearrange("a p c -> (a p) c")).then_inc(sem("l3f_w%d" % r), 16)
            sp.wait_ge(sem("l3x_att"), since("l3x_att", B))
            load(0, 0)
            load(1, 1)
            sp.wait_ge(sem("l3f_used"), since("l3f_used", 1))
            load(2, 2)
            with sp.Fori(1, E3 // 3) as i:
                for r in range(3):
                    sp.wait_ge(sem("l3f_used"), since("l3f_used", 3 * i + r - 1))
                    load(3 * i + r, r)
        parts = [(l0x_tensor, l0x_scalar, l0x_vector, l0x_gpsimd, None), (l0a_tensor, l0a_scalar, l0a_vector, l0a_gpsimd, None),
                 (l0f_tensor, l0f_scalar, l0f_vector, l0f_gpsimd, l0f_sync),
                 (l1x_tensor, l1x_scalar, l1x_vector, nothing, l1x_sync),
                 (l1a_tensor, l1a_scalar, l1a_vector, nothing, None),
                 (l1f_tensor, l1f_scalar, l1f_vector, nothing, None),
                 (l2x_tensor, l2x_scalar, l2x_vector, nothing, l2x_sync),
                 (l2a_tensor, l2a_scalar, l2a_vector, l2a_gpsimd, None),
                 (l2f_tensor, l2f_scalar, l2f_vector, nothing, l2f_sync),
                 (l3x_tensor, l3x_scalar, l3x_vector, nothing, l3x_sync),
                 (l3a_tensor, l3a_scalar, l3a_vector, l3a_gpsimd, None),
                 (l3f_tensor, l3f_scalar, l3f_vector, nothing, l3f_sync)]
        parts = parts[:layers]
        block = ctx.enter_context(nc.Block())

        @block.sync
        def _(sp):
            first = 4
            sp.dma_start(X[:], io["x"]).then_inc(sem("ld_x"), 16)
            sp.dma_start(CST[:], io["constants"]).then_inc(sem("ld_cst"), 16)
            sp.dma_start(CT32[:], io["ctx32"]).then_inc(sem("ld_ctx32"), 16)
            sp.dma_start(VEC[:], io["vectors"]).then_inc(sem("ld_cst"), 16)
            sp.dma_start(WTS[:, 0:first, :], io["weights"][:, 0:first, :]).then_inc(sem("ld_w0"), 16)
            sp.dma_start(WTS[:, first:, :], io["weights"][:, first:, :]).then_inc(sem("ld_w1"), 16)
            sp.dma_start(RW0[:], io["rw0"]).then_inc(sem("ld_small"), 16)
            sp.dma_start(ROW[:], io["rows"]).then_inc(sem("ld_small"), 16)
            sp.dma_start(WG2[:], io["wg2"]).then_inc(sem("ld_small"), 16)
            sp.dma_start(WG3[:], io["wg3"]).then_inc(sem("ld_small"), 16)
            sp.dma_start(B2[:], io["b2"]).then_inc(sem("ld_small"), 16)
            sp.dma_start(CONVW[:], io["convw"]).then_inc(sem("ld_small"), 16)
            sp.dma_start(ROUT[:], io["rout"]).then_inc(sem("ld_small"), 16)
            sp.dma_start(LROW[:].rearrange("p a d -> p (a d)"), io["lrow"]).then_inc(sem("ld_small"), 16)
            sp.dma_start(WNQ[:], io["wnq"]).then_inc(sem("ld_small"), 16)
            sp.dma_start(WNK[:], io["wnk"]).then_inc(sem("ld_small"), 16)
            for g in range(4):
                sp.dma_start(MASKI[32 * g:32 * g + 32, :], io["mask"]).then_inc(sem("ld_small"), 16)
            for part in parts:
                if part[4]:
                    part[4](sp)
            sp.wait_ge(sem("x_ready"), since("x_ready", 2 * layers + 2))
            sp.dma_start(io["out"], X[:]).then_inc(sem("stored"), 16)
            sp.wait_ge(sem("stored"), since("stored", 16))

        @block.tensor
        def _(pe):
            for part in parts:
                part[0](pe)

        @block.scalar
        def _(act):
            for part in parts:
                part[1](act)

        @block.vector
        def _(dve):
            dve.memset(EPS[:, 0:1], LN_EPS)
            dve.memset(EPS[:, 1:2], 1e-6)
            dve.wait_ge(sem("ld_x"), since("ld_x", 16))
            dve.wait_ge(sem("ld_cst"), since("ld_cst", 32))
            dve.wait_ge(sem("ld_w0"), since("ld_w0", 16))
            dve.wait_ge(sem("ld_w1"), since("ld_w1", 16))
            dve.wait_ge(sem("ld_small"), since("ld_small", 16 * SMALL_LOADS))
            dve.drain().then_inc(sem("x_ready"), 2)
            dve.drain().then_inc(sem("ld_first"), 16)
            for part in parts:
                part[2](dve)

        @block.gpsimd
        def _(pool):
            for part in parts:
                part[3](pool)


LAYERS = 12


def kernel(**inputs):
    import concourse.bacc as _bacc
    from concourse.bass_utils import run_bass_kernel_spmd as _run

    f = {k: np.asarray(x) for k, x in inputs.items()}
    arrays = {}
    arrays["x"] = f["x"].reshape(T, P).T
    ctx = f["ctx_1024"]
    arrays["ctx32"] = ctx[:, :Q].transpose(2, 0, 1)
    square = [f[n].T if flip else f[n] for n, flip in WEIGHTS]
    qkv = f["L1_attn_w_qkv"]
    square += [qkv[i * P:(i + 1) * P].T for i in range(3)]
    square += [f["L1_ffn_leaf_values"][i * P:(i + 1) * P] for i in range(2)]
    arrays["weights"] = np.stack(square, axis=1)
    cols = []
    for n in VECTORS:
        x = f[n].reshape(-1)
        if n == "L1_xattn_temperature":
            x = np.repeat(x, HD)
        cols.append(np.tile(x, P // x.size))
    arrays["vectors"] = np.stack(cols, axis=1)
    arrays["constants"] = np.concatenate(list(constant_blocks().values()), axis=1)
    arrays["ctx"] = ctx.transpose(2, 0, 1)
    arrays["mask"] = f["mask_1x1xSxS2_ik1"].reshape(Q, KEYS)
    arrays["wnq"] = np.tile(f["L1_xattn_wnq"], (P // HD, P // HD))
    arrays["wnk"] = np.tile(f["L1_xattn_wnk"], (P // HD, P // HD))
    arrays["ctx_tok"] = ctx[:, :2 * P].reshape(B, 2, P, P).transpose(2, 0, 1, 3)
    arrays["ctx_last"] = ctx[:, KEYS - 1].reshape(1, B * P)
    arrays["ctx_last_t"] = ctx[:, KEYS - 1].T
    arrays["convw"] = f["L1_attn_w_dwc"]
    arrays["rout"] = f["L1_ffn_routers"].T
    lam = np.concatenate([f["L2_attn_lambda_" + k] for k in ("q1", "k1", "q2", "k2")])
    arrays["lrow"] = np.broadcast_to(lam[None], (P, 4 * HD))
    arrays["wg2"] = f["L2_ffn_Wg"]
    arrays["wg3"] = f["L3_ffn_gate_w"]
    arrays["b2"] = np.concatenate([f["L3_ffn_bs2"][None], f["L3_ffn_b2"]])
    w2 = f["L2_ffn_w2"].reshape(16, 4, P, P).transpose(0, 2, 1, 3).reshape(16, P, 512)
    arrays["l2f_w"] = np.concatenate([f["L2_ffn_w1"], w2], axis=2)
    w1 = np.concatenate([f["L3_ffn_ws1"][None], f["L3_ffn_w1"]])
    w2 = np.concatenate([f["L3_ffn_ws2"][None], f["L3_ffn_w2"]]).reshape(9, 4, P, P).transpose(0, 2, 1, 3).reshape(9, P, 512)
    b1 = np.concatenate([f["L3_ffn_bs1"][None], f["L3_ffn_b1"]]).reshape(9, 4, P).transpose(0, 2, 1)
    arrays["l3f_w"] = np.concatenate([w1, w2, b1], axis=2)
    arrays["l3f_sel"] = part_selectors(9)
    arrays["rw0"] = f["L0_ffn_router_w"].T
    arrays["rows"] = np.broadcast_to(np.concatenate([f["L0_ffn_bias"], f["L3_ffn_gate_b"], f["L3_ffn_gate_b"]])[None], (P, 32))
    gates = [f["L0_ffn_sh_gate_w"][:, :P], f["L0_ffn_sh_gate_w"][:, P:], *f["L0_ffn_gate_w"]]
    ups = [f["L0_ffn_sh_up_w"][:, :P], f["L0_ffn_sh_up_w"][:, P:], *f["L0_ffn_up_w"]]
    downs = [f["L0_ffn_sh_down_w"][:P], f["L0_ffn_sh_down_w"][P:], *f["L0_ffn_down_w"]]
    arrays["l0f_w"] = np.stack([np.concatenate(x, axis=1) for x in zip(gates, ups, downs)])
    arrays["l0f_sel"] = part_selectors(18)

    nc = _bacc.Bacc("TRN2", target_bir_lowering=False, num_devices=1)
    feeds, io = {}, {}
    for name, x in arrays.items():
        x = np.ascontiguousarray(x)
        feeds["in_" + name] = x
        io[name] = nc.dram_tensor("in_" + name, x.shape, mybir.dt.from_np(x.dtype), kind="ExternalInput").ap()
    io["out"] = nc.dram_tensor("out_x", (P, T), F32, kind="ExternalOutput").ap()
    build(nc, io, LAYERS)
    r = _run(nc, [feeds], core_ids=[0])
    return np.ascontiguousarray(r.results[0]["out_x"].T).reshape(B, Q, P)
```

```python
from contextlib import ExitStack

import numpy as np

import concourse.bass as bass
from concourse import mybir

F32 = mybir.dt.float32
BF16 = mybir.dt.bfloat16
I32 = mybir.dt.int32
ALU = mybir.AluOpType
ACT = mybir.ActivationFunctionType
AX = mybir.AxisListType

P = 128
B, Q = 32, 32
T = B * Q
KEYS = 257
NT = T // P
HB = 512
HALVES = (0, 1)
HD = 8
LN_EPS = 1e-5
SHAPE_SCALE = float(1.0 / np.sqrt(np.float32(HD)))
LAMBDA_INIT = 0.8 - 0.6 * float(np.exp(-0.3))
BIG = 3.0e38
MASKED_OUT = -float(2.0 ** 127)
GROUPS = {"mean": P, "head_mean": HD, "pair_mean": 2 * HD}
CAPACITY = T // 16
FAR_SLOT = 4096.0

WEIGHTS = [
    ("L0_xattn_Wk", True), ("L0_xattn_Wv", True), ("L0_xattn_Wq", True), ("L0_xattn_Wo", True),
    ("L0_attn_q1_w", False), ("L0_attn_k1_w", False), ("L0_attn_k2_w", False), ("L0_attn_cp_w", False),
    ("L1_xattn_wq", True), ("L1_xattn_wk", True), ("L1_xattn_wv", False), ("L1_xattn_wo", False),
    ("L1_attn_w_proj", True), ("L1_ffn_Wq", True), ("L1_ffn_Wout_w", True),
    ("L2_attn_Wq", True), ("L2_attn_Wk", True), ("L2_attn_Wv", True), ("L2_attn_Wo", True),
    ("L3_xattn_Wq", False), ("L3_xattn_Wk", False), ("L3_xattn_Wv", False), ("L3_xattn_Wo", False),
    ("L3_attn_Wq", False), ("L3_attn_Wk", False), ("L3_attn_Wv", False), ("L3_attn_Wo", False),
]
MORE_WEIGHTS = ["L1a_q", "L1a_k", "L1a_v", "leaves0", "leaves1"]
WIDX = {n: i for i, n in enumerate([w for w, _ in WEIGHTS] + MORE_WEIGHTS)}
VECTORS = [
    "L0_xattn_bo", "L0_attn_q1_b", "L0_attn_k1_b", "L0_attn_k2_b", "L0_attn_cp_b",
    "L0_attn_gw_w", "L0_attn_gw_b", "L0_attn_sw_w", "L0_attn_sw_b",
    "L1_xattn_bq", "L1_xattn_bk", "L1_xattn_bv", "L1_xattn_bo", "L1_xattn_bnq", "L1_xattn_bnk",
    "L1_xattn_temperature", "L1_xattn_gamma", "L1_attn_b_proj", "L1_attn_b_dwc",
    "L1_ffn_Wout_b", "L3_xattn_b_q", "L3_xattn_b_k", "L3_xattn_b_v", "L3_xattn_b_o",
    "L3_attn_bo", "L3_attn_kln_w", "L3_attn_kln_b", "L3_attn_qln_w", "L3_attn_qln_b", "L3_ffn_bs2",
]
VIDX = {n: i for i, n in enumerate(VECTORS)}


def rope_tables():
    inv_freq = (1.0 / np.float32(10000.0) ** (np.arange(0, HD, 2, dtype=np.float32) / HD)).astype(np.float32)
    pos = np.arange(Q, dtype=np.float32)
    freqs = np.repeat(pos[:, None] * inv_freq[None, :], 2, axis=-1).astype(np.float32)
    sv = ((np.arange(0, HD, 2, dtype=np.float32) + np.float32(0.4 * HD)) / np.float32(1.4 * HD)).astype(np.float32)
    power = ((pos - Q // 2) / np.float32(512.0)).astype(np.float32)
    scale = (sv[None, :] ** power[:, None]).astype(np.float32)
    scale = np.concatenate([scale, scale], axis=-1)
    c, s = np.cos(freqs), np.sin(freqs)
    inv = np.float32(1.0) / scale
    return [x.T.astype(np.float32) for x in (c * scale, s * scale, c * inv, s * inv)]


def constant_blocks():
    p = np.arange(P)[:, None]
    c = np.arange(P)[None, :]
    head, col = p // HD, c // HD
    rot = np.zeros((P, P), np.float32)
    for i in range(0, P, 2):
        rot[i + 1, i] = -1.0
        rot[i, i + 1] = 1.0
    rope = [np.tile(x, (P // HD, 1)) for x in rope_tables()]
    q32 = np.arange(Q)[None, :]
    blocks = {
        "ident": p == c,
        "mean": np.full((P, P), 1.0 / P),
        "in_four": (p % 32) // HD == c // 32,
        "causal_cap": np.where(q32 <= p % 32, BIG, -BIG),
        "causal_keep": (p % 32) <= q32,
        "ones": np.ones((P, P)),
        "same_head": head == col,
        "head_mean": (head == col) / HD,
        "pair_mean": (p // 16 == c // 16) / 16.0,
        "in_two": (p % 32) // 16 == np.arange(64)[None, :] // 32,
        "rot": rot,
        "rope": np.concatenate(rope, axis=1),
        "seg_keep": np.broadcast_to(np.arange(P)[None, :] % Q != 0, (P, P)),
        "row_of": np.arange(P)[:, None] == 4 * (np.arange(2 * P)[None, :] // P) + np.arange(2 * P)[None, :] % P // 32,
        "batch_of": p // 32 == np.arange(4)[None, :],
        "g_row": p == c // 32,
        "own_head": p // 32 == (c % 32) // HD,
        "q_of": p % 32 == q32,
        "key_back": np.broadcast_to(np.arange(KEYS)[None, :] - 512.0, (P, KEYS)),
        "slot_iota": np.broadcast_to(np.arange(T)[None, :], (P, T)),
        "slot_of": p + P * np.arange(NT)[None, :],
        "until": p <= c,
        "before16": np.broadcast_to((np.arange(16)[None, :] < np.arange(16)[:, None]).reshape(1, 256), (P, 256)),
        "rest16": np.broadcast_to(15.0 - np.arange(16)[None, :], (P, 16)),
        "expert_back": np.broadcast_to(np.arange(16)[None, :] - 64.0, (P, 16)),
    }
    return {k: np.ascontiguousarray(v, dtype=np.float32) for k, v in blocks.items()}


def part_selectors(n):
    r = np.arange(3 * n)[None, :, None] % n == np.arange(n)[:, None, None]
    return np.ascontiguousarray(np.broadcast_to(r, (n, 3 * n, P))).astype(mybir.dt.np(BF16))


CONST_COLS = {}
_at = 0
for _name, _block in constant_blocks().items():
    CONST_COLS[_name] = (_at, _block.shape[1])
    _at += _block.shape[1]
CONST_WIDTH = _at
EARLY = CONST_COLS["ones"][0]


FAMILIES = {
    "q_projected": [(n, 2) for n in ("l0x_q", "l0a_q", "l1x_qa", "l1a_q", "l1f_q", "l2a_q", "l3x_q", "l3a_q")],
    "k_projected": [(n, 2) for n in ("l0x_k", "l0a_k", "l2a_k", "l3a_k")],
    "v_projected": [(n, 2) for n in ("l0x_v", "l0a_v", "l2a_v", "l3a_v")],
    "v_copied": [(n, 2) for n in ("l0x_vc", "l0a_vc", "l1a_vc", "l2a_vc", "l3a_vc")],
    "q_copied": [(n, 2) for n in ("l0x_qc", "l1f_qc", "l2a_qc", "l3a_qc")],
    "k_copied": [(n, 2) for n in ("l0x_kc", "l2a_kc", "l3a_kc")],
    "out_projected": [(n, 2) for n in ("l0x_out", "l0a_out", "l0f_out", "l1x_out", "l1a_out", "l1f_out", "l2a_out",
                                       "l3x_out", "l3a_out", "l3f_out")],
    "block_masked": [(n + "_masked", 8) for n in ("l0x", "l0a", "l0b", "l2a", "l3a")],
    "block_scores": [(n + "_scores", 4) for n in ("l0x", "l0a", "l0b", "l2a", "l3a")],
    "block_pt": [(n + "_pt", 4) for n in ("l0x", "l0a", "l0b", "l2a", "l3a")],
    "block_o": [(n + "_o", 4) for n in ("l0x", "l0a", "l0b", "l2a", "l3a")],
    "block_o_read": [(n + "_o_read", 4) for n in ("l0x", "l0a", "l0b", "l2a", "l3a")],
    "block_y": [(n + "_y", 4) for n in ("l0x", "l0a", "l0b", "l2a", "l3a")],
    "block_s_read": [(n + "_s_read", 4) for n in ("l0x", "l2a", "l3a")],
    "block_sm": [(n + "_sm", 4) for n in ("l0x", "l3a")],
    "block_exp": [(n + "_exp", 4) for n in ("l0x", "l2a", "l3a")],
    "combine_parts": [("l0f_parts", 1), ("l3f_parts", 1)],
    "combine_turned": [("l0f_turned", 2), ("l3f_turned", 2)],
    "combine_copied": [("l0f_combt", 2), ("l3f_combt", 2)],
    "router_logits": [("l0f_logits", 1), ("l2f_logits", 1), ("l3f_logits", 1)],
    "operands_prepared": [("l0a_gb", 1), ("l2x_sq", 1), ("l2a_ls", 1)],
    "queries_ready": [("l0a_qp", 2), ("l1a_qf", 2), ("l2a_qrope", 2), ("l3a_qn", 1)],
    "keys_ready": [("l0a_kp", 2), ("l1a_kf", 2), ("l2a_krope", 2), ("l3a_kn", 2)],
    "attended": [("l0a_yy", 2), ("l1a_y", 2), ("l2a_yn", 2)],
    "logits_shifted": [("l2f_lg", 1), ("l3f_lg", 1)],
    "units_weighted": [("l0f_mix", 2 + 36), ("l3f_mix", 4 + 72)],
    "to_be_summed": [("l1x_o2", 2), ("l1a_qk", 2)],
    "squared": [("l1x_sq", 2), ("l2a_sq", 2)],
    "rms_ready": [("l1x_sd", 2), ("l2a_sd", 2)],
    "rms_inverted": [("l1x_inv", 2), ("l2a_inv", 2)],
    "rms_spread": [("l1x_spread", 2), ("l2a_spread", 2)],
    "exp_ready": [("l2a_le", 1), ("l2f_e", 1), ("l3f_e", 1)],
    "activated": [("l0a_gs", 2), ("l0f_scores", 1), ("l1x_qt", 2), ("l1f_gs", 4)],
    "bank_copied": [("l0a_ec", 2), ("l1f_rc", 2), ("l2f_dc", 2), ("l3f_cc", 2)],
    "units_activated": [("l0f_silu", 2 + 36), ("l3f_gelu", 4 + 72)],
    "second_product": [("l0a_g", 2), ("l1a_qs", 2), ("l2a_qr", 2)],
    "third_product": [("l0a_r", 2), ("l2a_kr", 2)],
    "summed": [("l1x_var", 2), ("l1a_den", 2), ("l2a_var", 2)],
    "turned": [("l0a_e", 2), ("l1f_t", 4), ("l2f_xt", 1), ("l3f_ct", 2)],
    "expert_units": [("l0f_gate", 36), ("l2f_h", 16), ("l3f_h", 72)],
    "expert_w0": [("l0f_w0", 288), ("l2f_w0", 128), ("l3f_w0", 96)],
    "expert_w1": [("l0f_w1", 288), ("l2f_w1", 128), ("l3f_w1", 96)],
    "ctx_c0": [("l1x_c0", 128), ("l2x_c0", 64), ("l3x_c0", 128)],
    "ctx_c1": [("l1x_c1", 128), ("l2x_c1", 64), ("l3x_c1", 128)],
    "ctx_c2": [("l1x_c2", 128), ("l2x_c2", 64), ("l3x_c2", 128)],
    "ctx_c3": [("l1x_c3", 128), ("l2x_c3", 64), ("l3x_c3", 128)],
    **{"ctx_" + s: [("l1x_" + s, n), ("l3x_" + s, n)] for s, n in (
        ("k", B), ("kv", B), ("vl", 1), ("vlc", 1), ("vlast", 64), ("vlr", 16), ("vzero", 1), ("vall", B + 2), ("kall", B + 2), ("vb0", 16 * B), ("vb1", 16 * B), ("s", 4 * B), ("mx", 4 * B), ("p", 4 * B), ("t", B), ("t0", B),
        ("o", B), ("om", B), ("att", B), ("qb", B), ("q0", 2))},
}
FAMILY = {}
for _family, _members in FAMILIES.items():
    _n = 0
    for _name, _count in _members:
        FAMILY[_name] = (_family, _n)
        _n += _count


def build(nc, io):
    ctx = ExitStack()
    with ctx:
        def sb(name, shape, dt=F32):
            return ctx.enter_context(nc.sbuf_tensor(name, shape, dt))

        sems = {}

        def sem(name):
            name = FAMILY.get(name, (name, 0))[0]
            if name not in sems:
                sems[name] = ctx.enter_context(nc.semaphore(name))
            return sems[name]

        def since(name, n):
            return n + FAMILY.get(name, (name, 0))[1]

        ps = ctx.enter_context(nc.psum_tensor("ps", [P, 8, HB], F32))
        CST = sb("CST", [P, CONST_WIDTH])
        WTS = sb("WTS", [P, len(WIDX), P])
        VEC = sb("VEC", [P, len(VECTORS)])
        X = sb("X", [P, T])
        XN = sb("XN", [P, T])
        SCRATCH = sb("SCRATCH", [P, 6, T])
        A0, A1, A2, A3, A4, A5 = (SCRATCH[:, i, :] for i in range(6))
        TOK = sb("TOK", [P, NT, P])
        CT32 = sb("CT32", [P, B, Q])
        SHARED = sb("SHARED", [P, 12416])

        def part_of_shared(at, pattern, **sizes):
            n = int(np.prod(list(sizes.values())))
            return SHARED[:, at:at + n].rearrange(pattern, **sizes)

        MASKED = part_of_shared(0, "p (b c) -> p b c", b=B, c=P)
        SM = part_of_shared(4096, "p (r h k) -> p r h k", r=2, h=32, k=Q)
        PR = part_of_shared(6144, "p (r h k) -> p r h k", r=2, h=32, k=Q)
        PT = part_of_shared(8192, "p (r c) -> p r c", r=2, c=2 * HB)
        OM = part_of_shared(10240, "p (r c) -> p r c", r=2, c=2 * HB)
        KALL = part_of_shared(0, "p (b k) -> p b k", b=B, k=KEYS)
        VLAST = part_of_shared(B * KEYS, "p (b c) -> p b c", b=B, c=P)
        DIFF = sb("DIFF", [P, 2, 16, Q])
        ST = sb("ST", [P, 4, 64])

        def cst(name):
            a, n = CONST_COLS[name]
            return CST[:, a:a + n]

        def w(name):
            return WTS[:, WIDX[name], :]

        def vec(name):
            return VEC[:, VIDX[name]:VIDX[name] + 1]

        def half(x, h):
            return x[:, h * HB:(h + 1) * HB]

        def tile4(x, t):
            return x[:, t * P:(t + 1) * P].rearrange("p (b q) -> p b q", b=4)

        def over(x, axis, n):
            y = x.unsqueeze(axis)
            shape = list(y.shape)
            shape[axis] = n
            return y.broadcast_to(shape)

        EPS = sb("EPS", [P, 4])
        ROOT = sb("ROOT", [P, 2, 64])
        WNQ = sb("WNQ", [P, P])
        WNK = sb("WNK", [P, P])
        BN = sb("BN", [P, 2])
        LASTT = sb("LASTT", [P, B])
        MBIAS = sb("MBIAS", [P, KEYS], BF16)
        SELQ = sb("SELQ", [P, P], BF16)
        MASKI = sb("MASKI", [P, KEYS], I32)
        INVT = sb("INVT", [P, 1])
        HEADS = sb("HEADS", [P, 2, P])
        PX = sb("PX", [P, 2, 4, KEYS])
        CONVW = sb("CONVW", [P, 3])
        ROUT = sb("ROUT", [P, 255])
        WG2 = sb("WG2", [P, 16])
        WG3 = sb("WG3", [P, 8])
        RW0 = sb("RW0", [P, 16])
        ROW = sb("ROW", [P, 32])
        SMALL_LOADS = 16


        def inverse_tensor(pe, name, n, sq, mat, banks, between=None):
            size = GROUPS[mat]
            k = P // size
            column = cst(mat).rearrange("p (k g) -> p k g", g=size)[:, :, 0]
            if between:
                between(0)
            for h in HALVES:
                pe.wait_ge(sem(name + "_sq"), since(name + "_sq", 2 * n + h + 1))
                for t in range(4):
                    m = pe.matmul(ps[:, banks[0] + h, t * k:(t + 1) * k], half(sq, h)[:, t * P:(t + 1) * P], column,
                                  start=True, stop=True)
                m.then_inc(sem(name + "_var"), 1)
            if between:
                between(1)
            for h in HALVES:
                pe.wait_ge(sem(name + "_inv"), since(name + "_inv", 2 * n + h + 1))
                for t in range(4):
                    root = ROOT[:, h, t:t + 1].broadcast_to([P, P]) if k == 1 else half(sq, h)[:, t * P:(t + 1) * P]
                    m = pe.transpose(ps[:, banks[1] + h, t * P:(t + 1) * P], root, cst("ident"))
                m.then_inc(sem(name + "_spread"), 1)

        def inverse_scalar(act, name, n, mat, bank, eps):
            for h in HALVES:
                act.wait_ge(sem(name + "_var"), since(name + "_var", 2 * n + h + 1))
                w4 = 4 * P // GROUPS[mat]
                act.activation(ROOT[:, h, 0:w4], ps[:, bank + h, 0:w4], ACT.Sqrt, bias=eps).then_inc(sem(name + "_sd"), 1)

        def inverse_vector(dve, name, n, sq, mat):
            for h in HALVES:
                dve.wait_ge(sem(name + "_sd"), since(name + "_sd", 2 * n + h + 1))
                w4 = 4 * P // GROUPS[mat]
                m = dve.reciprocal(ROOT[:, h, 0:w4], ROOT[:, h, 0:w4])
                if w4 > 4:
                    dve.drain()
                    m = dve.tensor_copy(half(sq, h).rearrange("p (k g) -> p k g", k=w4), over(ROOT[:, h, 0:w4], 2, GROUPS[mat]))
                m.then_inc(sem(name + "_inv"), 1)

        def norm_tensor(pe, name, n, src, sq, mat, src_ready, src_count, bank=0, between=None):
            for h in HALVES:
                pe.wait_ge(sem(src_ready), since(src_ready, src_count + h + 1))
                pe.matmul(ps[:, bank + h, :], cst(mat), half(src, h), start=True, stop=True).then_inc(sem(name + "_mean"), 1)
            inverse_tensor(pe, name, n, sq, mat, (bank + 2, bank), between)

        def load_root_table(act):
            act.activation(EPS[:, 2:3], EPS[:, 0:1], ACT.Sqrt)

        def norm_scalar(act, name, n, xc, sq, mat, eps, bank=0, between=None):
            if not between and (name, n) != ("ln", 0):
                load_root_table(act)
            for h in HALVES:
                act.wait_ge(sem(name + "_xc"), since(name + "_xc", 2 * n + h + 1))
                act.activation(half(sq, h), half(xc, h), ACT.Square).then_inc(sem(name + "_sq"), 1)
            if between:
                between(0)
            inverse_scalar(act, name, n, mat, bank + 2, eps)
            if between:
                between(1)

        def norm_vector(dve, name, n, src, xc, sq, mat, out, out_ready, bank=0, between=None):
            for h in HALVES:
                dve.wait_ge(sem(name + "_mean"), since(name + "_mean", 2 * n + h + 1))
                dve.tensor_tensor(half(xc, h), half(src, h), ps[:, bank + h, :], ALU.subtract).then_inc(sem(name + "_xc"), 1)
            if between:
                between(0)
            inverse_vector(dve, name, n, sq, mat)
            if between:
                between(1)
            for h in HALVES:
                dve.wait_ge(sem(name + "_spread"), since(name + "_spread", 2 * n + h + 1))
                dve.tensor_tensor(half(out, h), half(xc, h), ps[:, bank + h, :], ALU.mult).then_inc(sem(out_ready), 1)

        def ln_tensor(pe, n, between=None):
            norm_tensor(pe, "ln", n, X, A1, "mean", "x_ready", 2 * n, between=between)

        def ln_scalar(act, n, between=None):
            norm_scalar(act, "ln", n, A0, A1, "mean", EPS[:, 0:1], between=between)

        def ln_vector(dve, n, between=None):
            norm_vector(dve, "ln", n, X, A0, A1, "mean", XN, "xn_ready", between=between)

        def project(pe, weight, src, banks, done, waits=()):
            for h in HALVES:
                for name, count in waits:
                    pe.wait_ge(sem(name), since(name, count + h))
                pe.matmul(ps[:, banks[h], :], weight, half(src, h), start=True, stop=True).then_inc(sem(done), 1)

        def add_to_residual(dve, name, banks, bias):
            for h in HALVES:
                dve.wait_ge(sem(name), since(name, h + 1))
                dve.scalar_tensor_tensor(out=half(X, h), in0=ps[:, banks[h], :], scalar=bias, in1=half(X, h),
                                         op0=ALU.add, op1=ALU.add).then_inc(sem("x_ready"), 1)

        def spread(pool, name, src, ready, base=0):
            for t in range(NT):
                if t % 4 == 0:
                    pool.wait_ge(sem(ready), since(ready, base + t // 4 + 1))
                pool.tensor_tensor(MASKED[:, 4 * t:4 * t + 4, :].rearrange("p b (h q) -> p b h q", h=4),
                                   over(tile4(src, t), 2, 4),
                                   over(cst("in_four").rearrange("p (h q) -> p h q", h=4), 1, 4),
                                   ALU.mult).then_inc(sem(name + "_masked"), 1)

        PAIRS = NT // 2

        def block_scores(pe, name, fixed, u, read):
            pe.wait_ge(sem(name + "_masked"), since(name + "_masked", 2 * u + 2))
            if u >= 1:
                pe.wait_ge(sem(name + read), since(name + read, u))
            for s in range(2):
                for b in range(4):
                    n = 4 * (2 * u + s) + b
                    for g in range(4):
                        m = pe.matmul(ps[32 * b:32 * b + 32, g, s * P:(s + 1) * P],
                                      fixed[32 * g:32 * g + 32, n * Q:(n + 1) * Q],
                                      MASKED[32 * g:32 * g + 32, n, :], start=True, stop=True)
            m.then_inc(sem(name + "_scores"), 1)

        def block_values(pe, name, values, u, width):
            pe.wait_ge(sem(name + "_pt"), since(name + "_pt", u + 1))
            if u >= 1:
                pe.wait_ge(sem(name + "_o_read"), since(name + "_o_read", u))
            for s in range(2):
                for b in range(4):
                    for g in range(4):
                        c = (2 * g + s) * width
                        m = pe.matmul(ps[32 * g:32 * g + 32, 4 + b, s * width:(s + 1) * width],
                                      values[32 * b:32 * b + 32, 2 * u + s, 32 * g:32 * g + 32],
                                      PT[32 * b:32 * b + 32, u % 2, c:c + width], start=True, stop=True)
            m.then_inc(sem(name + "_o"), 1)

        def block_tensor(pe, name, fixed, values, read, width=P):
            for u in range(PAIRS + 2):
                if u < PAIRS:
                    block_scores(pe, name, fixed, u, read)
                if u >= 2:
                    block_values(pe, name, values, u - 2, width)

        def block_take(dve, name, out, u, width=P):
            n = width // Q
            dve.wait_ge(sem(name + "_o"), since(name + "_o", u + 1))
            own = cst("in_four" if n == 4 else "in_two")
            om = OM[:, u % 2, 0:8 * width]
            dve.tensor_tensor(om.rearrange("p (b t c) -> p b t c", b=4, t=2),
                              ps[:, 4:8, 0:2 * width].rearrange("p b (t c) -> p b t c", t=2),
                              over(over(own, 1, 2), 1, 4), ALU.mult).then_inc(sem(name + "_o_read"), 1)
            dve.drain()
            for s in range(2):
                m = dve.tensor_reduce(tile4(out, 2 * u + s),
                                      om.rearrange("p (b t h q) -> p t b q h", b=4, t=2, h=n)[:, s], AX.X, ALU.add)
            m.then_inc(sem(name + "_y"), 1)

        def pair_scores():
            return ps[:, 0:4, 0:2 * P]

        def block_softmax_vector(dve, name, out, causal):
            for u in range(PAIRS + 2):
                if u < PAIRS:
                    dve.wait_ge(sem(name + "_scores"), since(name + "_scores", u + 1))
                    if u >= 2:
                        dve.wait_ge(sem(name + "_exp"), since(name + "_exp", u - 1))
                    sm = SM[:, u % 2]
                    s3 = pair_scores().rearrange("p g (c k) -> p g c k", k=Q)
                    sm3 = sm.rearrange("p (g c) k -> p g c k", g=4)
                    mx = ST[:, 0, 0:32]
                    if causal:
                        dve.tensor_tensor(sm3, s3, over(over(cst("causal_cap"), 1, 8), 1, 4),
                                          ALU.min).then_inc(sem(name + "_s_read"), 1)
                        dve.drain()
                        dve.tensor_reduce(mx, sm, AX.X, ALU.max)
                        dve.drain()
                        dve.tensor_tensor(sm, sm, over(mx, 2, Q), ALU.subtract).then_inc(sem(name + "_sm"), 1)
                    else:
                        mx3 = mx.rearrange("p (g c) -> p g c", g=4)
                        dve.tensor_reduce(mx3, s3, AX.X, ALU.max)
                        dve.drain()
                        dve.tensor_tensor(sm3, s3, over(mx3, 3, Q), ALU.subtract).then_inc(sem(name + "_s_read"), 1)
                if 1 <= u <= PAIRS:
                    n = u - 1
                    dve.wait_ge(sem(name + "_exp"), since(name + "_exp", n + 1))
                    pr = PR[:, n % 2]
                    total, inv = ST[:, 1, 0:32], ST[:, 2, 0:32]
                    dve.tensor_reduce(total, pr, AX.X, ALU.add)
                    dve.drain()
                    dve.reciprocal(inv, total)
                    dve.drain()
                    dve.tensor_tensor(pr, pr, over(inv, 2, Q), ALU.mult)
                    dve.drain()
                    if n >= 2:
                        dve.wait_ge(sem(name + "_o"), since(name + "_o", n - 1))
                    if name == "l2a":
                        two = pr.rearrange("p (h j) k -> p h j k", j=2)
                        diff = DIFF[:, n % 2]
                        dve.scalar_tensor_tensor(out=diff, in0=two[:, :, 1], scalar=NEG_LAMBDA[:], in1=two[:, :, 0],
                                                 op0=ALU.mult, op1=ALU.add)
                        dve.drain()
                        dve.transpose(PT[:, n % 2, 0:512],
                                      diff.rearrange("p h k -> p (h k)")).then_inc(sem(name + "_pt"), 1)
                    else:
                        dve.transpose(PT[:, n % 2], pr.rearrange("p h k -> p (h k)")).then_inc(sem(name + "_pt"), 1)
                if u >= 2:
                    block_take(dve, name, out, u - 2, 64 if name == "l2a" else P)

        def block_softmax_scalar(act, name, causal):
            for u in range(PAIRS):
                act.wait_ge(sem(name + ("_sm" if causal else "_s_read")), since(name + ("_sm" if causal else "_s_read"), u + 1))
                if u >= 2:
                    act.wait_ge(sem(name + "_pt"), since(name + "_pt", u - 1))
                act.activation(PR[:, u % 2], SM[:, u % 2], ACT.Exp).then_inc(sem(name + "_exp"), 1)

        def block_linear_vector(dve, name, out):
            for u in range(PAIRS + 1):
                if u < PAIRS:
                    dve.wait_ge(sem(name + "_scores"), since(name + "_scores", u + 1))
                    if u >= 2:
                        dve.wait_ge(sem(name + "_o"), since(name + "_o", u - 1))
                    dve.tensor_tensor(PT[:, u % 2].rearrange("p (g c k) -> p g c k", g=4, k=Q),
                                      pair_scores().rearrange("p g (c k) -> p g c k", k=Q),
                                      over(over(cst("causal_keep"), 1, 8), 1, 4), ALU.mult).then_inc(sem(name + "_pt"), 1)
                if u >= 1:
                    block_take(dve, name, out, u - 1)

        def l0x_tensor(pe):
            ctx32 = CT32[:].rearrange("p b q -> p (b q)")
            pe.wait_ge(sem("ld_w0"), since("ld_w0", 16))
            pe.wait_ge(sem("ld_ctx32"), since("ld_ctx32", 16))
            project(pe, w("L0_xattn_Wk"), ctx32, (6, 7), "l0x_k")
            for t in range(NT):
                m = pe.matmul(ps[:, 4 + t // 4, (t % 4) * P:(t % 4 + 1) * P], ctx32[:, t * P:(t + 1) * P], w("L0_xattn_Wv"),
                              start=True, stop=True)
                if t % 4 == 3:
                    m.then_inc(sem("l0x_v"), 1)
            ln_tensor(pe, 0)
            project(pe, w("L0_xattn_Wq"), XN, (6, 7), "l0x_q", [("xn_ready", 1), ("l0x_kc", 1)])
            pe.wait_ge(sem("l0x_qc"), since("l0x_qc", 2))
            pe.wait_ge(sem("l0x_vc"), since("l0x_vc", 2))
            pe.wait_ge(sem("ld_w1"), since("ld_w1", 16))
            pe.wait_ge(sem("heads_masked"), since("heads_masked", 1))
            for i, (c, bias) in enumerate((("q", "L1_xattn_bq"), ("k", "L1_xattn_bk"))):
                pe.matmul(ps[:, 4, i * P:(i + 1) * P], w("L1_xattn_w" + c), HEADS[:, i, :], start=True, stop=True)
                m = pe.matmul(ps[:, 4, 2 * P + i:2 * P + i + 1], HEADS[:, i, :], vec(bias), start=True, stop=True)
            m.then_inc(sem("heads_folded"), 1)
            block_tensor(pe, "l0x", A4, TOK, "_s_read")
            for h in HALVES:
                pe.wait_ge(sem("l0x_y"), since("l0x_y", 2 * h + 2))
                pe.matmul(ps[:, h, :], w("L0_xattn_Wo"), half(A5, h), start=True, stop=True).then_inc(sem("l0x_out"), 1)

        def l0x_scalar(act):
            for h in HALVES:
                act.wait_ge(sem("l0x_k"), since("l0x_k", h + 1))
                act.copy(half(A3, h), ps[:, 6 + h, :]).then_inc(sem("l0x_kc"), 1)
            for h in HALVES:
                act.wait_ge(sem("l0x_v"), since("l0x_v", h + 1))
                act.copy(TOK[:, 4 * h:4 * h + 4, :].rearrange("p t c -> p (t c)"), ps[:, 4 + h, :]).then_inc(sem("l0x_vc"), 1)
            ln_scalar(act, 0)
            for h in HALVES:
                act.wait_ge(sem("l0x_q"), since("l0x_q", h + 1))
                act.activation(half(A4, h), ps[:, 6 + h, :], ACT.Copy, scale=SHAPE_SCALE).then_inc(sem("l0x_qc"), 1)
            block_softmax_scalar(act, "l0x", True)

        def l0x_vector(dve):
            ln_vector(dve, 0)
            dve.wait_ge(sem("ld_small"), since("ld_small", 16 * SMALL_LOADS))
            dve.tensor_tensor(HEADS[:, 0, :], WNQ[:], cst("same_head"), ALU.mult)
            dve.tensor_tensor(HEADS[:, 1, :], WNK[:], cst("same_head"), ALU.mult)
            dve.drain().then_inc(sem("heads_masked"), 1)
            dve.reciprocal(INVT[:], vec("L1_xattn_temperature"))
            dve.tensor_scalar(MBIAS[:], MASKI[:], 0.0, MASKED_OUT, ALU.is_equal, ALU.mult)
            dve.tensor_copy(SELQ[:].rearrange("p (h q) -> p h q", h=4), over(cst("ident")[:, 0:Q], 1, 4))
            dve.wait_ge(sem("heads_folded"), since("heads_folded", 1))
            dve.tensor_copy(WNQ[:], ps[:, 4, 0:P])
            dve.tensor_copy(WNK[:], ps[:, 4, P:2 * P])
            dve.tensor_tensor(BN[:, 0:1], ps[:, 4, 2 * P:2 * P + 1], vec("L1_xattn_bnq"), ALU.add)
            dve.tensor_tensor(BN[:, 1:2], ps[:, 4, 2 * P + 1:2 * P + 2], vec("L1_xattn_bnk"), ALU.add)
            block_softmax_vector(dve, "l0x", A5, True)
            add_to_residual(dve, "l0x_out", (0, 1), vec("L0_xattn_bo"))

        def l0x_gpsimd(pool):
            pool.wait_ge(sem("ld_cst"), since("ld_cst", 32))
            spread(pool, "l0x", A3, "l0x_kc")

        SQD = float(np.sqrt(np.float32(HD)))
        K2_SCALE = float(0.02 / np.sqrt(np.float32(P)))
        GB = sb("GB", [P, 2, P])
        K2B = sb("K2B", [P, 1])

        def l0a_tensor(pe):
            ln_tensor(pe, 1)
            project(pe, w("L0_attn_q1_w"), XN, (4, 5), "l0a_q", [("xn_ready", 3)])
            project(pe, w("L0_attn_k1_w"), XN, (6, 7), "l0a_k")
            pe.wait_ge(sem("l0a_gb"), since("l0a_gb", 1))
            project(pe, GB[:, 0, :], XN, (0, 1), "l0a_g")
            project(pe, w("L0_attn_k2_w"), XN, (2, 3), "l0a_k2")
            project(pe, GB[:, 1, :], A1, (4, 5), "l0a_r", [("l0a_kc", 1)])
            for t in range(NT):
                m = pe.transpose(ps[:, 6 + t // 4, (t % 4) * P:(t % 4 + 1) * P], XN[:, t * P:(t + 1) * P], cst("ident"))
                if t % 4 == 3:
                    m.then_inc(sem("l0a_v"), 1)
            pe.wait_ge(sem("l0a_vc"), since("l0a_vc", 2))
            pe.wait_ge(sem("l0a_kp"), since("l0a_kp", 2))
            block_tensor(pe, "l0a", A3, TOK, "_pt")
            pe.wait_ge(sem("l0a_et"), since("l0a_et", 2))
            for t in range(NT):
                m = pe.transpose(ps[:, 4 + t // 4, (t % 4) * P:(t % 4 + 1) * P], A1[:, t * P:(t + 1) * P], cst("ident"))
                if t % 4 == 3:
                    m.then_inc(sem("l0a_e"), 1)
            pe.wait_ge(sem("l0a_ec"), since("l0a_ec", 2))
            block_tensor(pe, "l0b", A5, TOK, "_pt")
            for h in HALVES:
                pe.wait_ge(sem("l0a_yy"), since("l0a_yy", h + 1))
                pe.matmul(ps[:, h, :], w("L0_attn_cp_w"), half(A3, h), start=True, stop=True).then_inc(sem("l0a_out"), 1)

        def l0a_scalar(act):
            ln_scalar(act, 1)
            for h in HALVES:
                act.wait_ge(sem("l0a_g"), since("l0a_g", h + 1))
                act.activation(half(A2, h), ps[:, h, :], ACT.Sigmoid, bias=vec("L0_attn_gw_b")).then_inc(sem("l0a_gs"), 1)
            for h in HALVES:
                act.wait_ge(sem("l0a_k2"), since("l0a_k2", h + 1))
                act.activation(half(A5, h), ps[:, 2 + h, :], ACT.Sigmoid, bias=K2B[:], scale=K2_SCALE).then_inc(sem("l0a_k2s"), 1)
            for h in HALVES:
                act.wait_ge(sem("l0a_gmax"), since("l0a_gmax", h + 1))
                act.activation(half(A2, h), half(A2, h), ACT.Ln).then_inc(sem("l0a_ln"), 1)
            for h in HALVES:
                act.wait_ge(sem("l0a_v"), since("l0a_v", h + 1))
                act.copy(TOK[:, 4 * h:4 * h + 4, :].rearrange("p t c -> p (t c)"), ps[:, 6 + h, :]).then_inc(sem("l0a_vc"), 1)
            for h in HALVES:
                act.wait_ge(sem("l0a_cum"), since("l0a_cum", h + 1))
                act.activation(half(A2, h), half(A4, h), ACT.Exp).then_inc(sem("l0a_gc"), 1)
            for h in HALVES:
                act.wait_ge(sem("l0a_r"), since("l0a_r", h + 1))
                act.activation(half(A3, h), ps[:, 4 + h, :], ACT.Silu, bias=vec("L0_attn_sw_b")).then_inc(sem("l0a_rs"), 1)
            for h in HALVES:
                act.wait_ge(sem("l0a_e"), since("l0a_e", h + 1))
                act.copy(TOK[:, 4 * h:4 * h + 4, :].rearrange("p t c -> p (t c)"), ps[:, 4 + h, :]).then_inc(sem("l0a_ec"), 1)

        def l0a_vector(dve):
            dve.tensor_scalar(GB[:, 0, :], cst("same_head"), vec("L0_attn_gw_w"), None, ALU.mult)
            dve.tensor_scalar(GB[:, 1, :], cst("same_head"), vec("L0_attn_sw_w"), None, ALU.mult)
            dve.tensor_scalar(K2B[:], vec("L0_attn_k2_b"), K2_SCALE, None, ALU.mult).then_inc(sem("l0a_gb"), 1)
            ln_vector(dve, 1)
            for h in HALVES:
                dve.wait_ge(sem("l0a_q"), since("l0a_q", h + 1))
                dve.tensor_scalar(half(A0, h), ps[:, 4 + h, :], vec("L0_attn_q1_b"), None, ALU.add)
                dve.wait_ge(sem("l0a_k"), since("l0a_k", h + 1))
                dve.tensor_scalar(half(A1, h), ps[:, 6 + h, :], vec("L0_attn_k1_b"), None, ALU.add).then_inc(sem("l0a_kc"), 1)
            for h in HALVES:
                dve.wait_ge(sem("l0a_gs"), since("l0a_gs", h + 1))
                dve.tensor_scalar(half(A2, h), half(A2, h), 1e-6, None, ALU.max).then_inc(sem("l0a_gmax"), 1)
            for h in HALVES:
                dve.wait_ge(sem("l0a_ln"), since("l0a_ln", h + 1))
                for t in range(4 * h, 4 * h + 4):
                    dve.tensor_tensor_scan(A4[:, t * P:(t + 1) * P], cst("seg_keep"), A2[:, t * P:(t + 1) * P], 0.0,
                                           ALU.mult, ALU.add)
                dve.drain()
                dve.tensor_scalar(half(A4, h), half(A4, h), -30.0, 30.0, ALU.max, ALU.min).then_inc(sem("l0a_cum"), 1)
            for h in HALVES:
                dve.wait_ge(sem("l0a_gc"), since("l0a_gc", h + 1))
                dve.tensor_scalar(half(A2, h), half(A2, h), 1e-6, None, ALU.add)
                dve.tensor_scalar(half(A4, h), half(A0, h), 1.0 / SQD, None, ALU.mult)
                dve.drain()
                dve.tensor_tensor(half(A0, h), half(A0, h), half(A2, h), ALU.mult).then_inc(sem("l0a_qp"), 1)
                dve.scalar_tensor_tensor(out=half(A4, h), in0=half(A4, h), scalar=0.02, in1=half(A4, h), op0=ALU.mult,
                                         op1=ALU.min)
                dve.drain()
                dve.reciprocal(half(A2, h), half(A2, h))
                dve.wait_ge(sem("l0a_rs"), since("l0a_rs", h + 1))
                dve.tensor_tensor(half(A3, h), half(A3, h), half(A1, h), ALU.mult)
                dve.drain()
                dve.tensor_tensor(half(A3, h), half(A3, h), half(A2, h), ALU.mult).then_inc(sem("l0a_kp"), 1)
            block_linear_vector(dve, "l0a", A2)
            dve.drain()
            for h in HALVES:
                def batches(x):
                    return half(x, h).rearrange("p (b q) -> p b q", q=Q)
                dve.memset(batches(A1)[:, :, Q - 1:Q], 0.0)
                dve.tensor_tensor(batches(A1)[:, :, 0:Q - 1], batches(XN)[:, :, 1:Q], batches(A2)[:, :, 0:Q - 1],
                                  ALU.subtract)
            dve.drain().then_inc(sem("l0a_et"), 2)
            block_linear_vector(dve, "l0b", A0)
            dve.drain()
            for h in HALVES:
                def batches(x):
                    return half(x, h).rearrange("p (b q) -> p b q", q=Q)
                dve.tensor_copy(batches(A3)[:, :, 0:1], batches(A2)[:, :, 0:1])
                dve.tensor_tensor(batches(A3)[:, :, 1:Q], batches(A2)[:, :, 1:Q], batches(A0)[:, :, 0:Q - 1], ALU.add)
                dve.drain().then_inc(sem("l0a_yy"), 1)
            add_to_residual(dve, "l0a_out", (0, 1), vec("L0_attn_cp_b"))

        def l0a_gpsimd(pool):
            spread(pool, "l0a", A0, "l0a_qp")
            pool.wait_ge(sem("l0a_scores"), since("l0a_scores", PAIRS))
            spread(pool, "l0b", A4, "l0a_kp")

        NEG_LAMBDA = sb("NEG_LAMBDA", [P, 1])

        E0 = 18
        TURNS = sb("TURNS", [P, 4 * 4 * (KEYS + 2 * P)])

        def part_of_turns(at, pattern, **sizes):
            n = int(np.prod(list(sizes.values())))
            return TURNS[:, at:at + n].rearrange(pattern, **sizes)

        EW = part_of_turns(3084 + 2 * T, "p (r a n) -> p r a n", r=2, a=3, n=P)
        ESEL = sb("ESEL", [P, 2, P], BF16)
        RT = sb("RT", [P, 12, P])
        PARTS = sb("PARTS", [P, NT, 54], BF16)
        COMBT = sb("COMBT", [P, T], BF16)
        IDB = sb("IDB", [P, P], BF16)
        ZB = sb("ZB", [P, HB], BF16)
        HC = part_of_turns(3084, "p (r t) -> p r t", r=2, t=T)

        def rank(dve, values, out, n, big):
            m = big.rearrange("p (t j i) -> p t j i", t=NT, i=n)
            before = cst("before16").rearrange("p (j i) -> p j i", i=16)[:, 0:n, 0:n]
            dve.tensor_tensor(m, over(values, 2, n), over(values, 3, n), ALU.is_ge)
            dve.drain()
            dve.tensor_tensor(m, m, over(before, 1, NT), ALU.mult)
            dve.drain()
            rows, cols = RT[:, 10, 0:NT * n].rearrange("p (t j) -> p t j", t=NT), RT[:, 11, 0:NT * n].rearrange("p (t j) -> p t j", t=NT)
            dve.tensor_reduce(rows, m, AX.X, ALU.add)
            dve.tensor_reduce(cols, m.rearrange("p t j i -> p t i j"), AX.X, ALU.add)
            dve.drain()
            dve.tensor_tensor(rows, rows, cols, ALU.subtract)
            dve.drain()
            dve.tensor_tensor(out, rows, over(cst("rest16")[:, 16 - n:16], 1, NT), ALU.add)
            dve.drain()

        def split_parts(dve, comb, n, done):
            left = RT[:, 10, 0:NT * n] if n <= 16 else RT[:, 10:12, :].rearrange("p a b -> p (a b)")[:, 0:NT * n]
            left = left.rearrange("p (t e) -> p t e", t=NT)
            dve.tensor_copy(PARTS[:, :, 0:n], comb)
            dve.drain()
            dve.tensor_tensor(left, comb, PARTS[:, :, 0:n], ALU.subtract)
            dve.drain()
            dve.tensor_copy(PARTS[:, :, n:2 * n], left)
            dve.drain()
            dve.tensor_tensor(left, left, PARTS[:, :, n:2 * n], ALU.subtract)
            dve.drain()
            dve.tensor_copy(PARTS[:, :, 2 * n:3 * n], left).then_inc(sem(done), 1)

        def tiles(i, n=16, count=1):
            x = RT[:, i:i + count, :].rearrange("p a b -> p (a b)")
            return x[:, 0:NT * n].rearrange("p (t e) -> p t e", t=NT)

        def route_tensor(pe, weight, n):
            for t in range(NT):
                m = pe.matmul(ps[:, 0, t * n:(t + 1) * n], XN[:, t * P:(t + 1) * P], weight, start=True, stop=True)
            return m

        def turn_parts_tensor(pe, rows, name):
            pe.wait_ge(sem(name + "_parts"), since(name + "_parts", 1))
            for t in range(NT):
                m = pe.matmul(ps[0:rows, t // 4, (t % 4) * P:(t % 4 + 1) * P], PARTS[:, t, 0:rows], IDB[:], start=True, stop=True)
                if t % 4 == 3:
                    m.then_inc(sem(name + "_turned"), 1)

        def turn_parts_scalar(act, rows, name):
            for h in HALVES:
                act.wait_ge(sem(name + "_turned"), since(name + "_turned", h + 1))
                act.copy(half(COMBT, h)[0:rows], ps[0:rows, h, :]).then_inc(sem(name + "_combt"), 1)

        def l0f_tensor(pe):
            ln_tensor(pe, 2)
            pe.wait_ge(sem("xn_ready"), since("xn_ready", 6))
            pe.wait_ge(sem("ld_small"), since("ld_small", 16 * SMALL_LOADS))
            route_tensor(pe, RW0[:], 16).then_inc(sem("l0f_logits"), 1)
            turn_parts_tensor(pe, 54, "l0f")
            pe.wait_ge(sem("l0f_combt"), since("l0f_combt", 2))
            for h in HALVES:
                m = pe.matmul(ps[:, 6 + h, :], ZB[:, 0:P], ZB[:], start=True, stop=False, skip_group_check=True)
            m.then_inc(sem("l0f_down"), 1)

            def step(i, p):
                pe.wait_ge(sem("l0f_w%d" % p), since("l0f_w%d" % p, 32 * i + 32))
                for h in HALVES:
                    pe.wait_ge(sem("l0f_silu"), since("l0f_silu", 4 * i + 2 * p + h + 1))
                    pe.matmul(ps[:, h, :], EW[:, p, 0, :], half(XN, h), start=True, stop=True).then_inc(sem("l0f_gate"), 1)
                for h in HALVES:
                    pe.wait_ge(sem("l0f_mix"), since("l0f_mix", 4 * i + 2 * p + h + 1))
                    m = pe.matmul(ps[:, 6 + h, :], EW[:, 1 - p, 2, :], half(HC[:, 1 - p], h), start=False, stop=False,
                                  skip_group_check=True)
                m.then_inc(sem("l0f_down"), 1)
                for h in HALVES:
                    pe.matmul(ps[:, 2 + h, :], EW[:, p, 1, :], half(XN, h), start=True, stop=True)
                    pe.matmul(ps[:, 4 + h, :], ESEL[0:54, p, :], half(COMBT, h)[0:54], start=True, stop=True).then_inc(sem("l0f_up"), 1)

            with pe.Fori(0, E0 // 2) as i:
                step(i, 0)
                step(i, 1)
            for h in HALVES:
                pe.wait_ge(sem("l0f_mix"), since("l0f_mix", 2 * E0 + h + 1))
                pe.matmul(ps[:, 6 + h, :], EW[:, 1, 2, :], half(HC[:, 1], h), start=False, stop=True,
                          skip_group_check=True).then_inc(sem("l0f_out"), 1)

        def l0f_scalar(act):
            ln_scalar(act, 2)
            act.wait_ge(sem("l0f_logits"), since("l0f_logits", 1))
            act.activation(RT[:, 0, :], ps[:, 0, 0:P], ACT.Sigmoid).then_inc(sem("l0f_scores"), 1)
            turn_parts_scalar(act, 54, "l0f")
            act.drain().then_inc(sem("l0f_silu"), 2)
            with act.Fori(0, E0 // 2) as i:
                for p in range(2):
                    for h in HALVES:
                        act.wait_ge(sem("l0f_gate"), since("l0f_gate", 4 * i + 2 * p + h + 1))
                        act.wait_ge(sem("l0f_mix"), since("l0f_mix", 4 * i + 2 * p + h + 1))
                        act.activation(half(A0, h), ps[:, h, :], ACT.Silu).then_inc(sem("l0f_silu"), 1)

        def l0f_vector(dve):
            ln_vector(dve, 2)
            dve.memset(ZB[:], 0.0)
            dve.memset(HC[:, 1], 0.0)
            dve.memset(EW[:, 1, 2, :], 0.0)
            dve.tensor_copy(IDB[:], cst("ident"))
            dve.wait_ge(sem("l0f_scores"), since("l0f_scores", 1))
            scores, s = tiles(0), tiles(1)
            dve.tensor_tensor(s, scores, over(ROW[:, 0:16], 1, NT), ALU.add)
            dve.drain()
            four = RT[:, 1, :].rearrange("p (g a b) -> p g a b", a=2, b=2)
            hi, lo = (RT[:, k, 0:64].rearrange("p (g a) -> p g a", a=2) for k in (2, 3))
            dve.tensor_tensor(hi, four[:, :, :, 0], four[:, :, :, 1], ALU.max)
            dve.tensor_tensor(lo, four[:, :, :, 0], four[:, :, :, 1], ALU.min)
            dve.drain()
            top, low, second = RT[:, 4, 0:32], RT[:, 5, 0:32], RT[:, 6, 0:32]
            dve.tensor_tensor(top, hi[:, :, 0], hi[:, :, 1], ALU.max)
            dve.tensor_tensor(second, hi[:, :, 0], hi[:, :, 1], ALU.min)
            dve.tensor_tensor(low, lo[:, :, 0], lo[:, :, 1], ALU.max)
            dve.drain()
            dve.tensor_tensor(second, second, low, ALU.max)
            dve.drain()
            dve.tensor_tensor(top, top, second, ALU.add)
            dve.drain()
            big = SCRATCH[:, 0:2, :].rearrange("p a b -> p (a b)")
            grank = tiles(7, 4)
            rank(dve, tiles(4, 4), grank, 4, big[:, 0:P])
            dve.tensor_scalar(grank, grank, 2.0, None, ALU.is_lt)
            dve.drain()
            s4 = RT[:, 1, :].rearrange("p (g e) -> p g e", e=4)
            masked = RT[:, 8, :].rearrange("p (g e) -> p g e", e=4)
            gate4 = over(RT[:, 7, 0:32], 2, 4)
            dve.tensor_tensor(masked, s4, gate4, ALU.mult)
            dve.drain()
            dve.tensor_scalar(RT[:, 7, 0:32], RT[:, 7, 0:32], 1.0, None, ALU.subtract)
            dve.drain()
            dve.tensor_tensor(masked, masked, gate4, ALU.add)
            dve.drain()
            chosen = tiles(9)
            rank(dve, tiles(8), chosen, 16, big)
            dve.tensor_scalar(chosen, chosen, 4.0, None, ALU.is_lt)
            dve.drain()
            dve.tensor_tensor(chosen, chosen, scores, ALU.mult)
            dve.drain()
            total = RT[:, 2, 0:NT]
            dve.tensor_reduce(total, chosen, AX.X, ALU.add)
            dve.drain()
            dve.tensor_scalar(total, total, 1e-20, None, ALU.add)
            dve.drain()
            dve.reciprocal(total, total)
            dve.drain()
            dve.tensor_tensor(chosen, chosen, over(total, 2, 16), ALU.mult)
            comb = tiles(3, E0, 2)
            dve.memset(comb[:, :, 0:2], 1.0)
            dve.drain()
            dve.tensor_scalar(comb[:, :, 2:E0], chosen, 2.5, None, ALU.mult)
            dve.drain()
            split_parts(dve, comb, E0, "l0f_parts")
            dve.drain().then_inc(sem("l0f_mix"), 2)
            with dve.Fori(0, E0 // 2) as i:
                for p in range(2):
                    for h in HALVES:
                        dve.wait_ge(sem("l0f_silu"), since("l0f_silu", 4 * i + 2 * p + h + 3))
                        dve.wait_ge(sem("l0f_up"), since("l0f_up", 4 * i + 2 * p + h + 1))
                        dve.tensor_tensor(half(A1, h), half(A0, h), ps[:, 2 + h, :], ALU.mult)
                        dve.drain()
                        dve.tensor_tensor(half(HC[:, p], h), half(A1, h), ps[:, 4 + h, :], ALU.mult).then_inc(sem("l0f_mix"), 1)
            for h in HALVES:
                dve.wait_ge(sem("l0f_out"), since("l0f_out", h + 1))
                dve.tensor_tensor(half(X, h), ps[:, 6 + h, :], half(X, h), ALU.add).then_inc(sem("x_ready"), 1)

        def l0f_gpsimd(pool):
            pass

        def l0f_sync(sp):
            sp.wait_ge(sem("l0f_down"), since("l0f_down", 1))
            with sp.Fori(0, E0 // 2) as i:
                for p in range(2):
                    sp.wait_ge(sem("l0f_down"), since("l0f_down", 2 * i + p + 1))
                    sp.dma_start(EW[:, p].rearrange("p a b -> p (a b)"),
                                 io["l0f_w"][bass.ds(2 * i + p, 1), :, :].rearrange("a p c -> (a p) c")).then_inc(sem("l0f_w%d" % p), 16)
                    sp.dma_start(ESEL[0:54, p, :],
                                 io["l0f_sel"][bass.ds(2 * i + p, 1), :, :].rearrange("a p c -> (a p) c")).then_inc(sem("l0f_w%d" % p), 16)

        RING = 4
        CB = sb("CB", [P, RING, KEYS])
        VALL = part_of_turns(0, "p (b c) -> p b c", b=B, c=2 * P)
        QB = A3.rearrange("p (r g c) -> p r g c", r=2, g=4)
        OWN = A4[:, 0:4 * P].rearrange("p (g c) -> p g c", g=4)
        PTX = sb("PTX", [P, 2, 2, HB])
        PTL = sb("PTL", [4, 2, P])
        VB = CB[:, 2:4, 0:2 * P]
        RNT = sb("RNT", [8, 2, P])
        VLB = RNT[0:4]
        RX = sb("RX", [P, 2, P])
        FX = DIFF[:, 0, 0:4, :].rearrange("p a b -> p (a b)")
        YX = ST[:, 3, 0:Q]
        XST = sb("XST", [P, 2, 3, 4])
        VLR = sb("VLR", [B, P])

        def ctx_loads(sp, n):
            def load(b, r):
                sp.dma_start(CB[:, r, :], io["ctx"][:, bass.ds(b, 1), :].rearrange("p a k -> p (a k)"))\
                    .then_inc(sem(n + "_c%d" % r), 16)
            for r in range(RING):
                load(r, r)
            sp.wait_ge(sem(n + "_vlc"), since(n + "_vlc", 1))
            sp.wait_ge(sem(n + "_vzero"), since(n + "_vzero", 1))
            sp.dma_start(io["last_rows"], VLR[:]).then_inc(sem(n + "_vlr"), 16)
            sp.wait_ge(sem(n + "_vlr"), since(n + "_vlr", 16))
            for g in range(4):
                sp.dma_start(VLAST[g:g + 1, :, 32 * g:32 * g + 32], io["last_rows"][:, 32 * g:32 * g + 32].unsqueeze(0))\
                    .then_inc(sem(n + "_vlast"), 16)
            with sp.Fori(1, B // RING) as i:
                for r in range(RING):
                    sp.wait_ge(sem(n + "_kv"), since(n + "_kv", RING * i + r - RING + 1))
                    load(RING * i + r, r)

        def value_loads(sp, n):
            sp.wait_ge(sem(n + "_vall"), since(n + "_vall", B + 2))
            sp.wait_ge(sem(n + "_kv"), since(n + "_kv", B))
            sp.wait_ge(sem(n + "_vlast"), since(n + "_vlast", 64))

            def values(b, p):
                sp.dma_start(VB[:, p, :], VALL[:, bass.ds(b, 1), :].rearrange("p a k -> p (a k)")).then_inc(sem(n + "_vb%d" % p), 16)
                sp.dma_start(VLB[:, p, :], VLAST[0:4, bass.ds(b, 1), :].rearrange("p a k -> p (a k)")).then_inc(sem(n + "_vb%d" % p), 16)

            values(0, 0)
            values(1, 1)
            with sp.Fori(1, B // 2) as i:
                for p in range(2):
                    sp.wait_ge(sem(n + "_o"), since(n + "_o", 2 * i + p - 1))
                    values(2 * i + p, p)

        def ctx_gpsimd(pool, n, queries):
            def spread_queries(b, p):
                pool.tensor_tensor(QB[:, p].rearrange("p g (h q) -> p (g h) q", h=4), over(columns(queries, b), 1, 16),
                                   OWN.rearrange("p g (h q) -> p (g h) q", h=4), ALU.mult).then_inc(sem(n + "_qb"), 1)

            pool.wait_ge(sem(n + "_q0"), since(n + "_q0", 2))
            spread_queries(0, 0)
            spread_queries(1, 1)
            with pool.Fori(1, B // 2) as i:
                for p in range(2):
                    pool.wait_ge(sem(n + "_s"), since(n + "_s", 8 * i + 4 * p - 4))
                    spread_queries(2 * i + p, p)

        SEGMENTS = ((0, 3), (3, 6), (6, B // RING))

        def kv_tensor(pe, n, wk, wv, read, segment):
            if segment == 0:
                pe.matmul(ps[0:B, 4, 0:P], LASTT[:], wv, start=True, stop=True).then_inc(sem(n + "_vl"), 1)
            with pe.Fori(*SEGMENTS[segment]) as i:
                for r in range(RING):
                    b, p = RING * i + r, r % 2
                    pe.wait_ge(sem(n + "_c%d" % r), since(n + "_c%d" % r, 16 * i + 16))
                    pe.wait_ge(sem(n + read), since(n + read, b + 1))
                    pe.matmul(ps[:, 4 + p, 0:KEYS], wk, CB[:, r, :], start=True, stop=True).then_inc(sem(n + "_k"), 1)
                    pe.wait_ge(sem(n + "_vall"), since(n + "_vall", b + 1))
                    for c in range(2):
                        m = pe.matmul(ps[:, 6 + p, c * P:(c + 1) * P], CB[:, r, c * P:(c + 1) * P], wv, start=True, stop=True)
                    m.then_inc(sem(n + "_kv"), 1)

        def kv_scalar(act, segment):
            if segment == 0:
                act.wait_ge(sem("l1x_vlc"), since("l1x_vlc", 1))
                act.drain().then_inc(sem("l1x_kt"), 2)
            with act.Fori(*SEGMENTS[segment]) as i:
                for r in range(RING):
                    b, p = RING * i + r, r % 2
                    act.wait_ge(sem("l1x_k"), since("l1x_k", b + 1))
                    act.wait_ge(sem("l1x_kall"), since("l1x_kall", b + 1))
                    act.activation(PX[:, p, 0, :], ps[:, 4 + p, 0:KEYS], ACT.Tanh, bias=BN[:, 1:2]).then_inc(sem("l1x_kt"), 1)

        def kv_vector(dve, n, bk, segment):
            if segment == 0:
                dve.wait_ge(sem(n + "_vl"), since(n + "_vl", 1))
                dve.tensor_copy(VLR[:], ps[0:B, 4, 0:P]).then_inc(sem(n + "_vlc"), 1)
                dve.drain().then_inc(sem(n + "_vall"), 2)
                dve.drain().then_inc(sem(n + "_kall"), 2)
            with dve.Fori(*SEGMENTS[segment]) as i:
                for r in range(RING):
                    b, p = RING * i + r, r % 2
                    place = KALL[:, bass.ds(b, 1), :].rearrange("p a k -> p (a k)")
                    if bk is None:
                        dve.wait_ge(sem(n + "_kt"), since(n + "_kt", b + 3))
                        dve.tensor_scalar(place, PX[:, p, 0, :], 1.0, None, ALU.mult).then_inc(sem(n + "_kall"), 1)
                    else:
                        dve.wait_ge(sem(n + "_k"), since(n + "_k", b + 1))
                        dve.tensor_scalar(place, ps[:, 4 + p, 0:KEYS], bk, None, ALU.add).then_inc(sem(n + "_kall"), 1)
                    dve.wait_ge(sem(n + "_kv"), since(n + "_kv", b + 1))
                    dve.tensor_scalar(VALL[:, bass.ds(b, 1), :].rearrange("p a c -> p (a c)"), ps[:, 6 + p, 0:2 * P], 1.0, None,
                                      ALU.mult).then_inc(sem(n + "_vall"), 1)

        def kv_gpsimd(pool, n, ready):
            pool.wait_ge(sem("x_ready"), since("x_ready", ready))
            pool.memset(VLAST[0:4], 0.0).then_inc(sem(n + "_vzero"), 1)

        def columns(x, b):
            return x[:, b * Q:(b + 1) * Q] if is_static(b) else x[:, bass.ds(b * Q, Q)]

        def pipeline(eng, step):
            for b in range(4):
                step(b, b % 2, b // 2)
            with eng.Fori(2, B // 2 - 1) as i:
                step(2 * i, 0, i)
                step(2 * i + 1, 1, i)
            for b in range(B - 2, B + 2):
                step(b, b % 2, b // 2)

        def is_static(b):
            return isinstance(b, int)

        def has(b, lag):
            return not is_static(b) or 0 <= b - lag < B

        def later(b, n):
            return not is_static(b) or b - n >= 0

        def ctx_tensor(pe, n, masked):
            pe.wait_ge(sem(n + "_q0"), since(n + "_q0", 2))
            pe.wait_ge(sem(n + "_vlast"), since(n + "_vlast", 64))

            def step(b, p, i):
                o = 1 - p
                if has(b, 0):
                    pe.wait_ge(sem(n + "_qb"), since(n + "_qb", b + 1))
                    for g in range(4):
                        if later(b, 1):
                            pe.wait_ge(sem(n + "_p"), since(n + "_p", 4 * b + g - 3))
                        if masked:
                            pe.matmul(ps[:, g, 0:KEYS], SELQ[:], MBIAS[:], start=True, stop=False)
                        pe.matmul(ps[:, g, 0:KEYS], QB[:, p, g, :], KALL[:, bass.ds(b, 1), :].rearrange("p a k -> p (a k)"),
                                  start=not masked, stop=True).then_inc(sem(n + "_s"), 1)
                if has(b, 1):
                    pe.wait_ge(sem(n + "_p"), since(n + "_p", 4 * b))
                    if later(b, 2):
                        pe.wait_ge(sem(n + "_t0"), since(n + "_t0", b - 1))
                    for c in range(2):
                        for g in range(4):
                            pe.transpose(ps[:, 6 + c, g * P:(g + 1) * P], PX[:, o, g, c * P:(c + 1) * P], cst("ident"))
                    pe.transpose(ps[0:4, 4, 0:P], PX[:, o, :, KEYS - 1:KEYS].rearrange("p g a -> p (g a)"), cst("ident"))\
                        .then_inc(sem(n + "_t"), 1)
                if has(b, 2):
                    pe.wait_ge(sem(n + "_om"), since(n + "_om", b - 1))
                    if later(b, 3):
                        pe.wait_ge(sem(n + "_att"), since(n + "_att", b - 2))
                    pe.matmul(ps[:, 5, P:P + Q], RX[:, p, :], cst("q_of"), start=True, stop=True)
                    pe.wait_ge(sem(n + "_t0"), since(n + "_t0", b - 1))
                    pe.wait_ge(sem(n + "_vb%d" % p), since(n + "_vb%d" % p, 32 * i))
                    pe.matmul(ps[:, 5, 0:P], VLB[:, p, :], PTL[:, p, :], start=True, stop=False, skip_group_check=True)
                    for c in range(2):
                        for g in range(4):
                            m = pe.matmul(ps[32 * g:32 * g + 32, 5, 0:P], VB[:, p, c * P + 32 * g:c * P + 32 * g + 32],
                                          PTX[:, p, c, g * P:(g + 1) * P], start=False, stop=(c == 1), skip_group_check=True)
                    m.then_inc(sem(n + "_o"), 1)

            pipeline(pe, step)

        def ctx_scalar(act, n):
            def step(b, p, i):
                o = 1 - p
                if has(b, 0):
                    for g in range(4):
                        act.wait_ge(sem(n + "_mx"), since(n + "_mx", 4 * b + g + 1))
                        if later(b, 2):
                            act.wait_ge(sem(n + "_t"), since(n + "_t", b - 1))
                        act.activation(PX[:, p, g, :], ps[:, g, 0:KEYS], ACT.Exp, bias=XST[:, p, 0, g:g + 1],
                                       accum_out=XST[:, p, 1, g:g + 1]).then_inc(sem(n + "_p"), 1)
                if has(b, 1):
                    act.wait_ge(sem(n + "_t"), since(n + "_t", b))
                    if later(b, 3):
                        act.wait_ge(sem(n + "_o"), since(n + "_o", b - 2))
                    act.copy(PTX[:, o, 0, :], ps[:, 6, :])
                    act.copy(PTX[:, o, 1, :], ps[:, 7, :])
                    act.copy(PTL[:, o, :], ps[0:4, 4, 0:P])
                    act.drain().then_inc(sem(n + "_t0"), 1)

            pipeline(act, step)

        def ctx_vector(dve, n, out, bias):
            def step(b, p, i):
                o = 1 - p
                if has(b, 0):
                    for g in (0, 2):
                        dve.wait_ge(sem(n + "_s"), since(n + "_s", 4 * b + g + 2))
                        dve.tensor_reduce(XST[:, p, 0, g:g + 2], ps[:, g:g + 2, 0:KEYS], AX.X, ALU.max,
                                          negate=True).then_inc(sem(n + "_mx"), 2)
                if has(b, 1):
                    dve.wait_ge(sem(n + "_p"), since(n + "_p", 4 * b))
                    if later(b, 3):
                        dve.wait_ge(sem(n + "_o"), since(n + "_o", b - 2))
                    dve.reciprocal(XST[:, o, 2, :], XST[:, o, 1, :])
                    dve.drain()
                    dve.tensor_tensor(RX[:, o, :].rearrange("p (g c) -> p g c", g=4), over(XST[:, o, 2, :], 2, 32),
                                      cst("own_head").rearrange("p (g c) -> p g c", g=4), ALU.mult).then_inc(sem(n + "_om"), 1)
                if has(b, 2):
                    dve.wait_ge(sem(n + "_o"), since(n + "_o", b - 1))
                    dve.tensor_tensor(FX, ps[:, 5, 0:P], cst("in_four"), ALU.mult)
                    dve.drain()
                    dve.tensor_reduce(YX, FX.rearrange("p (h q) -> p q h", h=4), AX.X, ALU.add)
                    dve.drain()
                    dve.tensor_tensor(YX, YX, ps[:, 5, P:P + Q], ALU.mult)
                    dve.drain()
                    dve.tensor_scalar(columns(out, b - 2), YX, bias, None, ALU.add).then_inc(sem(n + "_att"), 1)

            pipeline(dve, step)

        def l1x_tensor(pe):
            def kv(segment):
                kv_tensor(pe, "l1x", WNK[:], w("L1_xattn_wv"), "_kt", segment)
            ln_tensor(pe, 3, kv)
            project(pe, WNQ[:], XN, (2, 3), "l1x_qa", [("xn_ready", 7)])
            kv(2)
            ctx_tensor(pe, "l1x", True)
            pe.wait_ge(sem("l1x_att"), since("l1x_att", B))
            for h in HALVES:
                pe.matmul(ps[:, h, :], w("L1_xattn_wo"), half(A2, h), start=True, stop=True).then_inc(sem("l1x_out"), 1)
            inverse_tensor(pe, "l1x", 0, A1, "mean", (2, 4))

        def l1x_scalar(act):
            def kv(segment):
                kv_scalar(act, segment)
            ln_scalar(act, 3, kv)
            for h in HALVES:
                act.wait_ge(sem("l1x_qa"), since("l1x_qa", h + 1))
                act.activation(half(A1, h), ps[:, 2 + h, :], ACT.Tanh, bias=BN[:, 0:1]).then_inc(sem("l1x_qt"), 1)
            kv(2)
            ctx_scalar(act, "l1x")
            load_root_table(act)
            for h in HALVES:
                act.wait_ge(sem("l1x_o2"), since("l1x_o2", h + 1))
                act.activation(half(A1, h), half(A0, h), ACT.Square).then_inc(sem("l1x_sq"), 1)
            inverse_scalar(act, "l1x", 0, "mean", 2, EPS[:, 1:2])

        def l1x_vector(dve):
            def kv(segment):
                kv_vector(dve, "l1x", None, segment)
            ln_vector(dve, 3, kv)
            for h in HALVES:
                dve.wait_ge(sem("l1x_qt"), since("l1x_qt", h + 1))
                dve.tensor_scalar(half(A1, h), half(A1, h), SHAPE_SCALE, INVT[:], ALU.mult, ALU.mult)
            kv(2)
            dve.tensor_tensor(OWN, over(cst("in_four"), 1, 4), over(cst("batch_of"), 2, P), ALU.mult)
            dve.drain().then_inc(sem("l1x_q0"), 2)
            ctx_vector(dve, "l1x", A2, vec("L1_xattn_bv"))
            for h in HALVES:
                dve.wait_ge(sem("l1x_out"), since("l1x_out", h + 1))
                dve.tensor_scalar(half(A0, h), ps[:, h, :], vec("L1_xattn_bo"), None, ALU.add).then_inc(sem("l1x_o2"), 1)
            inverse_vector(dve, "l1x", 0, A1, "mean")
            for h in HALVES:
                dve.wait_ge(sem("l1x_spread"), since("l1x_spread", h + 1))
                dve.tensor_tensor(half(A0, h), half(A0, h), ps[:, 4 + h, :], ALU.mult)
                dve.drain()
                dve.scalar_tensor_tensor(out=half(X, h), in0=half(A0, h), scalar=vec("L1_xattn_gamma"), in1=half(X, h),
                                         op0=ALU.mult, op1=ALU.add).then_inc(sem("x_ready"), 1)

        def l1x_sync(sp):
            ctx_loads(sp, "l1x")
            value_loads(sp, "l1x")

        def l1x_gpsimd(pool):
            kv_gpsimd(pool, "l1x", 8)
            ctx_gpsimd(pool, "l1x", A1)

        def nothing(eng):
            pass

        VO = part_of_shared(0, "p (t c) -> p t c", t=NT, c=132)
        KVM = part_of_shared(2048, "p (r b t c) -> p r b t c", r=2, b=4, t=2, c=P)
        KSUM = sb("KSUM", [P, B])

        def half_tok(x, h):
            return x[:, 4 * h:4 * h + 4, :].rearrange("p t c -> p (t c)")

        def l1a_tensor(pe):
            ln_tensor(pe, 4)
            for name, bank, done in (("L1a_q", 4, "l1a_q"), ("L1a_k", 6, "l1a_kv"), ("L1a_v", 0, "l1a_kv")):
                for t in range(NT):
                    if bank == 4 and t % 4 == 0:
                        pe.wait_ge(sem("xn_ready"), since("xn_ready", 9 + t // 4))
                    m = pe.matmul(ps[:, bank + t // 4, (t % 4) * P:(t % 4 + 1) * P], XN[:, t * P:(t + 1) * P], w(name),
                                  start=True, stop=True)
                    if t % 4 == 3:
                        m.then_inc(sem(done), 1)
            for h in HALVES:
                pe.wait_ge(sem("l1a_qf"), since("l1a_qf", h + 1))
                for t in range(4 * h, 4 * h + 4):
                    m = pe.transpose(ps[:, 4 + h, (t % 4) * P:(t % 4 + 1) * P], A1[:, t * P:(t + 1) * P], cst("ident"))
                m.then_inc(sem("l1a_qs"), 1)
            pe.wait_ge(sem("l1a_vc"), since("l1a_vc", 2))
            pe.wait_ge(sem("l1a_kf"), since("l1a_kf", 2))
            for u in range(PAIRS):
                if u >= 1:
                    pe.wait_ge(sem("l1a_m"), since("l1a_m", u))
                for s in range(2):
                    t = 2 * u + s
                    for b in range(4):
                        m = pe.matmul(ps[:, b, s * 129:(s + 1) * 129], TOK[32 * b:32 * b + 32, t, :],
                                      VO[32 * b:32 * b + 32, t, 0:129], start=True, stop=True)
                m.then_inc(sem("l1a_w"), 1)
                if u >= 1:
                    l1a_out(pe, u - 1)
            l1a_out(pe, PAIRS - 1)
            for h in HALVES:
                pe.wait_ge(sem("l1a_qk"), since("l1a_qk", h + 1))
                pe.matmul(ps[:, 4 + h, :], cst("same_head"), half(A1, h), start=True, stop=True).then_inc(sem("l1a_den"), 1)
            project(pe, w("L1_attn_w_proj"), A3, (0, 1), "l1a_out", [("l1a_y", 1)])

        def l1a_out(pe, u):
            pe.wait_ge(sem("l1a_m"), since("l1a_m", u + 1))
            pe.wait_ge(sem("l1a_q2"), since("l1a_q2", 2))
            for s in range(2):
                for b in range(4):
                    c = (2 * u + s) * P + b * Q
                    m = pe.matmul(ps[:, 6 + u // 2, c % HB:c % HB + Q], KVM[:, u % 2, b, s, :], A0[:, c:c + Q], start=True, stop=True)
            m.then_inc(sem("l1a_num"), 1)

        def l1a_scalar(act):
            ln_scalar(act, 4)
            for h in HALVES:
                act.wait_ge(sem("l1a_kv"), since("l1a_kv", 3 + h))
                act.copy(VO[:, 4 * h:4 * h + 4, 0:P], ps[:, h, :].rearrange("p (t c) -> p t c", t=4)).then_inc(sem("l1a_vc"), 1)
            for h in HALVES:
                act.wait_ge(sem("l1a_qs"), since("l1a_qs", h + 1))
                act.copy(half(A0, h), ps[:, 4 + h, :]).then_inc(sem("l1a_q2"), 1)

        def l1a_vector(dve):
            ln_vector(dve, 4)
            dve.memset(VO[:, :, P:P + 1], 1.0)

            def token_norm(x):
                g = x.rearrange("p (g d) -> p g d", d=HD)
                total = RT[:, 0, :]
                dve.tensor_reduce(total, g, AX.X, ALU.add)
                dve.drain()
                dve.reciprocal(total, total)
                dve.drain()
                dve.tensor_tensor(g, g, over(total, 2, HD), ALU.mult)
                dve.drain()

            def features(x, banks):
                dve.tensor_scalar(x, banks.rearrange("p h c -> p (h c)"), 0.0, 1e-6, ALU.max, ALU.add)
                dve.drain()
                token_norm(x)
                dve.tensor_tensor(A4, x, x, ALU.mult)
                dve.drain()
                dve.tensor_tensor(x, A4, x, ALU.mult)
                dve.drain()
                token_norm(x)

            dve.wait_ge(sem("l1a_q"), since("l1a_q", 2))
            features(A1, ps[:, 4:6, :])
            dve.drain().then_inc(sem("l1a_qf"), 2)
            dve.wait_ge(sem("l1a_kv"), since("l1a_kv", 2))
            features(TOK[:].rearrange("p t c -> p (t c)"), ps[:, 6:8, :])
            dve.drain().then_inc(sem("l1a_kf"), 2)
            for u in range(PAIRS):
                dve.wait_ge(sem("l1a_w"), since("l1a_w", u + 1))
                if u >= 2:
                    dve.wait_ge(sem("l1a_num"), since("l1a_num", u - 1))
                for s in range(2):
                    kv = ps[:, 0:4, s * 129:(s + 1) * 129]
                    dve.tensor_tensor(KVM[:, u % 2, :, s, :], kv[:, :, 0:P], over(cst("same_head"), 1, 4), ALU.mult)
                    dve.tensor_copy(KSUM[:, (2 * u + s) * 4:(2 * u + s) * 4 + 4], kv[:, :, P:P + 1].rearrange("p b a -> p (b a)"))
                dve.drain().then_inc(sem("l1a_m"), 1)
            for h in HALVES:
                def batches(x):
                    return half(x, h).rearrange("p (b q) -> p b q", q=Q)
                dve.wait_ge(sem("l1a_q2"), since("l1a_q2", h + 1))
                dve.tensor_tensor(batches(A1), batches(A0), over(KSUM[:, 16 * h:16 * h + 16], 2, Q),
                                  ALU.mult).then_inc(sem("l1a_qk"), 1)
            for h in HALVES:
                def batches(x):
                    return half(x, h).rearrange("p (b q) -> p b q", q=Q)
                z, y, o = half(A2, h), half(A4, h), half(A3, h)
                dve.wait_ge(sem("l1a_den"), since("l1a_den", h + 1))
                dve.tensor_scalar(z, ps[:, 4 + h, :], 1e-6, None, ALU.add)
                dve.drain()
                dve.reciprocal(z, z)
                dve.drain()
                dve.wait_ge(sem("l1a_num"), since("l1a_num", 2 * h + 2))
                dve.tensor_tensor(y, ps[:, 6 + h, :], z, ALU.mult)
                dve.drain()
                dve.tensor_scalar(o, y, CONVW[:, 1:2], vec("L1_attn_b_dwc"), ALU.mult, ALU.add)
                dve.drain()
                dve.scalar_tensor_tensor(out=batches(A3)[:, :, 1:Q], in0=batches(A4)[:, :, 0:Q - 1], scalar=CONVW[:, 0:1],
                                         in1=batches(A3)[:, :, 1:Q], op0=ALU.mult, op1=ALU.add)
                dve.drain()
                dve.scalar_tensor_tensor(out=batches(A3)[:, :, 0:Q - 1], in0=batches(A4)[:, :, 1:Q], scalar=CONVW[:, 2:3],
                                         in1=batches(A3)[:, :, 0:Q - 1], op0=ALU.mult, op1=ALU.add)
                dve.drain()
                dve.tensor_tensor(o, o, y, ALU.add).then_inc(sem("l1a_y"), 1)
            add_to_residual(dve, "l1a_out", (0, 1), vec("L1_attn_b_proj"))

        GATE = part_of_shared(0, "p (t n) -> p t n", t=NT, n=255)
        LEFT = part_of_shared(2048, "p (t n) -> p t n", t=NT, n=255)
        LP = [part_of_shared(4096 + 2048 * i, "p (t n) -> p t n", t=NT, n=256) for i in range(2)]
        LPT = part_of_shared(8192, "p (c n) -> p c n", c=2, n=T)

        def l1f_tensor(pe):
            ln_tensor(pe, 5)
            project(pe, w("L1_ffn_Wq"), XN, (4, 5), "l1f_q", [("xn_ready", 11)])
            for t in range(NT):
                pe.wait_ge(sem("l1f_qc"), since("l1f_qc", t // 4 + 1))
                m = pe.matmul(ps[:, t // 2, (t % 2) * 255:(t % 2 + 1) * 255], A0[:, t * P:(t + 1) * P], ROUT[:], start=True, stop=True)
                if t % 2 == 1:
                    m.then_inc(sem("l1f_g"), 1)
            pe.wait_ge(sem("l1f_lp"), since("l1f_lp", 1))
            for c in range(2):
                for t in range(NT):
                    m = pe.transpose(ps[:, 4 + 2 * c + t // 4, (t % 4) * P:(t % 4 + 1) * P], LP[1][:, t, c * P:(c + 1) * P], cst("ident"))
                    if t % 4 == 3:
                        m.then_inc(sem("l1f_t"), 1)
            pe.wait_ge(sem("l1f_lpt"), since("l1f_lpt", 4))
            for h in HALVES:
                pe.matmul(ps[:, h, :], w("leaves0"), half(LPT[:, 0, :], h), start=True, stop=False)
                pe.matmul(ps[:, h, :], w("leaves1"), half(LPT[:, 1, :], h), start=False, stop=True).then_inc(sem("l1f_r"), 1)
            project(pe, w("L1_ffn_Wout_w"), A1, (2, 3), "l1f_out", [("l1f_rc", 1)])

        def l1f_scalar(act):
            ln_scalar(act, 5)
            for h in HALVES:
                act.wait_ge(sem("l1f_q"), since("l1f_q", h + 1))
                act.copy(half(A0, h), ps[:, 4 + h, :]).then_inc(sem("l1f_qc"), 1)
            for u in range(4):
                act.wait_ge(sem("l1f_g"), since("l1f_g", u + 1))
                act.activation(GATE[:, 2 * u:2 * u + 2, :], ps[:, u, 0:510].rearrange("p (t n) -> p t n", t=2),
                               ACT.Sigmoid).then_inc(sem("l1f_gs"), 1)
            for c in range(2):
                for h in HALVES:
                    act.wait_ge(sem("l1f_t"), since("l1f_t", 2 * c + h + 1))
                    act.copy(half(LPT[:, c, :], h), ps[:, 4 + 2 * c + h, :]).then_inc(sem("l1f_lpt"), 1)
            for h in HALVES:
                act.wait_ge(sem("l1f_r"), since("l1f_r", h + 1))
                act.copy(half(A1, h), ps[:, h, :]).then_inc(sem("l1f_rc"), 1)

        def l1f_vector(dve):
            ln_vector(dve, 5)
            for u in range(4):
                dve.wait_ge(sem("l1f_gs"), since("l1f_gs", u + 1))
                dve.tensor_scalar(LEFT[:, 2 * u:2 * u + 2, :], GATE[:, 2 * u:2 * u + 2, :], -1.0, 1.0, ALU.mult, ALU.add)
            dve.drain()
            dve.tensor_copy(LP[0][:, :, 0:1], LEFT[:, :, 0:1])
            dve.tensor_copy(LP[0][:, :, 1:2], GATE[:, :, 0:1])
            dve.drain()
            for level in range(1, 8):
                n = 2 ** level
                src, dst = LP[(level - 1) % 2][:, :, 0:n], LP[level % 2][:, :, 0:2 * n].rearrange("p t (n s) -> p t n s", s=2)
                dve.tensor_tensor(dst[:, :, :, 0], src, LEFT[:, :, n - 1:2 * n - 1], ALU.mult)
                dve.tensor_tensor(dst[:, :, :, 1], src, GATE[:, :, n - 1:2 * n - 1], ALU.mult)
                dve.drain()
            dve.drain().then_inc(sem("l1f_lp"), 1)
            add_to_residual(dve, "l1f_out", (2, 3), vec("L1_ffn_Wout_b"))

        CX = part_of_turns(0, "p (r b k) -> p r b k", r=4, b=4, k=KEYS)
        CTOK = part_of_turns(4 * 4 * KEYS, "p (r b c n) -> p r b c n", r=4, b=4, c=2, n=P)
        SIM = part_of_shared(4104, "p (r k) -> p r k", r=2, k=KEYS)
        HIT = part_of_shared(4618, "p (r k) -> p r k", r=2, k=KEYS)
        RNB = part_of_shared(5132, "p (r k) -> p r k", r=2, k=KEYS)
        HITT = part_of_shared(5646, "p (r c n) -> p r c n", r=2, c=2, n=P)
        SQC = part_of_shared(6158, "p (g n) -> p g n", g=8, n=P)
        LASTROW = part_of_shared(7182, "p (t n) -> p t n", t=NT, n=P)
        HITL = sb("HITL", [4, 2, P])
        HITB = sb("HITB", [P, 2, 4])
        RN = sb("RN", [P, 2, 8])
        RL = sb("RL", [P, 16])
        XC = sb("XC", [P, 2, 4])

        def l2x_sync(sp):
            sp.wait_ge(sem("x_ready"), since("x_ready", 10))
            for t in range(NT):
                if t >= 4:
                    sp.wait_ge(sem("l2x_pv"), since("l2x_pv", t - 3))
                sp.dma_start(CX[:, t % 4], io["ctx"][:, 4 * t:4 * t + 4, :]).then_inc(sem("l2x_c%d" % (t % 4)), 16)
                sp.dma_start(CTOK[:, t % 4], io["ctx_tok"][:, 4 * t:4 * t + 4]).then_inc(sem("l2x_c%d" % (t % 4)), 16)
                if t == 3:
                    sp.wait_ge(sem("x_ready"), since("x_ready", 14))
                    sp.dma_start(LASTROW[0:4].rearrange("p t n -> p (t n)"), io["ctx_last"]).then_inc(sem("l2x_last"), 16)

        def l2x_tensor(pe):
            ln_tensor(pe, 6)
            pe.wait_ge(sem("l2x_sq"), since("l2x_sq", 1))
            for t in range(NT):
                pe.matmul(ps[:, 7, t:t + 1], A1[:, t * P:(t + 1) * P], cst("ones")[:, 0:1], start=True, stop=True)
                m = pe.matmul(ps[:, 7, 8 + t:9 + t], A2[:, t * P:(t + 1) * P], cst("ones")[:, 0:1], start=True, stop=True)
            m.then_inc(sem("l2x_n2"), 1)
            for t in range(NT + 1):
                if t < NT:
                    p = t % 2
                    pe.wait_ge(sem("l2x_c%d" % (t % 4)), since("l2x_c%d" % (t % 4), 32 * (t // 4 + 1)))
                    if t >= 2:
                        pe.wait_ge(sem("l2x_sim"), since("l2x_sim", t - 1))
                    for b in range(4):
                        n = (4 * t + b) * Q
                        m = pe.matmul(ps[32 * b:32 * b + 32, p, 0:KEYS], XN[:, n:n + Q], CX[:, t % 4, b, :], start=True, stop=True)
                    m.then_inc(sem("l2x_s"), 1)
                    pe.wait_ge(sem("l2x_rn"), since("l2x_rn", t + 1))
                    if t >= 2:
                        pe.wait_ge(sem("l2x_rnb"), since("l2x_rnb", t - 1))
                    pe.transpose(ps[0:8, 2 + p, 2 * P:3 * P], RN[:, p, :], cst("ident")).then_inc(sem("l2x_rt"), 1)
                    pe.wait_ge(sem("l2x_rtc"), since("l2x_rtc", t + 1))
                    for c in range(2):
                        m = pe.matmul(ps[:, 2 + p, c * P:(c + 1) * P], cst("row_of")[0:8, c * P:(c + 1) * P], RNT[:, p, :],
                                      start=True, stop=True)
                    m.then_inc(sem("l2x_r"), 1)
                if t >= 1:
                    u, p = t - 1, (t - 1) % 2
                    pe.wait_ge(sem("l2x_hit"), since("l2x_hit", u + 1))
                    for c in range(2):
                        pe.transpose(ps[:, 4 + p, c * P:(c + 1) * P], HIT[:, p, c * P:(c + 1) * P], cst("ident"))
                    pe.transpose(ps[0:4, 4 + p, 2 * P:3 * P], HITB[:, p, :], cst("ident")).then_inc(sem("l2x_ht"), 1)
                    pe.wait_ge(sem("l2x_hc"), since("l2x_hc", u + 1))
                    if u >= 1:
                        pe.wait_ge(sem("l2x_x"), since("l2x_x", u))
                    pe.matmul(ps[:, 6, 0:P], LASTROW[0:4, u, :], HITL[:, p, :], start=True, stop=False, skip_group_check=True)
                    for b in range(4):
                        for c in range(2):
                            m = pe.matmul(ps[:, 6, b * Q:(b + 1) * Q], CTOK[:, u % 4, b, c, :], HITT[:, p, c, b * Q:(b + 1) * Q],
                                          start=False, stop=(c == 1), skip_group_check=True)
                    m.then_inc(sem("l2x_pv"), 1)

        def l2x_scalar(act):
            ln_scalar(act, 6)
            act.wait_ge(sem("l2x_n2"), since("l2x_n2", 1))
            act.activation(RL[:], ps[:, 7, 0:16], ACT.Sqrt).then_inc(sem("l2x_nl"), 1)
            def squares(t):
                r = t % 4
                act.wait_ge(sem("l2x_c%d" % r), since("l2x_c%d" % r, 32 * (t // 4 + 1)))
                if t >= 1:
                    act.wait_ge(sem("l2x_ns"), since("l2x_ns", t))
                act.activation(SQC, CTOK[:, r].rearrange("p b c n -> p (b c) n"), ACT.Square).then_inc(sem("l2x_sc"), 1)

            squares(0)
            for t in range(NT + 1):
                if t < NT:
                    p = t % 2
                    act.wait_ge(sem("l2x_ns"), since("l2x_ns", t + 1))
                    act.activation(RN[:, p, :], RN[:, p, :], ACT.Sqrt).then_inc(sem("l2x_nr"), 1)
                    act.wait_ge(sem("l2x_rt"), since("l2x_rt", t + 1))
                    act.copy(RNT[:, p, :], ps[0:8, 2 + p, 2 * P:3 * P]).then_inc(sem("l2x_rtc"), 1)
                    act.wait_ge(sem("l2x_r"), since("l2x_r", t + 1))
                    if t >= 2:
                        act.wait_ge(sem("l2x_sim"), since("l2x_sim", t - 1))
                    act.copy(RNB[:, p, 0:2 * P], ps[:, 2 + p, 0:2 * P]).then_inc(sem("l2x_rnb"), 1)
                if t + 1 < NT:
                    squares(t + 1)
                if t >= 1:
                    u, p = t - 1, (t - 1) % 2
                    act.wait_ge(sem("l2x_ht"), since("l2x_ht", u + 1))
                    if u >= 2:
                        act.wait_ge(sem("l2x_pv"), since("l2x_pv", u - 1))
                    act.copy(HITT[:, p].rearrange("p c n -> p (c n)"), ps[:, 4 + p, 0:2 * P])
                    act.copy(HITL[:, p, :], ps[0:4, 4 + p, 2 * P:3 * P])
                    act.drain().then_inc(sem("l2x_hc"), 1)

        def l2x_vector(dve):
            ln_vector(dve, 6)
            dve.wait_ge(sem("l2x_last"), since("l2x_last", 16))
            dve.drain()
            dve.tensor_tensor(A2, XN[:], XN[:], ALU.mult)
            dve.tensor_tensor(A1.rearrange("p (b q) -> p b q", q=Q), over(LASTT[:], 2, Q), over(LASTT[:], 2, Q), ALU.mult)
            dve.drain().then_inc(sem("l2x_sq"), 1)
            dve.wait_ge(sem("l2x_nl"), since("l2x_nl", 1))
            dve.tensor_scalar(RL[:], RL[:], 1e-12, None, ALU.max)
            dve.drain()
            dve.reciprocal(RL[:], RL[:])
            dve.drain()
            for t in range(NT + 2):
                if t < NT:
                    p = t % 2
                    dve.wait_ge(sem("l2x_sc"), since("l2x_sc", t + 1))
                    if t >= 2:
                        dve.wait_ge(sem("l2x_r"), since("l2x_r", t - 1))
                    dve.tensor_reduce(RN[:, p, :].rearrange("p (c b) -> p b c", c=2), SQC.rearrange("p (b c) n -> p b c n", c=2),
                                      AX.X, ALU.add).then_inc(sem("l2x_ns"), 1)
                    dve.wait_ge(sem("l2x_nr"), since("l2x_nr", t + 1))
                    dve.tensor_scalar(RN[:, p, :], RN[:, p, :], 1e-12, None, ALU.max)
                    dve.drain()
                    dve.reciprocal(RN[:, p, :], RN[:, p, :]).then_inc(sem("l2x_rn"), 1)
                if 1 <= t <= NT:
                    u, p = t - 1, (t - 1) % 2
                    dve.tensor_copy(RNB[:, p, 2 * P:KEYS], RL[:, u:u + 1])
                    dve.drain()
                    dve.wait_ge(sem("l2x_rnb"), since("l2x_rnb", u + 1))
                    dve.wait_ge(sem("l2x_s"), since("l2x_s", u + 1))
                    if u >= 2:
                        dve.wait_ge(sem("l2x_ht"), since("l2x_ht", u - 1))
                    sim, hit, x = SIM[:, p, :], HIT[:, p, :], XC[:, p, :]
                    dve.scalar_tensor_tensor(out=sim, in0=ps[:, p, 0:KEYS], scalar=RL[:, 8 + u:9 + u], in1=RNB[:, p, :],
                                             op0=ALU.mult, op1=ALU.mult).then_inc(sem("l2x_sim"), 1)
                    dve.drain()
                    dve.tensor_reduce(x[:, 0:1], sim, AX.X, ALU.max)
                    dve.drain()
                    dve.scalar_tensor_tensor(out=sim, in0=sim, scalar=x[:, 0:1], in1=cst("key_back"), op0=ALU.is_equal, op1=ALU.mult)
                    dve.drain()
                    dve.tensor_reduce(x[:, 1:2], sim, AX.X, ALU.min)
                    dve.drain()
                    dve.tensor_scalar(hit, cst("key_back"), x[:, 1:2], None, ALU.is_equal)
                    dve.drain()
                    dve.tensor_scalar(HITB[:, p, :], cst("batch_of"), hit[:, KEYS - 1:KEYS], None, ALU.mult).then_inc(sem("l2x_hit"), 1)
                if t >= 2:
                    u = t - 2
                    dve.wait_ge(sem("l2x_pv"), since("l2x_pv", u + 1))
                    xs = X[:, u * P:(u + 1) * P]
                    dve.tensor_tensor(xs, ps[:, 6, 0:P], xs, ALU.add).then_inc(sem("l2x_x"), 1)
                    if u % 4 == 3:
                        dve.drain().then_inc(sem("x_ready"), 1)

        LROW = sb("LROW", [P, 4, HD])
        LSM = sb("LSM", [P, 4])

        def l2a_tensor(pe):
            ln_tensor(pe, 7)
            project(pe, w("L2_attn_Wq"), XN, (4, 5), "l2a_q", [("xn_ready", 15)])
            project(pe, w("L2_attn_Wk"), XN, (6, 7), "l2a_k")
            for t in range(NT):
                m = pe.matmul(ps[:, t // 4, (t % 4) * P:(t % 4 + 1) * P], XN[:, t * P:(t + 1) * P], w("L2_attn_Wv"), start=True, stop=True)
                if t % 4 == 3:
                    m.then_inc(sem("l2a_v"), 1)
            project(pe, cst("rot"), A0, (2, 3), "l2a_qr", [("l2a_qc", 1)])
            project(pe, cst("rot"), A1, (4, 5), "l2a_kr", [("l2a_kc", 1)])
            pe.wait_ge(sem("l2a_vc"), since("l2a_vc", 2))
            pe.wait_ge(sem("l2a_qrope"), since("l2a_qrope", 2))
            block_tensor(pe, "l2a", A2, TOK, "_s_read", 64)
            inverse_tensor(pe, "l2a", 0, A1, "pair_mean", (0, 4))
            project(pe, w("L2_attn_Wo"), A0, (2, 3), "l2a_out", [("l2a_yn", 1)])

        def l2a_scalar(act):
            act.wait_ge(sem("l2a_ls"), since("l2a_ls", 1))
            act.activation(LSM[:, 0:2], LSM[:, 0:2], ACT.Exp).then_inc(sem("l2a_le"), 1)
            ln_scalar(act, 7)
            for h in HALVES:
                act.wait_ge(sem("l2a_q"), since("l2a_q", h + 1))
                act.copy(half(A0, h), ps[:, 4 + h, :]).then_inc(sem("l2a_qc"), 1)
            for h in HALVES:
                act.wait_ge(sem("l2a_k"), since("l2a_k", h + 1))
                act.copy(half(A1, h), ps[:, 6 + h, :]).then_inc(sem("l2a_kc"), 1)
            for h in HALVES:
                act.wait_ge(sem("l2a_v"), since("l2a_v", h + 1))
                act.copy(half_tok(TOK, h), ps[:, h, :]).then_inc(sem("l2a_vc"), 1)
            block_softmax_scalar(act, "l2a", False)
            load_root_table(act)
            for h in HALVES:
                act.wait_ge(sem("l2a_y"), since("l2a_y", 2 * h + 2))
                act.activation(half(A1, h), half(A4, h), ACT.Square).then_inc(sem("l2a_sq"), 1)
            inverse_scalar(act, "l2a", 0, "pair_mean", 0, EPS[:, 0:1])

        def l2a_vector(dve):
            dve.tensor_tensor(LROW[:, 0, :], LROW[:, 0, :], LROW[:, 1, :], ALU.mult)
            dve.tensor_tensor(LROW[:, 2, :], LROW[:, 2, :], LROW[:, 3, :], ALU.mult)
            dve.drain()
            dve.tensor_reduce(LSM[:, 0:2], LROW[:].rearrange("p (a b) d -> p a b d", b=2)[:, :, 0], AX.X, ALU.add).then_inc(sem("l2a_ls"), 1)
            dve.wait_ge(sem("l2a_le"), since("l2a_le", 1))
            dve.tensor_tensor(NEG_LAMBDA[:], LSM[:, 1:2], LSM[:, 0:1], ALU.subtract)
            dve.drain()
            dve.tensor_scalar(NEG_LAMBDA[:], NEG_LAMBDA[:], LAMBDA_INIT, None, ALU.subtract)
            ln_vector(dve, 7)
            rope = cst("rope").rearrange("p (k q) -> p k q", k=4)

            def rotate(x, bank, k, out, done, scale):
                for h in HALVES:
                    dve.wait_ge(sem(done[0]), since(done[0], h + 1))
                    def batches(y):
                        return y.rearrange("p (b q) -> p b q", q=Q)
                    dve.tensor_tensor(batches(half(out, h)), batches(ps[:, bank + h, :]), over(rope[:, k + 1], 1, 16), ALU.mult)
                    dve.tensor_tensor(batches(half(A5, h)), batches(half(x, h)), over(rope[:, k], 1, 16), ALU.mult)
                    dve.drain()
                    dve.tensor_tensor(half(out, h), half(out, h), half(A5, h), ALU.add)
                    dve.drain()
                    if scale:
                        dve.tensor_scalar(half(out, h), half(out, h), SHAPE_SCALE, None, ALU.mult)
                        dve.drain()
                    dve.drain().then_inc(sem(done[1]), 1)

            rotate(A0, 2, 0, A2, ("l2a_qr", "l2a_qrope"), True)
            rotate(A1, 4, 2, A3, ("l2a_kr", "l2a_krope"), False)
            block_softmax_vector(dve, "l2a", A4, False)
            inverse_vector(dve, "l2a", 0, A1, "pair_mean")
            for h in HALVES:
                dve.wait_ge(sem("l2a_spread"), since("l2a_spread", h + 1))
                dve.scalar_tensor_tensor(out=half(A0, h), in0=half(A4, h), scalar=1.0 - LAMBDA_INIT, in1=ps[:, 4 + h, :],
                                         op0=ALU.mult, op1=ALU.mult).then_inc(sem("l2a_yn"), 1)
            for h in HALVES:
                dve.wait_ge(sem("l2a_out"), since("l2a_out", h + 1))
                dve.tensor_tensor(half(X, h), ps[:, 2 + h, :], half(X, h), ALU.add).then_inc(sem("x_ready"), 1)

        def l2a_gpsimd(pool):
            spread(pool, "l2a", A3, "l2a_krope")

        DISPATCH = part_of_shared(0, "p (t s) -> p t s", t=NT, s=HB).bitcast(BF16)
        COLLECT = part_of_shared(4096, "p (s t) -> p s t", s=NT, t=HB).bitcast(BF16)
        XPARTS = part_of_shared(8192, "p (r t c) -> p r t c", r=3, t=NT, c=64).bitcast(BF16)
        YPARTS = part_of_shared(9728, "p (r t c) -> p r t c", r=3, t=NT, c=64).bitcast(BF16)
        BIGW = part_of_turns(0, "p (r c) -> p r c", r=3, c=1028)
        W4 = part_of_turns(0, "p (r c) -> p r c", r=4, c=1024)
        HR = sb("HR", [P, 2, 4, CAPACITY])
        SLOT = sb("SLOT", [P, 2, NT])
        OHB = sb("OHB", [P, P], BF16)
        UNTB = sb("UNTB", [P, 2, P], BF16)

        def three_parts(dve, x, parts, left):
            dve.tensor_copy(parts[:, 0], x)
            dve.drain()
            dve.tensor_tensor(left, x, parts[:, 0], ALU.subtract)
            dve.drain()
            dve.tensor_copy(parts[:, 1], left)
            dve.drain()
            dve.tensor_tensor(left, left, parts[:, 1], ALU.subtract)
            dve.drain()
            dve.tensor_copy(parts[:, 2], left)
            dve.drain()

        def as_tiles(x):
            return x.rearrange("p (t c) -> p t c", t=NT)

        def l2f_tensor(pe):
            ln_tensor(pe, 8)
            pe.wait_ge(sem("xn_ready"), since("xn_ready", 18))
            route_tensor(pe, WG2[:], 16).then_inc(sem("l2f_logits"), 1)
            for t in range(NT):
                m = pe.transpose(ps[:, 4 + t // 4, (t % 4) * P:(t % 4 + 1) * P], XN[:, t * P:(t + 1) * P], cst("ident"))
            m.then_inc(sem("l2f_xt"), 1)
            pe.wait_ge(sem("l2f_oh"), since("l2f_oh", 1))
            pe.matmul(ps[:, 1, 0:P], UNTB[:, 0, :], OHB[:], start=True, stop=True)
            pe.matmul(ps[:, 1, P:2 * P], UNTB[:, 1, :], OHB[:], start=True, stop=True).then_inc(sem("l2f_pre"), 1)
            for k in range(2):
                pe.wait_ge(sem("l2f_diag"), since("l2f_diag", k + 1))
                for t in range(NT):
                    m = pe.matmul(ps[:, 2 * k + t // 4, (t % 4) * P:(t % 4 + 1) * P], cst("ones"), (A3, A4)[k][:, t * P:(t + 1) * P],
                                  start=True, stop=True)
                m.then_inc(sem("l2f_row"), 1)
            pe.wait_ge(sem("l2f_disp"), since("l2f_disp", 1))
            for h in HALVES:
                n = 0
                for t in range(NT):
                    for r in range(3):
                        m = pe.matmul(ps[:, 6 + h, :], XPARTS[:, r, t, :], half(DISPATCH[:, t, :], h), start=(n == 0), stop=(n == 23))
                        n += 1
                m.then_inc(sem("l2f_ds"), 1)
            pe.wait_ge(sem("l2f_dc"), since("l2f_dc", 2))
            def hidden(pair, q, i):
                pe.wait_ge(sem("l2f_w%d" % q), since("l2f_w%d" % q, 32 * i + 32))
                for p in range(2):
                    pe.wait_ge(sem("l2f_hr"), since("l2f_hr", 2 * pair + p + 1))
                    for c in range(4):
                        m = pe.matmul(ps[:, p, c * CAPACITY:(c + 1) * CAPACITY], W4[:, 2 * q + p, c * P:(c + 1) * P],
                                      columns(A0, 2 * pair + p), start=True, stop=True)
                    m.then_inc(sem("l2f_h"), 1)

            def columns(x, e):
                return x[:, e * CAPACITY:(e + 1) * CAPACITY] if is_static(e) else x[:, bass.ds(CAPACITY * e, CAPACITY)]

            def outputs(pair, q, i):
                pe.wait_ge(sem("l2f_v%d" % q), since("l2f_v%d" % q, 32 * i + 32))
                pe.wait_ge(sem("l2f_yc"), since("l2f_yc", pair + 1))
                for p in range(2):
                    pe.wait_ge(sem("l2f_hr"), since("l2f_hr", 2 * pair + p + 3))
                    for c in range(4):
                        m = pe.matmul(ps[64 * p:64 * p + 64, 2, 0:P], HR[:, p, c, :], W4[:, 2 * q + p, 512 + c * P:512 + (c + 1) * P],
                                      start=(c == 0), stop=(c == 3))
                    m.then_inc(sem("l2f_y"), 1)

            hidden(0, 0, 0)
            with pe.Fori(0, 3) as i:
                hidden(2 * i + 1, 1, i)
                outputs(2 * i, 0, i)
                hidden(2 * i + 2, 0, i + 1)
                outputs(2 * i + 1, 1, i)
            hidden(7, 1, 3)
            outputs(6, 0, 3)
            outputs(7, 1, 3)
            pe.wait_ge(sem("l2f_yp"), since("l2f_yp", 1))
            for h in HALVES:
                n = 0
                for t in range(NT):
                    for r in range(3):
                        m = pe.matmul(ps[:, 4 + h, :], YPARTS[:, r, t, :], half(COLLECT[:, t, :], h), start=(n == 0), stop=(n == 23))
                        n += 1
                m.then_inc(sem("l2f_out"), 1)

        def l2f_scalar(act):
            ln_scalar(act, 8)
            act.wait_ge(sem("l2f_lg"), since("l2f_lg", 1))
            act.activation(RT[:, 1, :], RT[:, 0, :], ACT.Exp).then_inc(sem("l2f_e"), 1)
            for k in range(2):
                act.wait_ge(sem("l2f_row"), since("l2f_row", k + 1))
                for h in HALVES:
                    act.copy(half((A1, A2)[k], h), ps[:, 2 * k + h, :])
                act.drain().then_inc(sem("l2f_rowc"), 1)
            for h in HALVES:
                act.wait_ge(sem("l2f_ds"), since("l2f_ds", h + 1))
                act.copy(half(A0, h), ps[:, 6 + h, :]).then_inc(sem("l2f_dc"), 1)
            act.drain().then_inc(sem("l2f_hr"), 2)
            def relu(i, p):
                act.wait_ge(sem("l2f_h"), since("l2f_h", 2 * i + p + 1))
                act.activation(HR[:, p].rearrange("p c s -> p (c s)"), ps[:, p, 0:4 * CAPACITY], ACT.Relu).then_inc(sem("l2f_hr"), 1)

            relu(0, 0)
            relu(0, 1)
            with act.Fori(1, 8) as i:
                for p in range(2):
                    act.wait_ge(sem("l2f_y"), since("l2f_y", 2 * i + p - 1))
                    relu(i, p)

        def l2f_vector(dve):
            dve.tensor_copy(UNTB[:, 0, :], cst("until"))
            dve.tensor_copy(UNTB[:, 1, :], cst("ones"))
            ln_vector(dve, 8)
            logit, e, oh, key = tiles(0), tiles(1), tiles(2), tiles(3)
            mx, total, gate, idx, loc = (RT[:, 4, 16 * k:16 * k + NT] for k in range(5))
            dve.wait_ge(sem("l2f_logits"), since("l2f_logits", 1))
            lg = ps[:, 0, 0:P].rearrange("p (t e) -> p t e", t=NT)
            dve.tensor_reduce(mx, lg, AX.X, ALU.max)
            dve.drain()
            dve.tensor_tensor(logit, lg, over(mx, 2, 16), ALU.subtract).then_inc(sem("l2f_lg"), 1)
            dve.wait_ge(sem("l2f_xt"), since("l2f_xt", 1))
            three_parts(dve, ps[:, 4:6, :].rearrange("p h (t c) -> p (h t) c", t=4), XPARTS, as_tiles(A5))
            dve.wait_ge(sem("l2f_e"), since("l2f_e", 1))
            dve.tensor_reduce(total, e, AX.X, ALU.add)
            dve.drain()
            dve.reciprocal(total, total)
            dve.drain()
            dve.tensor_tensor(e, e, over(total, 2, 16), ALU.mult)
            dve.drain()
            dve.tensor_reduce(gate, e, AX.X, ALU.max)
            dve.drain()
            dve.tensor_tensor(oh, e, over(gate, 2, 16), ALU.is_equal)
            dve.drain()
            dve.tensor_tensor(oh, oh, over(cst("expert_back"), 1, NT), ALU.mult)
            dve.drain()
            dve.tensor_reduce(idx, oh, AX.X, ALU.min)
            dve.drain()
            dve.tensor_tensor(oh, over(cst("expert_back"), 1, NT), over(idx, 2, 16), ALU.is_equal)
            dve.drain()
            dve.tensor_copy(OHB[:], RT[:, 2, :]).then_inc(sem("l2f_oh"), 1)
            dve.wait_ge(sem("l2f_pre"), since("l2f_pre", 1))
            dve.memset(key[:, 0:1, :], 0.0)
            dve.drain()
            for t in range(1, NT):
                dve.tensor_tensor(key[:, t:t + 1, :], key[:, t - 1:t, :], ps[:, 1, P + (t - 1) * 16:P + t * 16].unsqueeze(1), ALU.add)
                dve.drain()
            dve.tensor_tensor(RT[:, 3, :], RT[:, 3, :], ps[:, 1, 0:P], ALU.add)
            dve.drain()
            dve.tensor_tensor(RT[:, 3, :], RT[:, 3, :], RT[:, 2, :], ALU.mult)
            dve.drain()
            dve.tensor_reduce(loc, key, AX.X, ALU.add)
            dve.drain()
            dve.tensor_scalar(loc, loc, 1.0, None, ALU.subtract)
            dve.drain()
            slot = SLOT[:, 0, :]
            dve.tensor_scalar(slot, loc, float(CAPACITY), FAR_SLOT, ALU.is_ge, ALU.mult)
            dve.drain()
            dve.tensor_tensor(slot, slot, loc, ALU.add)
            dve.drain()
            dve.tensor_scalar(idx, idx, 64.0, float(CAPACITY), ALU.add, ALU.mult)
            dve.drain()
            dve.tensor_tensor(slot, slot, idx, ALU.add)
            dve.drain()
            dve.tensor_tensor(as_tiles(A3), over(cst("ident"), 1, NT), over(slot, 2, P), ALU.mult).then_inc(sem("l2f_diag"), 1)
            dve.tensor_tensor(as_tiles(A4), over(cst("ident"), 1, NT), over(gate, 2, P), ALU.mult).then_inc(sem("l2f_diag"), 1)
            for t in range(NT):
                dve.tensor_scalar(DISPATCH[:, t, :], cst("slot_iota"), slot[:, t:t + 1], None, ALU.is_equal)
            dve.drain().then_inc(sem("l2f_disp"), 1)
            dve.wait_ge(sem("l2f_rowc"), since("l2f_rowc", 1))
            for t in range(NT):
                dve.tensor_scalar(COLLECT[:, t, :], A1, cst("slot_of")[:, t:t + 1], None, ALU.is_equal)
            dve.drain().then_inc(sem("l2f_yc"), 1)
            with dve.Fori(0, 8) as i:
                dve.wait_ge(sem("l2f_y"), since("l2f_y", 2 * i + 2))
                dve.tensor_scalar(A5[:, bass.ds(P * i, P)], ps[:, 2, 0:P], 1.0, None, ALU.mult).then_inc(sem("l2f_yc"), 1)
            dve.drain()
            three_parts(dve, as_tiles(A5), YPARTS, as_tiles(A3))
            dve.drain().then_inc(sem("l2f_yp"), 1)
            dve.wait_ge(sem("l2f_rowc"), since("l2f_rowc", 2))
            for h in HALVES:
                dve.wait_ge(sem("l2f_out"), since("l2f_out", h + 1))
                dve.tensor_tensor(half(A3, h), ps[:, 4 + h, :], half(A2, h), ALU.mult)
                dve.drain()
                dve.tensor_tensor(half(X, h), half(X, h), half(A3, h), ALU.add).then_inc(sem("x_ready"), 1)

        def l2f_sync(sp):
            def load(e, r, at, name):
                sp.dma_start(W4[:, r, at:at + 512], io["l2f_w"][bass.ds(e, 1), :, at:at + 512].rearrange("a p c -> (a p) c"))\
                    .then_inc(sem("l2f_%s%d" % (name, r // 2)), 16)
            sp.wait_ge(sem("l2x_pv"), since("l2x_pv", NT))
            for q in range(2):
                for at, name in ((0, "w"), (512, "v")):
                    load(2 * q, 2 * q, at, name)
                    load(2 * q + 1, 2 * q + 1, at, name)
            with sp.Fori(1, 4) as i:
                for q in range(2):
                    for at, name, used in ((0, "w", "l2f_h"), (512, "v", "l2f_y")):
                        sp.wait_ge(sem(used), since(used, 4 * i + 2 * q - 2))
                        for p in range(2):
                            load(4 * i + 2 * q + p, 2 * q + p, at, name)

        def l3x_tensor(pe):
            def kv(segment):
                kv_tensor(pe, "l3x", w("L3_xattn_Wk"), w("L3_xattn_Wv"), "_kall", segment)
            ln_tensor(pe, 9, kv)
            project(pe, w("L3_xattn_Wq"), XN, (2, 3), "l3x_q", [("xn_ready", 19)])
            kv(2)
            ctx_tensor(pe, "l3x", False)
            pe.wait_ge(sem("l3x_att"), since("l3x_att", B))
            for h in HALVES:
                pe.matmul(ps[:, h, :], w("L3_xattn_Wo"), half(A2, h), start=True, stop=True).then_inc(sem("l3x_out"), 1)

        def l3x_scalar(act):
            ln_scalar(act, 9)
            ctx_scalar(act, "l3x")

        def l3x_vector(dve):
            def kv(segment):
                kv_vector(dve, "l3x", vec("L3_xattn_b_k"), segment)
            ln_vector(dve, 9, kv)
            for h in HALVES:
                dve.wait_ge(sem("l3x_q"), since("l3x_q", h + 1))
                dve.tensor_scalar(half(A1, h), ps[:, 2 + h, :], vec("L3_xattn_b_q"), SHAPE_SCALE, ALU.add, ALU.mult)
            kv(2)
            dve.tensor_tensor(OWN, over(cst("in_four"), 1, 4), over(cst("batch_of"), 2, P), ALU.mult)
            dve.drain().then_inc(sem("l3x_q0"), 2)
            ctx_vector(dve, "l3x", A2, vec("L3_xattn_b_v"))
            add_to_residual(dve, "l3x_out", (0, 1), vec("L3_xattn_b_o"))

        def l3x_gpsimd(pool):
            kv_gpsimd(pool, "l3x", 20)
            ctx_gpsimd(pool, "l3x", A1)

        def l3x_sync(sp):
            ctx_loads(sp, "l3x")
            value_loads(sp, "l3x")

        def l3a_tensor(pe):
            ln_tensor(pe, 10)
            project(pe, w("L3_attn_Wq"), XN, (4, 5), "l3a_q", [("xn_ready", 21)])
            project(pe, w("L3_attn_Wk"), XN, (6, 7), "l3a_k")
            for t in range(NT):
                m = pe.matmul(ps[:, t // 4, (t % 4) * P:(t % 4 + 1) * P], XN[:, t * P:(t + 1) * P], w("L3_attn_Wv"), start=True, stop=True)
                if t % 4 == 3:
                    m.then_inc(sem("l3a_v"), 1)
            pe.wait_ge(sem("l3a_vc"), since("l3a_vc", 2))
            norm_tensor(pe, "hn", 0, A3, A1, "head_mean", "l3a_qc", 0)
            norm_tensor(pe, "hn", 1, A4, A1, "head_mean", "l3a_kc", 0, 4)
            pe.wait_ge(sem("l3a_qn"), since("l3a_qn", 1))
            block_tensor(pe, "l3a", A3, TOK, "_s_read")
            for h in HALVES:
                pe.wait_ge(sem("l3a_y"), since("l3a_y", 2 * h + 2))
                pe.matmul(ps[:, h, :], w("L3_attn_Wo"), half(A5, h), start=True, stop=True).then_inc(sem("l3a_out"), 1)

        def l3a_scalar(act):
            ln_scalar(act, 10)
            for h in HALVES:
                act.wait_ge(sem("l3a_q"), since("l3a_q", h + 1))
                act.copy(half(A3, h), ps[:, 4 + h, :]).then_inc(sem("l3a_qc"), 1)
            for h in HALVES:
                act.wait_ge(sem("l3a_k"), since("l3a_k", h + 1))
                act.copy(half(A4, h), ps[:, 6 + h, :]).then_inc(sem("l3a_kc"), 1)
            for h in HALVES:
                act.wait_ge(sem("l3a_v"), since("l3a_v", h + 1))
                act.copy(half_tok(TOK, h), ps[:, h, :]).then_inc(sem("l3a_vc"), 1)
            norm_scalar(act, "hn", 0, A0, A1, "head_mean", EPS[:, 0:1])
            norm_scalar(act, "hn", 1, A0, A1, "head_mean", EPS[:, 0:1], 4)
            block_softmax_scalar(act, "l3a", True)

        def l3a_vector(dve):
            ln_vector(dve, 10)
            norm_vector(dve, "hn", 0, A3, A0, A1, "head_mean", A3, "l3a_qm")
            dve.drain()
            dve.tensor_scalar(A3, A3, vec("L3_attn_qln_w"), vec("L3_attn_qln_b"), ALU.mult, ALU.add)
            dve.drain()
            dve.tensor_scalar(A3, A3, SHAPE_SCALE, None, ALU.mult).then_inc(sem("l3a_qn"), 1)
            norm_vector(dve, "hn", 1, A4, A0, A1, "head_mean", A4, "l3a_qm", 4)
            dve.drain()
            dve.tensor_scalar(A4, A4, vec("L3_attn_kln_w"), vec("L3_attn_kln_b"), ALU.mult, ALU.add)
            dve.drain().then_inc(sem("l3a_kn"), 2)
            block_softmax_vector(dve, "l3a", A5, True)
            add_to_residual(dve, "l3a_out", (0, 1), vec("L3_attn_bo"))

        def l3a_gpsimd(pool):
            spread(pool, "l3a", A4, "l3a_kn")

        E3 = 9
        ESEL3 = sb("ESEL3", [32, 3, P], BF16)
        B2 = sb("B2", [E3, P])
        COMB9 = sb("COMB9", [E3, T])

        def l3f_tensor(pe):
            ln_tensor(pe, 11)
            pe.wait_ge(sem("xn_ready"), since("xn_ready", 24))
            route_tensor(pe, WG3[:], 8).then_inc(sem("l3f_logits"), 1)
            turn_parts_tensor(pe, 3 * E3, "l3f")
            comb = tiles(3, E3)
            for t in range(NT):
                m = pe.transpose(ps[0:E3, 2 + t // 4, (t % 4) * P:(t % 4 + 1) * P], comb[:, t, :], cst("ident"))
                if t % 4 == 3:
                    m.then_inc(sem("l3f_ct"), 1)
            pe.wait_ge(sem("l3f_combt"), since("l3f_combt", 2))
            for h in HALVES:
                pe.wait_ge(sem("l3f_cc"), since("l3f_cc", h + 1))
                pe.matmul(ps[:, 6 + h, :], B2[:], half(COMB9, h), start=True, stop=False, skip_group_check=True)
            with pe.Fori(0, E3 // 3) as i:
                for r in range(3):
                    e = 3 * i + r
                    pe.wait_ge(sem("l3f_w%d" % r), since("l3f_w%d" % r, 32 * i + 32))
                    for c in range(4):
                        n, o = 8 * e + 2 * c, (r - 1) % 3 if c == 0 else r
                        for h in HALVES:
                            pe.wait_ge(sem("l3f_gelu"), since("l3f_gelu", n + h + 1))
                            pe.matmul(ps[:, 2 * (c % 2) + h, :], BIGW[:, r, c * P:(c + 1) * P], half(XN, h),
                                      start=True, stop=True).then_inc(sem("l3f_h"), 1)
                        for h in HALVES:
                            pe.wait_ge(sem("l3f_mix"), since("l3f_mix", n + h + 3))
                            d = (c - 1) % 4
                            m = pe.matmul(ps[:, 6 + h, :], BIGW[:, o, 512 + d * P:512 + (d + 1) * P], half(HC[:, 1 - c % 2], h),
                                          start=False, stop=False, skip_group_check=True)
                        if c == 0:
                            m.then_inc(sem("l3f_used"), 1)
                            for h in HALVES:
                                m = pe.matmul(ps[:, 4 + h, :], ESEL3[0:3 * E3, r, :], half(COMBT, h)[0:3 * E3], start=True, stop=True)
                            m.then_inc(sem("l3f_b"), 1)
            for h in HALVES:
                pe.wait_ge(sem("l3f_mix"), since("l3f_mix", 8 * E3 + h + 3))
                pe.matmul(ps[:, 6 + h, :], BIGW[:, 2, 896:1024], half(HC[:, 1], h), start=False, stop=True,
                          skip_group_check=True).then_inc(sem("l3f_out"), 1)

        def l3f_scalar(act):
            ln_scalar(act, 11)
            act.wait_ge(sem("l3f_lg"), since("l3f_lg", 1))
            act.activation(tiles(2, 8), tiles(1, 8), ACT.Exp).then_inc(sem("l3f_e"), 1)
            turn_parts_scalar(act, 3 * E3, "l3f")
            for h in HALVES:
                act.wait_ge(sem("l3f_ct"), since("l3f_ct", h + 1))
                act.copy(half(COMB9, h), ps[0:E3, 2 + h, :]).then_inc(sem("l3f_cc"), 1)
            act.drain().then_inc(sem("l3f_gelu"), 4)
            with act.Fori(0, E3 // 3) as i:
                for r in range(3):
                    for c in range(4):
                        for h in HALVES:
                            n = 8 * (3 * i + r) + 2 * c + h
                            act.wait_ge(sem("l3f_h"), since("l3f_h", n + 1))
                            act.wait_ge(sem("l3f_mix"), since("l3f_mix", n + 1))
                            act.activation(half((A0, A1)[c % 2], h), ps[:, 2 * (c % 2) + h, :], ACT.Gelu,
                                           bias=BIGW[:, r, 1024 + c:1025 + c]).then_inc(sem("l3f_gelu"), 1)

        def l3f_vector(dve):
            ln_vector(dve, 11)
            dve.memset(HC[:, 1], 0.0)
            dve.memset(BIGW[:, 2, 896:1024], 0.0)
            logit, less, ex, comb = tiles(0, 8), tiles(1, 8), tiles(2, 8), tiles(3, E3)
            mx, total = RT[:, 5, 0:NT], RT[:, 5, 16:16 + NT]
            dve.wait_ge(sem("l3f_logits"), since("l3f_logits", 1))
            dve.tensor_tensor(logit, ps[:, 0, 0:64].rearrange("p (t e) -> p t e", t=NT), over(ROW[:, 16:24], 1, NT), ALU.add)
            dve.drain()
            dve.tensor_reduce(mx, logit, AX.X, ALU.max)
            dve.drain()
            dve.tensor_tensor(less, logit, over(mx, 2, 8), ALU.subtract).then_inc(sem("l3f_lg"), 1)
            chosen = tiles(9, 8)
            rank(dve, logit, chosen, 8, SCRATCH[:, 0, 0:512])
            dve.tensor_scalar(chosen, chosen, 2.0, None, ALU.is_lt)
            dve.drain()
            dve.wait_ge(sem("l3f_e"), since("l3f_e", 1))
            dve.tensor_tensor(chosen, chosen, ex, ALU.mult)
            dve.drain()
            dve.tensor_reduce(total, chosen, AX.X, ALU.add)
            dve.drain()
            dve.reciprocal(total, total)
            dve.memset(comb[:, :, 0:1], 1.0)
            dve.drain()
            dve.tensor_tensor(comb[:, :, 1:E3], chosen, over(total, 2, 8), ALU.mult)
            dve.drain()
            split_parts(dve, comb, E3, "l3f_parts")
            dve.drain().then_inc(sem("l3f_mix"), 4)
            with dve.Fori(0, E3 // 3) as i:
                for r in range(3):
                    dve.wait_ge(sem("l3f_b"), since("l3f_b", 3 * i + r + 1))
                    for c in range(4):
                        for h in HALVES:
                            n = 8 * (3 * i + r) + 2 * c + h
                            dve.wait_ge(sem("l3f_gelu"), since("l3f_gelu", n + 5))
                            dve.tensor_tensor(half(HC[:, c % 2], h), half((A0, A1)[c % 2], h), ps[:, 4 + h, :],
                                              ALU.mult).then_inc(sem("l3f_mix"), 1)
            for h in HALVES:
                dve.wait_ge(sem("l3f_out"), since("l3f_out", h + 1))
                dve.tensor_tensor(half(X, h), ps[:, 6 + h, :], half(X, h), ALU.add).then_inc(sem("x_ready"), 1)

        def l3f_sync(sp):
            def load(e, r):
                src = io["l3f_w"][bass.ds(e, 1)] if not is_static(e) else io["l3f_w"][e:e + 1]
                sel = io["l3f_sel"][bass.ds(e, 1)] if not is_static(e) else io["l3f_sel"][e:e + 1]
                sp.dma_start(BIGW[:, r, :], src.rearrange("a p c -> (a p) c")).then_inc(sem("l3f_w%d" % r), 16)
                sp.dma_start(ESEL3[0:3 * E3, r, :], sel.rearrange("a p c -> (a p) c")).then_inc(sem("l3f_w%d" % r), 16)
            sp.wait_ge(sem("l3x_att"), since("l3x_att", B))
            load(0, 0)
            load(1, 1)
            sp.wait_ge(sem("l3f_used"), since("l3f_used", 1))
            load(2, 2)
            with sp.Fori(1, E3 // 3) as i:
                for r in range(3):
                    sp.wait_ge(sem("l3f_used"), since("l3f_used", 3 * i + r - 1))
                    load(3 * i + r, r)
        parts = [(l0x_tensor, l0x_scalar, l0x_vector, l0x_gpsimd, None), (l0a_tensor, l0a_scalar, l0a_vector, l0a_gpsimd, None),
                 (l0f_tensor, l0f_scalar, l0f_vector, l0f_gpsimd, l0f_sync),
                 (l1x_tensor, l1x_scalar, l1x_vector, l1x_gpsimd, l1x_sync),
                 (l1a_tensor, l1a_scalar, l1a_vector, nothing, None),
                 (l1f_tensor, l1f_scalar, l1f_vector, nothing, None),
                 (l2x_tensor, l2x_scalar, l2x_vector, nothing, l2x_sync),
                 (l2a_tensor, l2a_scalar, l2a_vector, l2a_gpsimd, None),
                 (l2f_tensor, l2f_scalar, l2f_vector, nothing, l2f_sync),
                 (l3x_tensor, l3x_scalar, l3x_vector, l3x_gpsimd, l3x_sync),
                 (l3a_tensor, l3a_scalar, l3a_vector, l3a_gpsimd, None),
                 (l3f_tensor, l3f_scalar, l3f_vector, nothing, l3f_sync)]
        block = ctx.enter_context(nc.Block())

        @block.sync
        def _(sp):
            first = 4
            sp.dma_start(WTS[:, 0:first, :], io["weights"][:, 0:first, :]).then_inc(sem("ld_w0"), 16)
            sp.dma_start(CT32[:], io["ctx32"]).then_inc(sem("ld_ctx32"), 16)
            sp.dma_start(CST[:, 0:EARLY], io["constants"][:, 0:EARLY]).then_inc(sem("ld_cst"), 16)
            sp.dma_start(VEC[:], io["vectors"]).then_inc(sem("ld_cst"), 16)
            sp.dma_start(X[:], io["x"]).then_inc(sem("ld_x"), 16)
            sp.dma_start(CST[:, EARLY:], io["constants"][:, EARLY:]).then_inc(sem("ld_small"), 16)
            sp.dma_start(LASTT[:], io["ctx_last_t"]).then_inc(sem("ld_small"), 16)
            sp.dma_start(WTS[:, first:, :], io["weights"][:, first:, :]).then_inc(sem("ld_w1"), 16)
            sp.dma_start(RW0[:], io["rw0"]).then_inc(sem("ld_small"), 16)
            sp.dma_start(ROW[:], io["rows"]).then_inc(sem("ld_small"), 16)
            sp.dma_start(WG2[:], io["wg2"]).then_inc(sem("ld_small"), 16)
            sp.dma_start(WG3[:], io["wg3"]).then_inc(sem("ld_small"), 16)
            sp.dma_start(B2[:], io["b2"]).then_inc(sem("ld_small"), 16)
            sp.dma_start(CONVW[:], io["convw"]).then_inc(sem("ld_small"), 16)
            sp.dma_start(ROUT[:], io["rout"]).then_inc(sem("ld_small"), 16)
            sp.dma_start(LROW[:].rearrange("p a d -> p (a d)"), io["lrow"]).then_inc(sem("ld_small"), 16)
            sp.dma_start(WNQ[:], io["wnq"]).then_inc(sem("ld_small"), 16)
            sp.dma_start(WNK[:], io["wnk"]).then_inc(sem("ld_small"), 16)
            for g in range(4):
                sp.dma_start(MASKI[32 * g:32 * g + 32, :], io["mask"]).then_inc(sem("ld_small"), 16)
            for part in parts:
                if part[4]:
                    part[4](sp)
            sp.wait_ge(sem("x_ready"), since("x_ready", 2 * len(parts) + 2))
            sp.dma_start(io["out"], X[:]).then_inc(sem("stored"), 16)
            sp.wait_ge(sem("stored"), since("stored", 16))

        @block.tensor
        def _(pe):
            for part in parts:
                part[0](pe)

        @block.scalar
        def _(act):
            for part in parts:
                part[1](act)

        @block.vector
        def _(dve):
            dve.memset(EPS[:, 0:1], LN_EPS)
            dve.memset(EPS[:, 1:2], 1e-6)
            dve.wait_ge(sem("ld_x"), since("ld_x", 16))
            dve.wait_ge(sem("ld_cst"), since("ld_cst", 32))
            dve.drain().then_inc(sem("x_ready"), 2)
            for part in parts:
                part[2](dve)

        @block.gpsimd
        def _(pool):
            for part in parts:
                part[3](pool)



def kernel(**inputs):
    import concourse.bacc as _bacc
    from concourse.bass_utils import run_bass_kernel_spmd as _run

    f = {k: np.asarray(x) for k, x in inputs.items()}
    arrays = {}
    arrays["x"] = f["x"].reshape(T, P).T
    ctx = f["ctx_1024"]
    arrays["ctx32"] = ctx[:, :Q].transpose(2, 0, 1)
    square = [f[n].T if flip else f[n] for n, flip in WEIGHTS]
    qkv = f["L1_attn_w_qkv"]
    square += [qkv[i * P:(i + 1) * P].T for i in range(3)]
    square += [f["L1_ffn_leaf_values"][i * P:(i + 1) * P] for i in range(2)]
    arrays["weights"] = np.stack(square, axis=1)
    cols = []
    for n in VECTORS:
        x = f[n].reshape(-1)
        if n == "L1_xattn_temperature":
            x = np.repeat(x, HD)
        cols.append(np.tile(x, P // x.size))
    arrays["vectors"] = np.stack(cols, axis=1)
    arrays["constants"] = np.concatenate(list(constant_blocks().values()), axis=1)
    arrays["ctx"] = ctx.transpose(2, 0, 1)
    arrays["mask"] = f["mask_1x1xSxS2_ik1"].reshape(Q, KEYS)
    arrays["wnq"] = np.tile(f["L1_xattn_wnq"], (P // HD, P // HD))
    arrays["wnk"] = np.tile(f["L1_xattn_wnk"], (P // HD, P // HD))
    arrays["ctx_tok"] = ctx[:, :2 * P].reshape(B, 2, P, P).transpose(2, 0, 1, 3)
    arrays["ctx_last"] = ctx[:, KEYS - 1].reshape(NT, 4, P).transpose(1, 0, 2).reshape(4, NT * P)
    arrays["ctx_last_t"] = ctx[:, KEYS - 1].T
    arrays["convw"] = f["L1_attn_w_dwc"]
    arrays["rout"] = f["L1_ffn_routers"].T
    lam = np.concatenate([f["L2_attn_lambda_" + k] for k in ("q1", "k1", "q2", "k2")])
    arrays["lrow"] = np.broadcast_to(lam[None], (P, 4 * HD))
    arrays["wg2"] = f["L2_ffn_Wg"]
    arrays["wg3"] = f["L3_ffn_gate_w"]
    arrays["b2"] = np.concatenate([f["L3_ffn_bs2"][None], f["L3_ffn_b2"]])
    w2 = f["L2_ffn_w2"].reshape(16, 4, P, P).transpose(0, 2, 1, 3).reshape(16, P, 512)
    arrays["l2f_w"] = np.concatenate([f["L2_ffn_w1"], w2], axis=2)
    w1 = np.concatenate([f["L3_ffn_ws1"][None], f["L3_ffn_w1"]])
    w2 = np.concatenate([f["L3_ffn_ws2"][None], f["L3_ffn_w2"]]).reshape(9, 4, P, P).transpose(0, 2, 1, 3).reshape(9, P, 512)
    b1 = np.concatenate([f["L3_ffn_bs1"][None], f["L3_ffn_b1"]]).reshape(9, 4, P).transpose(0, 2, 1)
    arrays["l3f_w"] = np.concatenate([w1, w2, b1], axis=2)
    arrays["l3f_sel"] = part_selectors(9)
    arrays["rw0"] = f["L0_ffn_router_w"].T
    arrays["rows"] = np.broadcast_to(np.concatenate([f["L0_ffn_bias"], f["L3_ffn_gate_b"], f["L3_ffn_gate_b"]])[None], (P, 32))
    gates = [f["L0_ffn_sh_gate_w"][:, :P], f["L0_ffn_sh_gate_w"][:, P:], *f["L0_ffn_gate_w"]]
    ups = [f["L0_ffn_sh_up_w"][:, :P], f["L0_ffn_sh_up_w"][:, P:], *f["L0_ffn_up_w"]]
    downs = [f["L0_ffn_sh_down_w"][:P], f["L0_ffn_sh_down_w"][P:], *f["L0_ffn_down_w"]]
    arrays["l0f_w"] = np.stack([np.concatenate(x, axis=1) for x in zip(gates, ups, downs)])
    arrays["l0f_sel"] = part_selectors(18)

    nc = _bacc.Bacc("TRN2", target_bir_lowering=False, num_devices=1)
    feeds, io = {}, {}
    for name, x in arrays.items():
        x = np.ascontiguousarray(x)
        feeds["in_" + name] = x
        io[name] = nc.dram_tensor("in_" + name, x.shape, mybir.dt.from_np(x.dtype), kind="ExternalInput").ap()
    io["last_rows"] = nc.dram_tensor("last_rows", (B, P), F32).ap()
    io["out"] = nc.dram_tensor("out_x", (P, T), F32, kind="ExternalOutput").ap()
    build(nc, io)
    r = _run(nc, [feeds], core_ids=[0])
    return np.ascontiguousarray(r.results[0]["out_x"].T).reshape(B, Q, P)
```
